# Optimizing a Trainium2 kernel written in Bass

```python
import numpy as np
import jax
import jax.numpy as jnp

def _softmax(x, axis=-1):
    return jax.nn.softmax(x, axis=axis)

def _gelu(x):
    return jax.nn.gelu(x, approximate=True)

def _silu(x):
    return jax.nn.silu(x)

def _sigmoid(x):
    return jax.nn.sigmoid(x)

def _layernorm(x, axis=-1, eps=1e-05):
    m = jnp.mean(x, axis=axis, keepdims=True)
    v = jnp.var(x, axis=axis, keepdims=True)
    return (x - m) / jnp.sqrt(v + eps)

def _scatter_add(tgt, idx, src, axis=0):
    return tgt.at[idx].add(src)

def _segment_sum(src, seg, n):
    return jax.ops.segment_sum(src, seg, n)
kernel_name = 'mk_seq_preln_d1_jaxref_r8_c0404a'

def setup_inputs(seed: int=0):
    np.random.seed(seed)
    _w = jnp.asarray

    def _L0_attn_setup():
        import math
        import jax, jax.numpy as jnp
        import numpy as np
        D_MODEL = 128
        D_STATE = 64
        D_CONV = 4
        HEADDIM = 64
        EXPAND = 2
        NGROUPS = 1
        CHUNK = 64
        LORA = 48
        THETA_CLIP = math.pi / 2
        D_INNER = EXPAND * D_MODEL
        NHEADS = D_INNER // HEADDIM
        NBLK = D_STATE // 2
        CONV_DIM = D_INNER + 2 * NGROUPS * D_STATE
        D_IN_PROJ = 2 * D_INNER + 2 * NGROUPS * D_STATE + NHEADS
        BATCH, SEQ = (2, 256)
        RMS_EPS = 1e-05

        def _forward(x, in_proj_w, conv_w, conv_b, dt_bias, lambda_base, theta_base, theta_w1, theta_w2, viscosity_eta, D, norm_w, out_proj_w):
            Bsz, L, _ = x.shape
            zxbcdt = x @ in_proj_w.T
            z = zxbcdt[..., :D_INNER]
            xBC = zxbcdt[..., D_INNER:D_INNER + CONV_DIM]
            dt = jax.nn.softplus(zxbcdt[..., -NHEADS:] + dt_bias)
            xp = jnp.pad(xBC, ((0, 0), (D_CONV - 1, 0), (0, 0)))
            conv = conv_b
            for k in range(D_CONV):
                conv = conv + xp[:, k:k + L, :] * conv_w[:, k]
            xBC = jax.nn.silu(conv)
            x_ssm = xBC[..., :D_INNER].reshape(Bsz, L, NHEADS, HEADDIM)
            Bg = xBC[..., D_INNER:D_INNER + NGROUPS * D_STATE].reshape(Bsz, L, NGROUPS, D_STATE)
            Cg = xBC[..., D_INNER + NGROUPS * D_STATE:].reshape(Bsz, L, NGROUPS, D_STATE)
            rep = NHEADS // NGROUPS
            Bh = jnp.repeat(Bg, rep, axis=2)
            Ch = jnp.repeat(Cg, rep, axis=2)
            B_c = jax.lax.complex(Bh[..., 0::2], Bh[..., 1::2])
            C_c = jax.lax.complex(Ch[..., 0::2], Ch[..., 1::2])
            lora = jnp.tanh(x @ theta_w1) @ theta_w2
            theta = jnp.clip(theta_base[None, None] + lora.reshape(Bsz, L, NHEADS, NBLK), -THETA_CLIP, THETA_CLIP)
            lambda_eff = lambda_base[None, None] + viscosity_eta[None, None] * theta ** 2
            log_z = jax.lax.complex(-lambda_eff * dt[..., None], theta * dt[..., None])
            x_disc = x_ssm * dt[..., None]
            Nc = L // CHUNK

            def chunkify(a):
                return a.reshape(Bsz, Nc, CHUNK, *a.shape[2:]).swapaxes(0, 1)
            mask = jnp.tril(jnp.ones((CHUNK, CHUNK), bool))[None, :, :, None, None]
            state0 = jnp.zeros((Bsz, NHEADS, HEADDIM, NBLK), jnp.complex64)

            def step(state, inp):
                lz, bc, cc, xc = inp
                cumlog = jnp.cumsum(lz, axis=1)
                diff = cumlog[:, :, None] - cumlog[:, None, :]
                real = jnp.where(mask, diff.real, -60.0)
                A = jnp.where(mask, jnp.exp(jax.lax.complex(real, diff.imag)), 0.0)
                scaled_B = A * bc[:, :, None]
                S_intra = jnp.einsum('btshk,bshp->bthpk', scaled_B, xc.astype(jnp.complex64))
                S_total = jnp.exp(cumlog)[:, :, :, None, :] * state[:, None] + S_intra
                y = jnp.einsum('bthk,bthpk->bthp', cc, S_total).real
                return (S_total[:, -1], y)
            _, ys = jax.lax.scan(step, state0, (chunkify(log_z), chunkify(B_c), chunkify(C_c), chunkify(x_disc)))
            y = ys.swapaxes(0, 1).reshape(Bsz, L, NHEADS, HEADDIM)
            y = y + x_ssm * D[None, None, :, None]
            y = y.reshape(Bsz, L, D_INNER)
            g = y * jax.nn.silu(z)
            g = g * jax.lax.rsqrt(jnp.mean(g * g, axis=-1, keepdims=True) + RMS_EPS) * norm_w
            return g @ out_proj_w.T
        key = jax.random.key(seed)
        ks = jax.random.split(key, 12)
        x = jax.random.normal(ks[0], (BATCH, SEQ, D_MODEL), jnp.float32)
        in_proj_w = jax.random.normal(ks[1], (D_IN_PROJ, D_MODEL), jnp.float32) * 0.02
        conv_w = jax.random.normal(ks[2], (CONV_DIM, D_CONV), jnp.float32) * 0.2
        conv_b = jnp.zeros((CONV_DIM,), jnp.float32)
        dt = jnp.exp(jax.random.uniform(ks[3], (NHEADS,)) * (math.log(0.1) - math.log(0.001)) + math.log(0.001))
        dt = jnp.maximum(dt, 0.0001)
        dt_bias = dt + jnp.log(-jnp.expm1(-dt))
        lambda_base = jax.random.uniform(ks[4], (NHEADS, NBLK), minval=1.0, maxval=16.0)
        theta_base = jax.random.uniform(ks[5], (NHEADS, NBLK), minval=-math.pi / 16, maxval=math.pi / 16)
        theta_w1 = jax.random.normal(ks[6], (D_MODEL, LORA), jnp.float32) * 0.01
        theta_w2 = jax.random.uniform(ks[7], (LORA, NHEADS * NBLK), minval=-0.01, maxval=0.01)
        viscosity_eta = jax.random.normal(ks[8], (NHEADS, NBLK), jnp.float32) * 0.01
        D = jnp.ones((NHEADS,), jnp.float32)
        norm_w = jnp.ones((D_INNER,), jnp.float32)
        out_proj_w = jax.random.normal(ks[9], (D_MODEL, D_INNER), jnp.float32) * 0.02
        return dict(x=x, in_proj_w=in_proj_w, conv_w=conv_w, conv_b=conv_b, dt_bias=dt_bias, lambda_base=lambda_base, theta_base=theta_base, theta_w1=theta_w1, theta_w2=theta_w2, viscosity_eta=viscosity_eta, D=D, norm_w=norm_w, out_proj_w=out_proj_w)
    _L0_attn_in = _L0_attn_setup()

    def _L0_ffn_setup():
        import jax, jax.numpy as jnp
        import numpy as np
        D_MODEL = 128
        D1, D2 = (32, 32)
        F1, F2 = (64, 64)
        E = 64
        TOP_K = 2

        def kmoe(x_flat, W_router, A, B, scale, bias, d_in1, d_in2, d_out1, d_out2, top_k):
            logits = x_flat @ W_router.T
            vals, idx = jax.lax.top_k(logits, top_k)
            probs = jax.nn.softmax(vals, axis=-1)
            xs = x_flat.reshape(-1, d_in1, d_in2)
            Ag = A[idx]
            Bg = B[idx]
            Y = jnp.einsum('nkoi,nij,nkpj->nkop', Ag, xs, Bg)
            out = jnp.einsum('nkop,nk->nop', Y, probs).reshape(-1, d_out1 * d_out2)
            return out * scale + bias
        key = jax.random.key(seed)
        ks = jax.random.split(key, 12)
        s = 0.02
        return {'x': jax.random.normal(ks[0], (4, 256, D_MODEL), dtype=jnp.float32), 'W_up': jax.random.normal(ks[1], (E, D1 * D2), dtype=jnp.float32) * s, 'A_up': jax.random.normal(ks[2], (E, F1, D1), dtype=jnp.float32) * s, 'B_up': jax.random.normal(ks[3], (E, F2, D2), dtype=jnp.float32) * s, 'scale_up': jnp.ones((1,), dtype=jnp.float32), 'bias_up': jnp.zeros((F1 * F2,), dtype=jnp.float32), 'W_down': jax.random.normal(ks[4], (E, F1 * F2), dtype=jnp.float32) * s, 'A_down': jax.random.normal(ks[5], (E, D1, F1), dtype=jnp.float32) * s, 'B_down': jax.random.normal(ks[6], (E, D2, F2), dtype=jnp.float32) * s, 'scale_down': jnp.ones((1,), dtype=jnp.float32), 'bias_down': jnp.zeros((D1 * D2,), dtype=jnp.float32)}
    _L0_ffn_in = _L0_ffn_setup()
    _d = {'L0_attn_x': _L0_attn_in['x'], 'L0_attn_in_proj_w': _L0_attn_in['in_proj_w'], 'L0_attn_conv_w': _L0_attn_in['conv_w'], 'L0_attn_conv_b': _L0_attn_in['conv_b'], 'L0_attn_dt_bias': _L0_attn_in['dt_bias'], 'L0_attn_lambda_base': _L0_attn_in['lambda_base'], 'L0_attn_theta_base': _L0_attn_in['theta_base'], 'L0_attn_theta_w1': _L0_attn_in['theta_w1'], 'L0_attn_theta_w2': _L0_attn_in['theta_w2'], 'L0_attn_viscosity_eta': _L0_attn_in['viscosity_eta'], 'L0_attn_D': _L0_attn_in['D'], 'L0_attn_norm_w': _L0_attn_in['norm_w'], 'L0_attn_out_proj_w': _L0_attn_in['out_proj_w'], 'L0_ffn_W_up': _L0_ffn_in['W_up'], 'L0_ffn_A_up': _L0_ffn_in['A_up'], 'L0_ffn_B_up': _L0_ffn_in['B_up'], 'L0_ffn_scale_up': _L0_ffn_in['scale_up'], 'L0_ffn_bias_up': _L0_ffn_in['bias_up'], 'L0_ffn_W_down': _L0_ffn_in['W_down'], 'L0_ffn_A_down': _L0_ffn_in['A_down'], 'L0_ffn_B_down': _L0_ffn_in['B_down'], 'L0_ffn_scale_down': _L0_ffn_in['scale_down'], 'L0_ffn_bias_down': _L0_ffn_in['bias_down']}
    _x0 = _d['L0_attn_x']
    _d['L0_attn_x'] = jax.random.normal(jax.random.fold_in(jax.random.key(seed), 1), (4, 1024, 128), dtype=_x0.dtype)
    del _x0
    return _d

def reference(L0_attn_x, L0_attn_in_proj_w, L0_attn_conv_w, L0_attn_conv_b, L0_attn_dt_bias, L0_attn_lambda_base, L0_attn_theta_base, L0_attn_theta_w1, L0_attn_theta_w2, L0_attn_viscosity_eta, L0_attn_D, L0_attn_norm_w, L0_attn_out_proj_w, L0_ffn_W_up, L0_ffn_A_up, L0_ffn_B_up, L0_ffn_scale_up, L0_ffn_bias_up, L0_ffn_W_down, L0_ffn_A_down, L0_ffn_B_down, L0_ffn_scale_down, L0_ffn_bias_down):

    def _L0_attn_ref(x, in_proj_w, conv_w, conv_b, dt_bias, lambda_base, theta_base, theta_w1, theta_w2, viscosity_eta, D, norm_w, out_proj_w):
        import math
        import jax, jax.numpy as jnp
        import numpy as np
        D_MODEL = 128
        D_STATE = 64
        D_CONV = 4
        HEADDIM = 64
        EXPAND = 2
        NGROUPS = 1
        CHUNK = 64
        LORA = 48
        THETA_CLIP = math.pi / 2
        D_INNER = EXPAND * D_MODEL
        NHEADS = D_INNER // HEADDIM
        NBLK = D_STATE // 2
        CONV_DIM = D_INNER + 2 * NGROUPS * D_STATE
        D_IN_PROJ = 2 * D_INNER + 2 * NGROUPS * D_STATE + NHEADS
        BATCH, SEQ = (2, 256)
        RMS_EPS = 1e-05

        def _forward(x, in_proj_w, conv_w, conv_b, dt_bias, lambda_base, theta_base, theta_w1, theta_w2, viscosity_eta, D, norm_w, out_proj_w):
            Bsz, L, _ = x.shape
            zxbcdt = x @ in_proj_w.T
            z = zxbcdt[..., :D_INNER]
            xBC = zxbcdt[..., D_INNER:D_INNER + CONV_DIM]
            dt = jax.nn.softplus(zxbcdt[..., -NHEADS:] + dt_bias)
            xp = jnp.pad(xBC, ((0, 0), (D_CONV - 1, 0), (0, 0)))
            conv = conv_b
            for k in range(D_CONV):
                conv = conv + xp[:, k:k + L, :] * conv_w[:, k]
            xBC = jax.nn.silu(conv)
            x_ssm = xBC[..., :D_INNER].reshape(Bsz, L, NHEADS, HEADDIM)
            Bg = xBC[..., D_INNER:D_INNER + NGROUPS * D_STATE].reshape(Bsz, L, NGROUPS, D_STATE)
            Cg = xBC[..., D_INNER + NGROUPS * D_STATE:].reshape(Bsz, L, NGROUPS, D_STATE)
            rep = NHEADS // NGROUPS
            Bh = jnp.repeat(Bg, rep, axis=2)
            Ch = jnp.repeat(Cg, rep, axis=2)
            B_c = jax.lax.complex(Bh[..., 0::2], Bh[..., 1::2])
            C_c = jax.lax.complex(Ch[..., 0::2], Ch[..., 1::2])
            lora = jnp.tanh(x @ theta_w1) @ theta_w2
            theta = jnp.clip(theta_base[None, None] + lora.reshape(Bsz, L, NHEADS, NBLK), -THETA_CLIP, THETA_CLIP)
            lambda_eff = lambda_base[None, None] + viscosity_eta[None, None] * theta ** 2
            log_z = jax.lax.complex(-lambda_eff * dt[..., None], theta * dt[..., None])
            x_disc = x_ssm * dt[..., None]
            Nc = L // CHUNK

            def chunkify(a):
                return a.reshape(Bsz, Nc, CHUNK, *a.shape[2:]).swapaxes(0, 1)
            mask = jnp.tril(jnp.ones((CHUNK, CHUNK), bool))[None, :, :, None, None]
            state0 = jnp.zeros((Bsz, NHEADS, HEADDIM, NBLK), jnp.complex64)

            def step(state, inp):
                lz, bc, cc, xc = inp
                cumlog = jnp.cumsum(lz, axis=1)
                diff = cumlog[:, :, None] - cumlog[:, None, :]
                real = jnp.where(mask, diff.real, -60.0)
                A = jnp.where(mask, jnp.exp(jax.lax.complex(real, diff.imag)), 0.0)
                scaled_B = A * bc[:, :, None]
                S_intra = jnp.einsum('btshk,bshp->bthpk', scaled_B, xc.astype(jnp.complex64))
                S_total = jnp.exp(cumlog)[:, :, :, None, :] * state[:, None] + S_intra
                y = jnp.einsum('bthk,bthpk->bthp', cc, S_total).real
                return (S_total[:, -1], y)
            _, ys = jax.lax.scan(step, state0, (chunkify(log_z), chunkify(B_c), chunkify(C_c), chunkify(x_disc)))
            y = ys.swapaxes(0, 1).reshape(Bsz, L, NHEADS, HEADDIM)
            y = y + x_ssm * D[None, None, :, None]
            y = y.reshape(Bsz, L, D_INNER)
            g = y * jax.nn.silu(z)
            g = g * jax.lax.rsqrt(jnp.mean(g * g, axis=-1, keepdims=True) + RMS_EPS) * norm_w
            return g @ out_proj_w.T
        return _forward(x, in_proj_w, conv_w, conv_b, dt_bias, lambda_base, theta_base, theta_w1, theta_w2, viscosity_eta, D, norm_w, out_proj_w)

    def _L0_ffn_ref(x, W_up, A_up, B_up, scale_up, bias_up, W_down, A_down, B_down, scale_down, bias_down):
        import jax, jax.numpy as jnp
        import numpy as np
        D_MODEL = 128
        D1, D2 = (32, 32)
        F1, F2 = (64, 64)
        E = 64
        TOP_K = 2

        def kmoe(x_flat, W_router, A, B, scale, bias, d_in1, d_in2, d_out1, d_out2, top_k):
            logits = x_flat @ W_router.T
            vals, idx = jax.lax.top_k(logits, top_k)
            probs = jax.nn.softmax(vals, axis=-1)
            xs = x_flat.reshape(-1, d_in1, d_in2)
            Ag = A[idx]
            Bg = B[idx]
            Y = jnp.einsum('nkoi,nij,nkpj->nkop', Ag, xs, Bg)
            out = jnp.einsum('nkop,nk->nop', Y, probs).reshape(-1, d_out1 * d_out2)
            return out * scale + bias
        orig_shape = x.shape
        x_flat = x.reshape(-1, D1 * D2)
        h = kmoe(x_flat, W_up, A_up, B_up, scale_up, bias_up, D1, D2, F1, F2, TOP_K)
        h = jax.nn.gelu(h, approximate=False)
        y = kmoe(h, W_down, A_down, B_down, scale_down, bias_down, F1, F2, D1, D2, TOP_K)
        return y.reshape(*orig_shape[:-1], D_MODEL)
    x = L0_attn_x
    x = x + _L0_attn_ref(_layernorm(x, axis=-1), L0_attn_in_proj_w, L0_attn_conv_w, L0_attn_conv_b, L0_attn_dt_bias, L0_attn_lambda_base, L0_attn_theta_base, L0_attn_theta_w1, L0_attn_theta_w2, L0_attn_viscosity_eta, L0_attn_D, L0_attn_norm_w, L0_attn_out_proj_w)
    x = x + _L0_ffn_ref(_layernorm(x, axis=-1), L0_ffn_W_up, L0_ffn_A_up, L0_ffn_B_up, L0_ffn_scale_up, L0_ffn_bias_up, L0_ffn_W_down, L0_ffn_A_down, L0_ffn_B_down, L0_ffn_scale_down, L0_ffn_bias_down)
    return x

_drawn_inputs = setup_inputs


def setup_inputs(seed=0):
    import zlib

    import numpy as np

    out = dict(_drawn_inputs(seed))
    spreads = {'L0_attn_conv_b': (0.0, 0.1),
     'L0_attn_D': (1.0, 0.598),
     'L0_attn_norm_w': (1.0, 0.2),
     'L0_ffn_bias_up': (0.0, 0.8),
     'L0_ffn_bias_down': (0.0, 0.1)}
    factors = {'L0_attn_dt_bias': 64.0,
     'L0_attn_lambda_base': 8.0,
     'L0_attn_theta_base': 8.0,
     'L0_attn_theta_w1': 8.0,
     'L0_attn_theta_w2': 8.0,
     'L0_attn_viscosity_eta': 8.0,
     'L0_ffn_W_up': 8.0,
     'L0_ffn_A_up': 8.0,
     'L0_ffn_B_up': 8.0,
     'L0_ffn_W_down': 8.0,
     'L0_ffn_A_down': 8.0,
     'L0_ffn_B_down': 8.0}
    for name, (base, spread) in spreads.items():
        noise = np.random.default_rng([zlib.crc32(name.encode()), seed]).standard_normal(out[name].shape)
        drawn = base * np.exp(spread * noise) if base else spread * noise
        out[name] = jnp.asarray(drawn.astype(out[name].dtype))
    for name, factor in factors.items():
        out[name] = (out[name] * factor).astype(out[name].dtype)
    return out
```

```python
import math
from contextlib import ExitStack

import numpy as np

import concourse.bass as bass
from concourse import mybir

FP32 = mybir.dt.float32
I32 = mybir.dt.int32
U32 = mybir.dt.uint32
ALU = mybir.AluOpType
ACT = mybir.ActivationFunctionType
AX = mybir.AxisListType

P = 128
BATCH, LENGTH, DM = 4, 1024, 128
DI = 256
HEADS, HD = 4, 64
NK = 32
LORA = 48
TAPS = 4
CHUNK = 64
SEG = 512
NSEG = BATCH * LENGTH // SEG
TILES = SEG // P
NC = SEG // CHUNK
MID = CHUNK // 2 - 1
LIMIT = 30.0
EPS = 1e-5
TWO_PI_HI = 6.28125
TWO_PI_LO = 2 * math.pi - 6.28125
ROUND = 12582912.0
PI_SAFE = 3.1415925

E = 64
D1 = D2 = 32
F1 = F2 = 64
TOK = SEG * DM // (D1 * D2)
RPT = D1 * D2 // DM
GRP = 8
PAIR = 2 * GRP

NW = 2 * DI + 2 * 2 * NK + HEADS
C_Z, C_X, C_BC, C_DT = 0, DI, 2 * DI, 2 * DI + 4 * NK


def block_kernel(nc, x, w_in, conv_w, conv_b, dt_bias, lam_base, th_base, th_w1, th_w2, eta, d_skip,
                 norm_w, w_out, w_up, a_up, b_up, scale_up, bias_up, w_down, a_down, b_down,
                 scale_down, bias_down, seg_flags, out, x1_scratch, x2_scratch):
    ctx = ExitStack()
    with ctx:
        def sb(name, shape, dt=FP32):
            return ctx.enter_context(nc.sbuf_tensor(name, shape, dt))

        def sem(name):
            return ctx.enter_context(nc.semaphore(name))

        ident = sb("ident", [P, P])
        ones = sb("ones", [P, P])
        causal = sb("causal", [P, CHUNK])
        keep = sb("keep", [P, SEG])
        im_sign = sb("im_sign", [P, 1])
        neg_sign = sb("neg_sign", [P, 1])
        re_row = sb("re_row", [P, 1])
        im_row = sb("im_row", [P, 1])
        minus_half = sb("minus_half", [P, TILES])
        half_pi = sb("half_pi", [P, 1])
        pick = sb("pick", [P, 2 * P])
        win = sb("win", [P, NW])
        w1 = sb("w1", [P, LORA])
        w2 = sb("w2", [LORA, P])
        wout = sb("wout", [P, 2, DM])
        wup = sb("wup", [P, RPT, E])
        cw = sb("cw", [P, 3, TAPS])
        cb = sb("cb", [P, 3])
        dtb = sb("dtb", [P, HEADS])
        lamb = sb("lamb", [P, 1])
        thb = sb("thb", [P, 1])
        etas = sb("etas", [P, 1])
        dsk = sb("dsk", [P, 2])
        nw = sb("nw", [P, 2])
        flags = sb("flags", [P, NSEG])
        au = sb("au", [P, E, F1])
        bu = sb("bu", [P, E, F2])
        ad = sb("ad", [P, E, D1])
        bd = sb("bd", [P, E, D2])
        wdn = sb("wdn", [P, F2, E])
        bias_u = sb("bias_u", [F1, F2])
        bias_d = sb("bias_d", [D1, D2])
        scale_u = sb("scale_u", [F1, 1])
        scale_d = sb("scale_d", [D1, 1])

        xin = sb("xin", [P, TILES, DM])
        x1 = sb("x1", [P, TILES, DM])
        xn = sb("xn", [P, TILES, DM])
        xnT = sb("xnT", [P, SEG])
        xpre = sb("xpre", [P, 3, TAPS - 1 + SEG])
        cv = sb("cv", [P, 3, SEG])
        zs = sb("zs", [P, 2, SEG])
        tmp = sb("tmp", [P, SEG])
        dtx = sb("dtx", [P, TILES * HEADS, NK])
        stats = sb("stats", [P, TILES, 6])
        mv = sb("mv", [P, TILES, 2])
        rstd = sb("rstd", [P, TILES])
        dts = sb("dts", [P, 8, TILES * HEADS])
        phi = sb("phi", [P, NC + 1])
        ksm = sb("ksm", [P, 2, NC])
        fsm = sb("fsm", [P, 3, NC])
        mref = sb("mref", [P, 2, NC])
        bend = sb("bend", [P, 3, NC])
        causal_ok = sb("causal_ok", [P, CHUNK])
        state = sb("state", [P, 2, HD])
        fdec = sb("fdec", [P, 2, 2, NC])
        viol = sb("viol", [P, 2])
        okf = sb("okf", [P, 2])
        oki = sb("oki", [1, 1], I32)
        lg = sb("lg", [TOK, E])
        top = sb("top", [TOK, 8])
        topi = sb("topi", [TOK, 8], U32)
        pr = sb("pr", [TOK, 8])
        offs = sb("offs", [1, 2, TOK, 2], I32)
        pb = sb("pb", [F1, TOK, 2])
        hpre = sb("hpre", [F1, 2, GRP * F2])
        sel = sb("sel", [P, 2, P])
        yo = sb("yo", [D1, 2, GRP * D2])

        arena = sb("arena", [P, 18432 + 6 * NC])
        at = [0]

        def carve(words):
            at[0] += words
            return arena[:, at[0] - words:at[0]]

        EC = 4 * SEG + 3 * NC
        st = carve(2 * EC).rearrange("p (a n) -> p a n", a=2)
        cbr = carve(4 * SEG).rearrange("p (a n) -> p a n", a=4)
        k1 = carve(2 * SEG).rearrange("p (a n) -> p a n", a=2)
        k2 = carve(2 * SEG).rearrange("p (a n) -> p a n", a=2)
        c1 = carve(2 * SEG).rearrange("p (a n) -> p a n", a=2)
        c2 = carve(2 * SEG).rearrange("p (a n) -> p a n", a=2)
        cbq = carve(2 * SEG).rearrange("p (a n) -> p a n", a=2)
        late = at[0]
        lo = carve(SEG)
        th = carve(SEG)
        nl = carve(SEG)
        om = carve(SEG)
        rr = carve(SEG)
        ang = carve(SEG)
        dd = carve(SEG)
        dm = carve(SEG)
        ep = carve(SEG)
        em = carve(SEG)
        sn = carve(SEG)
        cs = carve(SEG)
        kk = carve(SEG)
        at[0] = late
        xd = carve(2 * SEG).rearrange("p (a c n) -> p a c n", a=2, n=HD)
        bt = carve(2 * SEG).rearrange("p (a c n) -> p a c n", a=2, n=2 * NK)
        gs = carve(2 * SEG).rearrange("p (a c n) -> p a c n", a=2, n=CHUNK)
        vv = carve(2 * SEG).rearrange("p (a c n) -> p a c n", a=2, n=HD)
        ss = carve(2 * SEG).rearrange("p (a c n) -> p a c n", a=2, n=HD)
        gg = carve(2 * SEG).rearrange("p (a n) -> p a n", a=2)
        gq = carve(2 * SEG).rearrange("p (a n) -> p a n", a=2)
        at[0] = late + 4 * SEG
        gen_st = carve(4 * SEG).rearrange("p (a n) -> p a n", a=4)
        gen_w = carve(SEG)
        gen_p = carve(SEG)
        at[0] = late + 12 * SEG
        gen_y = carve(2 * SEG).rearrange("p (a n) -> p a n", a=2)
        at[0] = 0
        hh = carve(TOK * F2).rearrange("p (n f) -> p n f", f=F2)
        xi = carve(TOK * D2).rearrange("p (n j) -> p n j", j=D2)
        xr = carve(TOK * D2).rearrange("p (n j) -> p n j", j=D2)
        xp = carve(2 * PAIR * D2).rearrange("p (g n k j) -> p g n k j", g=2, k=2, j=D2)
        t1 = carve(2 * PAIR * F1).rearrange("p (g n k f) -> p g n k f", g=2, k=2, f=F1)
        hs = carve(2 * GRP * F2).rearrange("p (g n f) -> p g n f", g=2, f=F2)
        t2 = carve(2 * PAIR * D1).rearrange("p (g n k f) -> p g n k f", g=2, k=2, f=D1)
        ec = sb("ec", [P, EC])
        gen_src = sb("gen_src", [P, 2, SEG])

        bank = [ctx.enter_context(nc.psum_tensor(f"bank{n}", [P, 512], FP32)) for n in range(8)]

        names = ("weights zeros consts selfs x_in var1 rstd1 xn1 xnT_ps xnT w1_ps dt_ps xbc_ps z_ps tails lora th_ps "
                 "softneg softexp soft1p softln dt_tok dtr_ps xpre_in conv xc zsilu x_tr rep_bc dtheta thsq "
                 "viol_in ok_ps okd angle sincos expd ecs stacked keys q1 q2 k2r bt_ps g_ps btc xds u_ps gsm "
                 "states y_ps gated gsq o_ps rmsin rms x1r var2 rstd2 xn2 x2T_ps x2T lg_ps diff pexp probs "
                 "row_ps rows_in scr xi_in xr_in xp_in t1_ps t1a_in t1b_in h_ps hpre_in h_in lgd_ps drow_ps drows_in hs_in t2_ps "
                 "t2_in y2_ps ys out_sb stored dv pl flag gen_src_in gen_dma gen_sel gen_x_ps gen_prod gen_y_ps gen_done gen_steps gen_loop gen_add passed").split()
        s = {n: sem("s_" + n) for n in names}
        block = ctx.enter_context(nc.Block())


        class Steps:

            def __init__(self, eng, sem_, i, per):
                self.eng, self.sem, self.i, self.per, self.n = eng, sem_, i, per, 0

            def __call__(self, ins):
                ins.then_inc(self.sem, 1)
                self.n += 1
                self.eng.wait_ge(self.sem, self.i * self.per + self.n)

            def done(self):
                assert self.n == self.per, (self.n, self.per)

        def apart(eng):
            eng.sem_inc(s["passed"], 1)

        class General:

            def __init__(self, eng, name):
                self.eng = eng
                self.runs = eng.alloc_register(f"{name}_general_runs")
                self.flag = eng.alloc_register(f"{name}_factored")
                eng.reg_mov(self.runs, 0)

            def read_flag(self, i):
                self.eng.wait_ge(s["flag"], i + 1)
                apart(self.eng)
                self.eng.reg_load(self.flag, oki[0:1, 0:1])

            def taken(self):
                return self.eng.If_eq(self.flag, 0)

            def before(self):
                return self.eng.snap(self.runs, min_val=0, max_val=NSEG)

            def count(self):
                self.eng.reg_add(self.runs, self.runs, 1)

        PAIRS = ((0, 0), (0, 1), (1, 0), (1, 1))

        @block.sync
        def _(sp):
            sp.wait_ge(s["zeros"], 5)
            for dst, src in ((win, w_in), (w1, th_w1), (w2, th_w2), (wup, w_up), (cw, conv_w), (cb, conv_b),
                             (dtb, dt_bias), (lamb, lam_base), (thb, th_base), (etas, eta), (dsk, d_skip),
                             (nw, norm_w), (wout, w_out), (flags, seg_flags), (bias_u, bias_up),
                             (bias_d, bias_down), (scale_u, scale_up), (scale_d, scale_down)):
                sp.dma_start(dst[:], src).then_inc(s["weights"], 16)
            sp.dma_start(xin[:], x[0:SEG, :].rearrange("(c p) d -> p c d", p=P)).then_inc(s["x_in"], 16)
            sp.dma_start(au[0:D1], a_up).then_inc(s["weights"], 16)
            sp.dma_start(bu[0:D2], b_up).then_inc(s["weights"], 16)
            sp.dma_start(ad[0:F1], a_down).then_inc(s["weights"], 16)
            sp.dma_start(bd[0:F2], b_down).then_inc(s["weights"], 16)
            sp.dma_start(wdn[0:F1], w_down).then_inc(s["weights"], 16)
            general = General(sp, "sp")
            with sp.Fori(0, NSEG) as i:
                sp.wait_ge(s["xc"], i * 3 + 3)
                for h in range(2):
                    for a, (first, second) in enumerate(((0, 0), (NK, NK), (2 * NK, 3 * NK), (3 * NK, 2 * NK))):
                        for r, src in ((0, first), (NK, second)):
                            to = h * 2 * NK + r
                            sp.dma_start(cbr[to:to + NK, a, :], cv[src:src + NK, 2, :]).then_inc(s["rep_bc"], 16)
                sp.wait_ge(s["ecs"], i + 1)
                for q, h in PAIRS:
                    for r in range(2):
                        src, to = (2 * q + h) * NK, h * 2 * NK + r * NK
                        sp.dma_start(st[to:to + NK, q, :], ec[src:src + NK, :]).then_inc(s["stacked"], 16)
                        sp.dma_start(k1[to:to + NK, q, :], ec[src:src + NK, (2 + r) * SEG:(3 + r) * SEG])\
                            .then_inc(s["keys"], 16)
                general.read_flag(i)
                with general.taken():
                    n = general.before()
                    sp.wait_ge(s["gen_src_in"], n + 1)
                    for q in range(2):
                        if q == 1:
                            sp.wait_ge(s["gen_done"], n * 2 + 1)
                        for h in range(2):
                            for r in range(2):
                                src, to = (2 * q + h) * NK, h * 2 * NK + r * NK
                                for a, array in enumerate((gen_src[:, 0], cs, sn, gen_src[:, 1])):
                                    sp.dma_start(gen_st[to:to + NK, a], array[src:src + NK, :])\
                                        .then_inc(s["gen_dma"], 16)
                    general.count()
                here = i * SEG
                sp.wait_ge(s["x1r"], i * TILES + TILES)
                sp.dma_start(x1_scratch[bass.ds(here, SEG), :].rearrange("(c p) d -> p c d", p=P), x1[:])\
                    .then_inc(s["scr"], 16)
                sp.wait_ge(s["xn2"], i * TILES + TILES)
                sp.dma_start(x2_scratch[bass.ds(here, SEG), :].rearrange("(c p) d -> p c d", p=P), xn[:])\
                    .then_inc(s["scr"], 16)
                sp.wait_ge(s["o_ps"], i + 1)
                sp.wait_ge(s["scr"], i * 32 + 32)
                sp.dma_start(xi[0:D1], x2_scratch[bass.ds(here, SEG), :]
                             .rearrange("(n r) (q j) -> (r q) n j", r=RPT, j=D2)).then_inc(s["xi_in"], 16)
                sp.dma_start(xr[0:D1], x1_scratch[bass.ds(here, SEG), :]
                             .rearrange("(n r) (q j) -> (r q) n j", r=RPT, j=D2)).then_inc(s["xr_in"], 16)
                sp.dma_start(xin[:], x[bass.ds(here + SEG, SEG), :].rearrange("(c p) d -> p c d", p=P))\
                    .then_inc(s["x_in"], 16)
                sp.wait_ge(s["out_sb"], i * (TOK // GRP) + TOK // GRP)
                sp.dma_start(out[bass.ds(here, SEG), :].rearrange("(n r) (q j) -> (r q) n j", r=RPT, j=D2),
                             xr[0:D1]).then_inc(s["stored"], 16)
            sp.wait_ge(s["stored"], 16 * NSEG)
            sp.wait_ge(s["x_in"], 16 * (NSEG + 1))
            sp.wait_ge(s["scr"], 32 * NSEG)

        @block.gpsimd
        def _(pool):
            nc.gpsimd.memset(au[:], 0.0).then_inc(s["zeros"], 1)
            nc.gpsimd.memset(bu[:], 0.0).then_inc(s["zeros"], 1)
            nc.gpsimd.memset(ad[:], 0.0).then_inc(s["zeros"], 1)
            nc.gpsimd.memset(bd[:], 0.0).then_inc(s["zeros"], 1)
            nc.gpsimd.memset(wdn[:], 0.0).then_inc(s["zeros"], 1)
            nc.gpsimd.memset(arena[:], 0.0).then_inc(s["consts"], 1)
            nc.gpsimd.memset(ones[:], 1.0).then_inc(s["consts"], 1)
            nc.gpsimd.memset(ident[:], 0.0).then_inc(s["consts"], 1)
            nc.gpsimd.memset(pick[:], 0.0).then_inc(s["consts"], 1)
            nc.gpsimd.memset(causal[:], 1.0).then_inc(s["consts"], 1)
            nc.gpsimd.memset(keep[:], 1.0).then_inc(s["consts"], 1)
            nc.gpsimd.memset(im_sign[:], 1.0).then_inc(s["consts"], 1)
            nc.gpsimd.memset(neg_sign[:], -1.0).then_inc(s["consts"], 1)
            nc.gpsimd.memset(re_row[:], 1.0).then_inc(s["consts"], 1)
            nc.gpsimd.memset(im_row[:], 0.0).then_inc(s["consts"], 1)
            nc.gpsimd.memset(minus_half[:], -0.5).then_inc(s["consts"], 1)
            nc.gpsimd.memset(half_pi[:], math.pi / 2).then_inc(s["consts"], 1)
            nc.gpsimd.memset(xpre[:], 0.0).then_inc(s["consts"], 1)
            nc.gpsimd.memset(phi[:], 0.0).then_inc(s["consts"], 1)
            nc.gpsimd.memset(state[:], 0.0).then_inc(s["consts"], 1)
            pool.wait_ge(s["consts"], 15)

            def shaped(ins):
                made[0] += 1
                ins.then_inc(s["selfs"], 1)
                pool.wait_ge(s["selfs"], made[0])

            made = [0]
            shaped(nc.gpsimd.affine_select(out=ident[:], in_=ident[:], compare_op=ALU.not_equal, fill=1.0, base=0,
                                           pattern=[[-1, P]], channel_multiplier=1))
            for h in range(2):
                half = slice(h * CHUNK, h * CHUNK + CHUNK)
                shaped(nc.gpsimd.affine_select(out=causal[half], in_=causal[half], compare_op=ALU.is_ge, fill=0.0,
                                               base=0, pattern=[[1, CHUNK]], channel_multiplier=-1))
                for column, value in ((im_sign, -1.0), (neg_sign, 1.0), (re_row, 0.0), (im_row, 1.0)):
                    shaped(nc.gpsimd.memset(column[h * CHUNK + NK:h * CHUNK + 2 * NK], value))
                shaped(nc.gpsimd.memset(pick[half, CHUNK + h * CHUNK:CHUNK + h * CHUNK + 1], 1.0))
            shaped(nc.gpsimd.memset(keep[:].rearrange("p (c n) -> p c n", n=CHUNK)[:, :, 0:1], 0.0))
            with pool.Fori(0, NSEG) as i:
                step = Steps(pool, s["pl"], i, 1)
                pool.wait_ge(s["var1"], i + 1)
                nc.gpsimd.tensor_tensor(rstd[:], mv[:, :, 1], minus_half[:], ALU.pow).then_inc(s["rstd1"], 1)
                pool.wait_ge(s["dtheta"], i + 1)
                nc.gpsimd.tensor_tensor(rr[:, :], th[:, :], th[:, :], ALU.mult).then_inc(s["thsq"], 1)
                pool.wait_ge(s["rmsin"], i + 1)
                nc.gpsimd.tensor_tensor(rstd[:], mv[:, :, 0], minus_half[:], ALU.pow).then_inc(s["rms"], 1)
                pool.wait_ge(s["var2"], i + 1)
                apart(pool)
                step(nc.gpsimd.tensor_copy(rstd[:], mv[:, :, 1]))
                nc.gpsimd.tensor_tensor(rstd[:], rstd[:], minus_half[:], ALU.pow).then_inc(s["rstd2"], 1)
                step.done()
                pool.wait_ge(s["xi_in"], i * 16 + 16)
                pool.wait_ge(s["rows_in"], i * 2 + 2)
                NG = TOK // GRP
                apart(pool)
                with pool.Fori(0, TOK // PAIR) as g:
                    for half in range(2):
                        pool.wait_ge(s["t1_ps"], i * NG + g * 2 + 1)
                        n0 = g * PAIR + half * GRP
                        nc.gpsimd.tensor_tensor(
                            xp[0:D1, half],
                            xi[0:D1, bass.ds(n0, GRP), :].unsqueeze(2).to_broadcast([D1, GRP, 2, D2]),
                            pb[0:D1, bass.ds(n0, GRP), :].unsqueeze(3).to_broadcast([D1, GRP, 2, D2]),
                            ALU.mult).then_inc(s["xp_in"], 1)
                pool.wait_ge(s["h_in"], i * NG + NG + 1)
                apart(pool)
                with pool.Fori(0, TOK // PAIR) as g:
                    for half in range(2):
                        pool.wait_ge(s["t2_ps"], i * NG + g * 2 + 1)
                        n0 = g * PAIR + half * GRP
                        apart(pool)
                        nc.gpsimd.tensor_copy(hs[0:F1, half], hh[0:F1, bass.ds(n0, GRP), :]).then_inc(s["hs_in"], 1)

        @block.scalar
        def _(act):
            act.wait_ge(s["consts"], 15)
            act.wait_ge(s["selfs"], 14)
            for free in ("h_in", "t1a_in",):
                act.sem_inc(s[free], 1)
            with act.Fori(0, NSEG) as i:
                NG = TOK // GRP
                act.wait_ge(s["xnT_ps"], i + 1)
                nc.scalar.activation(xnT[:], bank[0][:], ACT.Copy).then_inc(s["xnT"], 1)
                act.wait_ge(s["w1_ps"], i + 1)
                nc.scalar.activation(lo[0:LORA, :], bank[1][0:LORA, :], ACT.Tanh).then_inc(s["lora"], 1)
                act.wait_ge(s["tails"], i + 1)
                for a in range(3):
                    act.wait_ge(s["xbc_ps"], i * 3 + a + 1)
                    nc.scalar.activation(xpre[:, a, TAPS - 1:], bank[3 + a][:], ACT.Copy).then_inc(s["xpre_in"], 1)
                for a in range(2):
                    act.wait_ge(s["z_ps"], i * 2 + a + 1)
                    nc.scalar.activation(zs[:, a, :], bank[6 + a][:], ACT.Silu).then_inc(s["zsilu"], 1)
                act.wait_ge(s["softneg"], i + 1)
                nc.scalar.activation(dts[:, 2, :], dts[:, 1, :], ACT.Exp).then_inc(s["softexp"], 1)
                act.wait_ge(s["soft1p"], i + 1)
                nc.scalar.activation(dts[:, 4, :], dts[:, 3, :], ACT.Ln).then_inc(s["softln"], 1)
                for a in range(3):
                    act.wait_ge(s["conv"], i * 3 + a + 1)
                    nc.scalar.activation(cv[:, a, :], cv[:, a, :], ACT.Silu).then_inc(s["xc"], 1)
                act.wait_ge(s["angle"], i * 2 + 2)
                nc.scalar.activation(sn[:, :], ang[:, :], ACT.Sin).then_inc(s["sincos"], 1)
                nc.scalar.activation(cs[:, :], kk[:, :], ACT.Sin, bias=half_pi[:, 0:1]).then_inc(s["sincos"], 1)
                act.wait_ge(s["okd"], i + 1)
                nc.scalar.activation(ep[:, :], dd[:, :], ACT.Exp).then_inc(s["expd"], 1)
                nc.scalar.activation(em[:, :], dm[:, :], ACT.Exp).then_inc(s["expd"], 1)
                nc.scalar.activation(ec[:, 4 * SEG:], fsm[:, :, :].rearrange("p a c -> p (a c)"), ACT.Exp)\
                    .then_inc(s["expd"], 1)
                nc.scalar.activation(gen_src[:, 0, :], nl[:, :], ACT.Exp).then_inc(s["expd"], 1)
                for q in range(2):
                    act.wait_ge(s["bt_ps"], i * 2 + q + 1)
                    for par in range(2):
                        for h in range(2):
                            nc.scalar.activation(
                                bt[h * CHUNK:(h + 1) * CHUNK, q].rearrange("p (c two) n -> p c two n", two=2)[:, :, par, :],
                                bank[5 + q][par * CHUNK:(par + 1) * CHUNK, :]
                                .rearrange("p (c h n) -> p c h n", c=TILES, h=2)[:, :, h, :],
                                ACT.Copy).then_inc(s["btc"], 1)
                for q in range(2):
                    act.wait_ge(s["gated"], i * 2 + q + 1)
                    nc.scalar.activation(gq[:, q, :], gg[:, q, :], ACT.Square).then_inc(s["gsq"], 1)
                act.wait_ge(s["x2T_ps"], i + 1)
                nc.scalar.activation(xnT[:], bank[7][:], ACT.Copy).then_inc(s["x2T"], 1)
                act.wait_ge(s["diff"], i * 2 + 1)
                nc.scalar.activation(pr[:, 1:2], pr[:, 0:1], ACT.Exp).then_inc(s["pexp"], 1)
                apart(act)
                with act.Fori(0, TOK // PAIR) as g:
                    act.wait_ge(s["t1_ps"], i * NG + g * 2 + 1 + 1)
                    for b in range(2):
                        nc.scalar.activation(t1[0:D2, 0].rearrange("p n k f -> p (n k f)")[:, b * 512:(b + 1) * 512],
                                             bank[b][0:D2, :], ACT.Copy).then_inc(s["t1a_in"], 1)
                    for half in range(2):
                        act.wait_ge(s["hpre_in"], i * NG + g * 2 + half + 1 + 1)
                        nc.scalar.activation(hh[0:F1, bass.ds(g * PAIR + half * GRP, GRP), :],
                                             hpre[:, half].rearrange("p (n f) -> p n f", f=F2), ACT.Gelu)\
                            .then_inc(s["h_in"], 1)
                act.wait_ge(s["diff"], i * 2 + 2)
                nc.scalar.activation(pr[:, 1:2], pr[:, 0:1], ACT.Exp).then_inc(s["pexp"], 1)

        @block.vector
        def _(dve):
            dve.wait_ge(s["weights"], 16 * 23)
            dve.wait_ge(s["consts"], 15)
            dve.wait_ge(s["selfs"], 14)
            V = nc.vector
            for q in range(2):
                V.tensor_scalar(wout[:, q], wout[:, q], nw[:, q:q + 1], None, ALU.mult).then_inc(s["weights"], 1)
            NG = TOK // GRP

            def top2(step, i, layer, logits):
                step(V.tensor_copy(lg[:], logits))
                apart(dve)
                step(V.max(top[:], lg[:]))
                apart(dve)
                step(V.max_index(topi[:], top[:], lg[:]))
                step(V.tensor_scalar(pr[:, 6:8], topi[:, 0:2], float(F1 if layer == 0 else D1), None, ALU.mult))
                V.tensor_tensor(pr[:, 0:1], top[:, 1:2], top[:, 0:1], ALU.subtract).then_inc(s["diff"], 1)
                dve.wait_ge(s["pexp"], i * 2 + layer + 1)
                step(V.tensor_scalar(pr[:, 2:3], pr[:, 1:2], 1.0, None, ALU.add))
                step(V.reciprocal(pr[:, 4:5], pr[:, 2:3]))
                V.tensor_tensor(pr[:, 5:6], pr[:, 4:5], pr[:, 1:2], ALU.mult).then_inc(s["probs"], 1)
                ps = bank[6] if layer == 0 else bank[7]
                dve.wait_ge(s["row_ps"], i * 2 + layer + 1)
                V.tensor_copy(offs[:, layer].rearrange("p n k -> p k n"),
                              ps[0:1, 128:128 + 2 * TOK].rearrange("p (k n) -> p k n", k=2)).then_inc(s["rows_in"] if layer == 0 else s["drows_in"], 1)
                V.tensor_copy(pb[:, :, :].rearrange("p n k -> p k n"),
                              ps[0:F1, 256:256 + 2 * TOK].rearrange("p (k n) -> p k n", k=2)).then_inc(s["rows_in"] if layer == 0 else s["drows_in"], 1)

            def reduce_angle(step, ang_, k_):
                step(V.tensor_scalar(k_, ang_, 1 / (2 * math.pi), ROUND, ALU.mult, ALU.add))
                step(V.tensor_scalar(k_, k_, ROUND, None, ALU.subtract))
                step(V.scalar_tensor_tensor(ang_, k_, -TWO_PI_HI, ang_, ALU.mult, ALU.add))
                step(V.scalar_tensor_tensor(ang_, k_, -TWO_PI_LO, ang_, ALU.mult, ALU.add))

            def layernorm_stats(step, src, name, i):
                for c in range(TILES):
                    ins = V.bn_stats(stats[:, c], src[:, c])
                    if c < TILES - 1:
                        ins.then_inc(s["dv"], 1)
                        step.n += 1
                    else:
                        step(ins)
                for c in range(TILES):
                    apart(dve)
                    step(V.bn_aggr(mv[:, c], stats[:, c]))
                V.tensor_scalar(mv[:, :, 1], mv[:, :, 1], EPS, None, ALU.add).then_inc(s[name], 1)

            general = General(dve, "dve")
            for free in ("t1b_in", "hpre_in", "t2_in", "ys",):
                dve.sem_inc(s[free], 1)
            with dve.Fori(0, NSEG) as i:
                step = Steps(dve, s["dv"], i, DVE_STEPS)
                dve.wait_ge(s["x_in"], i * 16 + 16)
                V.tensor_scalar(xpre[:, :, 0:TAPS - 1], xpre[:, :, SEG:], flags[:, bass.ds(i, 1)], None, ALU.mult)\
                    .then_inc(s["tails"], 1)
                layernorm_stats(step, xin, "var1", i)
                dve.wait_ge(s["rstd1"], i + 1)
                for c in range(TILES):
                    V.tensor_scalar(xn[:, c], xin[:, c], mv[:, c, 0:1], rstd[:, c:c + 1], ALU.subtract, ALU.mult)\
                        .then_inc(s["xn1"], 1)
                dve.wait_ge(s["dt_ps"], i + 1)
                step(V.tensor_tensor(dts[:, 0].rearrange("p (c h) -> p c h", h=HEADS),
                                     bank[2][:, 0:TILES * HEADS].rearrange("p (c h) -> p c h", h=HEADS),
                                     dtb[:, :].unsqueeze(1).to_broadcast([P, TILES, HEADS]), ALU.add))
                V.scalar_tensor_tensor(dts[:, 1], dts[:, 0], -1.0, dts[:, 0], ALU.mult, ALU.min).then_inc(s["softneg"], 1)
                dve.wait_ge(s["softexp"], i + 1)
                V.tensor_scalar(dts[:, 3], dts[:, 2], 1.0, None, ALU.add).then_inc(s["soft1p"], 1)
                dve.wait_ge(s["soft1p"], i + 1)
                step(V.tensor_scalar(dts[:, 5], dts[:, 3], -1.0, None, ALU.add))
                step(V.tensor_scalar(dts[:, 6], dts[:, 5], 1e-30, None, ALU.max))
                step(V.reciprocal(dts[:, 6], dts[:, 6]))
                step(V.tensor_tensor(dts[:, 6], dts[:, 6], dts[:, 2], ALU.mult))
                step(V.tensor_scalar(dts[:, 5], dts[:, 5], 0.0, None, ALU.is_equal))
                step(V.tensor_tensor(dts[:, 5], dts[:, 5], dts[:, 2], ALU.mult))
                dve.wait_ge(s["softln"], i + 1)
                step(V.tensor_tensor(dts[:, 6], dts[:, 6], dts[:, 4], ALU.mult))
                step(V.tensor_tensor(dts[:, 6], dts[:, 6], dts[:, 5], ALU.add))
                step(V.tensor_scalar(dts[:, 0], dts[:, 0], 0.0, None, ALU.max))
                V.tensor_tensor(dtx[:], dts[:, 6].unsqueeze(2).to_broadcast([P, TILES * HEADS, NK]),
                                dts[:, 0].unsqueeze(2).to_broadcast([P, TILES * HEADS, NK]), ALU.add)\
                    .then_inc(s["dt_tok"], 1)
                for a in range(3):
                    dve.wait_ge(s["xpre_in"], i * 3 + a + 1)
                    step(V.tensor_scalar(cv[:, a], xpre[:, a, 0:SEG], cw[:, a, 0:1], cb[:, a:a + 1], ALU.mult, ALU.add))
                    for k in range(1, TAPS):
                        ins = V.scalar_tensor_tensor(cv[:, a], xpre[:, a, k:k + SEG], cw[:, a, k:k + 1], cv[:, a],
                                                     ALU.mult, ALU.add)
                        if k < TAPS - 1:
                            step(ins)
                        else:
                            ins.then_inc(s["conv"], 1)
                dve.wait_ge(s["th_ps"], i + 1)
                step(V.tensor_scalar(th[:, :], bank[0][:], thb[:, 0:1], math.pi / 2, ALU.add, ALU.min))
                V.tensor_scalar(th[:, :], th[:, :], -math.pi / 2, None, ALU.max).then_inc(s["dtheta"], 1)
                dve.wait_ge(s["dtheta"], i + 1)
                dve.wait_ge(s["dtr_ps"], i + 1)
                step(V.tensor_copy(gen_src[:, 1, :], bank[1][:]))
                step(V.tensor_tensor(om[:, :], th[:, :], gen_src[:, 1, :], ALU.mult))
                step(V.tensor_tensor_scan(ang[:, :], keep[:], om[:, :], 0.0, ALU.mult, ALU.add))
                dve.wait_ge(s["thsq"], i + 1)
                step(V.tensor_scalar(rr[:, :], rr[:, :], etas[:, 0:1], lamb[:, 0:1], ALU.mult, ALU.add))
                step(V.scalar_tensor_tensor(nl[:, :], rr[:, :], -1.0, gen_src[:, 1, :], ALU.mult, ALU.mult))
                step(V.tensor_tensor_scan(rr[:, :], keep[:], nl[:, :], 0.0, ALU.mult, ALU.add))
                rc = rr[:, :].rearrange("p (c n) -> p c n", n=CHUNK)
                step(V.tensor_tensor(dd[:, :].rearrange("p (c n) -> p c n", n=CHUNK), rc,
                                     rc[:, :, MID:MID + 1].to_broadcast([P, NC, CHUNK]), ALU.subtract))
                step(V.tensor_reduce(viol[:, 0:1], dd[:, :], AX.X, ALU.max, apply_absolute_value=True))
                V.tensor_scalar(viol[:, 1:2], viol[:, 0:1], LIMIT, None, ALU.is_le).then_inc(s["viol_in"], 1)
                step(V.tensor_scalar(phi[:, 0:1], phi[:, NC:NC + 1], flags[:, bass.ds(i, 1)], None, ALU.mult))
                angc = ang[:, :].rearrange("p (c n) -> p c n", n=CHUNK)
                step(V.tensor_copy(ksm[:, 0], angc[:, :, CHUNK - 1]))
                reduce_angle(step, ksm[:, 0], ksm[:, 1])
                step(V.tensor_tensor_scan(phi[:, 1:], ones[:, 0:NC], ksm[:, 0], phi[:, 0:1], ALU.mult, ALU.add))
                step(V.tensor_tensor(angc, angc, phi[:, 0:NC].unsqueeze(2).to_broadcast([P, NC, CHUNK]), ALU.add))
                reduce_angle(step, ang[:, :], kk[:, :])
                V.tensor_scalar(ang[:, :], ang[:, :], PI_SAFE, -PI_SAFE, ALU.min, ALU.max).then_inc(s["angle"], 1)
                dve.wait_ge(s["angle"], i * 2 + 1)
                V.scalar_tensor_tensor(kk[:, :], ang[:, :], -1.0, ang[:, :], ALU.mult, ALU.min).then_inc(s["angle"], 1)
                dve.wait_ge(s["ok_ps"], i + 1)
                step(V.tensor_scalar(okf[:, 0:1], bank[2][:, 64:65], P - 0.5, None, ALU.is_gt))
                step(V.tensor_scalar(okf[:, 1:2], okf[:, 0:1], -1.0, 1.0, ALU.mult, ALU.add))
                V.tensor_copy(oki[:], okf[0:1, 0:1]).then_inc(s["flag"], 1)
                step(V.tensor_scalar(causal_ok[:], causal[:], okf[:, 0:1], None, ALU.mult))
                step(V.tensor_scalar(mref[:, 0], rc[:, :, MID], okf[:, 0:1], None, ALU.mult))
                step(V.scalar_tensor_tensor(mref[:, 1], rc[:, :, CHUNK - 1], okf[:, 1:2], mref[:, 0],
                                            ALU.mult, ALU.add))
                step(V.tensor_copy(fsm[:, 0], mref[:, 0]))
                step(V.tensor_tensor(fsm[:, 1], rc[:, :, CHUNK - 1], mref[:, 1], ALU.subtract))
                step(V.tensor_tensor(fsm[:, 2], mref[:, 1], mref[:, 0], ALU.subtract))
                step(V.tensor_tensor(dd[:, :].rearrange("p (c n) -> p c n", n=CHUNK), rc,
                                     mref[:, 0].unsqueeze(2).to_broadcast([P, NC, CHUNK]), ALU.subtract))
                V.tensor_tensor(dm[:, :].rearrange("p (c n) -> p c n", n=CHUNK),
                                mref[:, 1].unsqueeze(2).to_broadcast([P, NC, CHUNK]), rc, ALU.subtract)\
                    .then_inc(s["okd"], 1)
                dve.wait_ge(s["sincos"], i * 2 + 2)
                dve.wait_ge(s["expd"], i * 4 + 4)
                for n, (e_, t_) in enumerate(((ep, cs), (ep, sn), (em, cs), (em, sn))):
                    ins = V.tensor_tensor(ec[:, n * SEG:(n + 1) * SEG], e_, t_, ALU.mult)
                    if n < 3:
                        step(ins)
                    else:
                        ins.then_inc(s["ecs"], 1)
                for q in range(2):
                    dve.wait_ge(s["x_tr"], i * 2 + q + 1)
                    for par in range(2):
                        rows = slice(par * CHUNK, (par + 1) * CHUNK)
                        for h in range(2):
                            V.tensor_tensor(
                                xd[h * CHUNK:(h + 1) * CHUNK, q].rearrange("p (c two) n -> p c two n", two=2)[:, :, par, :],
                                bank[3 + q][rows, :].rearrange("p (c h n) -> p c h n", c=TILES, h=2)[:, :, h, :],
                                dtx[rows].rearrange("p (c h) k -> p c h k", h=HEADS)[:, :, 2 * q + h, 0:1]
                                .to_broadcast([CHUNK, TILES, HD]),
                                ALU.mult).then_inc(s["xds"], 1)
                dve.wait_ge(s["rep_bc"], i * 256 + 256)
                step(V.tensor_tensor(cbq[:, 0], cbr[:, 2], cbr[:, 0], ALU.mult))
                step(V.scalar_tensor_tensor(tmp[:], cbr[:, 3], neg_sign[:, 0:1], cbr[:, 1], ALU.mult, ALU.mult))
                step(V.tensor_tensor(cbq[:, 0], cbq[:, 0], tmp[:], ALU.add))
                step(V.scalar_tensor_tensor(cbq[:, 1], cbr[:, 3], neg_sign[:, 0:1], cbr[:, 0], ALU.mult, ALU.mult))
                step(V.tensor_tensor(tmp[:], cbr[:, 2], cbr[:, 1], ALU.mult))
                step(V.tensor_tensor(cbq[:, 1], cbq[:, 1], tmp[:], ALU.subtract))
                b_re = cbr[:, 0].rearrange("p (c n) -> p c n", n=CHUNK)[:, :, CHUNK - 1]
                b_im = cbr[:, 1].rearrange("p (c n) -> p c n", n=CHUNK)[:, :, CHUNK - 1]
                step(V.tensor_scalar(bend[:, 0], b_re, re_row[:, 0:1], None, ALU.mult))
                step(V.scalar_tensor_tensor(bend[:, 0], b_im, im_row[:, 0:1], bend[:, 0], ALU.mult, ALU.add))
                step(V.tensor_scalar(bend[:, 2], b_re, im_row[:, 0:1], None, ALU.mult))
                step(V.scalar_tensor_tensor(bend[:, 1], b_im, re_row[:, 0:1], bend[:, 2], ALU.mult, ALU.subtract))
                dve.wait_ge(s["stacked"], i * 128 + 128)

                def chunked(a):
                    return a.rearrange("p (c n) -> p c n", n=CHUNK)

                for q in range(2):
                    cosp, sinp, cosm, sinm = (st[:, q, n * SEG:(n + 1) * SEG] for n in range(4))
                    step(V.tensor_tensor(chunked(k2[:, q]), chunked(cosm),
                                         bend[:, 0].unsqueeze(2).to_broadcast([P, NC, CHUNK]), ALU.mult))
                    step(V.tensor_tensor(chunked(tmp[:]), chunked(sinm),
                                         bend[:, 1].unsqueeze(2).to_broadcast([P, NC, CHUNK]), ALU.mult))
                    V.tensor_tensor(k2[:, q], k2[:, q], tmp[:], ALU.add).then_inc(s["k2r"], 1)
                    dve.wait_ge(s["k2r"], i * 2 + q + 1)
                    step(V.tensor_tensor(c1[:, q], cbq[:, 0], cosp, ALU.mult))
                    step(V.tensor_tensor(tmp[:], cbq[:, 1], sinp, ALU.mult))
                    V.tensor_tensor(c1[:, q], c1[:, q], tmp[:], ALU.add).then_inc(s["q1"], 1)
                    dve.wait_ge(s["q1"], i * 2 + q + 1)
                    step(V.scalar_tensor_tensor(c2[:, q], cbr[:, 2], im_sign[:, 0:1], cosp, ALU.mult, ALU.mult))
                    step(V.tensor_tensor(tmp[:], cbr[:, 3], sinp, ALU.mult))
                    V.tensor_tensor(c2[:, q], c2[:, q], tmp[:], ALU.subtract).then_inc(s["q2"], 1)
                    if q == 0:
                        dve.wait_ge(s["q2"], i * 2 + 1)
                for q in range(2):
                    step(V.tensor_scalar(state[:, q], state[:, q], flags[:, bass.ds(i, 1)], None, ALU.mult))
                general.read_flag(i)
                with general.taken():
                    n = general.before()
                    once = Steps(dve, s["gen_steps"], n, 15)
                    once(V.tensor_tensor(gen_src[:, 0], gen_src[:, 0], keep[:], ALU.mult))
                    V.tensor_copy(gen_src[:, 1], gen_src[:, 1]).then_inc(s["gen_src_in"], 1)
                    for q in range(2):
                        decay, cosine, sine, keys = (gen_st[:, a] for a in range(4))
                        dve.wait_ge(s["gen_dma"], n * 512 + q * 256 + 256)
                        once(V.tensor_scalar(gen_w, cosine, re_row[:, 0:1], None, ALU.mult))
                        once(V.scalar_tensor_tensor(gen_w, sine, im_row[:, 0:1], gen_w, ALU.mult, ALU.add))
                        once(V.tensor_tensor(keys, keys, gen_w, ALU.mult))
                        once(V.tensor_tensor(tmp[:], cbq[:, 0], cosine, ALU.mult))
                        once(V.tensor_tensor(gen_w, cbq[:, 1], sine, ALU.mult))
                        once(V.tensor_tensor(tmp[:], tmp[:], gen_w, ALU.add))
                        once(V.memset(gen_y[:, q], 0.0))
                        apart(dve)
                        with dve.Fori(0, HD) as p:
                            at_p = n * (2 * HD) + q * HD + p
                            loop = Steps(dve, s["gen_loop"], at_p, 3)
                            V.tensor_copy(sel[:, 0].rearrange("p (h k) -> p h k", h=2),
                                          ident[:].rearrange("p (h w) -> p h w", h=2)[:, :, bass.ds(p, 1)]
                                          .to_broadcast([P, 2, 2 * NK])).then_inc(s["gen_sel"], 1)
                            V.tensor_copy(sel[:, 1], pick[:, bass.ds(p * -1 + HD, P)]).then_inc(s["gen_sel"], 1)
                            dve.wait_ge(s["gen_x_ps"], at_p + 1)
                            loop(V.tensor_tensor(gen_p, bank[5][:], keys, ALU.mult))
                            loop(V.tensor_tensor_scan(gen_w, decay, gen_p, 0.0, ALU.mult, ALU.add))
                            V.tensor_tensor(gen_p, gen_w, tmp[:], ALU.mult).then_inc(s["gen_prod"], 1)
                            dve.wait_ge(s["gen_y_ps"], at_p + 1)
                            loop(V.tensor_tensor(gen_y[:, q], gen_y[:, q], bank[6][:], ALU.add))
                            apart(dve)
                        V.tensor_copy(okf[:, 0:1], okf[:, 0:1]).then_inc(s["gen_done"], 1)
                        dve.wait_ge(s["gen_done"], n * 2 + q + 1)
                        apart(dve)
                    once.done()
                for q in range(2):
                    dve.wait_ge(s["g_ps"], i * 2 + q + 1)
                    V.tensor_tensor(gs[:, q], bank[q][:].rearrange("p (c n) -> p c n", n=CHUNK),
                                    causal_ok[:, :].unsqueeze(1).to_broadcast([P, NC, CHUNK]), ALU.mult)\
                        .then_inc(s["gsm"], 1)
                for q in range(2):
                    emid, gend, rho = (st[:, q, 4 * SEG + n * NC:4 * SEG + (n + 1) * NC] for n in range(3))
                    step(V.tensor_tensor(fdec[:, q, 0, 0:NC - 1], gend[:, 0:NC - 1], emid[:, 1:NC], ALU.mult))
                    step(V.tensor_tensor(fdec[:, q, 1, 0:NC - 1], fdec[:, q, 0, 0:NC - 1], rho[:, 1:NC], ALU.mult))
                    step(V.tensor_scalar(ss[:, q, 0], state[:, q], emid[:, 0:1], None, ALU.mult))
                dve.wait_ge(s["u_ps"], i * 2 + 2)
                uq = [bank[7], bank[2]]
                for c in range(NC):
                    for q in range(2):
                        u = uq[q][:, c * HD:(c + 1) * HD]
                        if c == 0:
                            rho0 = st[:, q, 4 * SEG + 2 * NC:4 * SEG + 2 * NC + 1]
                            ins = V.scalar_tensor_tensor(vv[:, q, 0], ss[:, q, 0], rho0, u, ALU.mult, ALU.add)
                        else:
                            ins = V.scalar_tensor_tensor(vv[:, q, c], vv[:, q, c - 1], fdec[:, q, 1, c - 1:c], u,
                                                         ALU.mult, ALU.add)
                        step(ins)
                for q in range(2):
                    V.tensor_tensor(ss[:, q, 1:NC], vv[:, q, 0:NC - 1],
                                    fdec[:, q, 0, 0:NC - 1].unsqueeze(2).to_broadcast([P, NC - 1, HD]), ALU.mult)\
                        .then_inc(s["states"], 1)
                    step(V.tensor_scalar(state[:, q], vv[:, q, NC - 1], st[:, q, 4 * SEG + 2 * NC - 1:4 * SEG + 2 * NC],
                                         None, ALU.mult))
                dve.wait_ge(s["zsilu"], i * 2 + 2)
                for q in range(2):
                    dve.wait_ge(s["y_ps"], i * 2 + q + 1)
                    apart(dve)
                    with general.taken():
                        n = general.before()
                        V.tensor_tensor(bank[3 + q][:], bank[3 + q][:], gen_y[:, q], ALU.add)\
                            .then_inc(s["gen_add"], 1)
                        dve.wait_ge(s["gen_add"], n * 2 + q + 1)
                        apart(dve)
                        if q == 1:
                            general.count()
                    step(V.scalar_tensor_tensor(tmp[:], cv[:, q], dsk[:, q:q + 1], bank[3 + q][:], ALU.mult, ALU.add))
                    V.tensor_tensor(gg[:, q], tmp[:], zs[:, q], ALU.mult).then_inc(s["gated"], 1)
                    if q == 0:
                        dve.wait_ge(s["gated"], i * 2 + 1)
                dve.wait_ge(s["o_ps"], i + 1)
                V.tensor_scalar(mv[:, :, 0], bank[6][:, 0:TILES], 1.0 / DI, EPS, ALU.mult, ALU.add)\
                    .then_inc(s["rmsin"], 1)
                dve.wait_ge(s["rms"], i + 1)
                for c in range(TILES):
                    V.scalar_tensor_tensor(x1[:, c], bank[5][:, c * DM:(c + 1) * DM], rstd[:, c:c + 1], xin[:, c],
                                           ALU.mult, ALU.add).then_inc(s["x1r"], 1)
                dve.wait_ge(s["x1r"], i * TILES + TILES)
                layernorm_stats(step, x1, "var2", i)
                dve.wait_ge(s["rstd2"], i + 1)
                for c in range(TILES):
                    V.tensor_scalar(xn[:, c], x1[:, c], mv[:, c, 0:1], rstd[:, c:c + 1], ALU.subtract, ALU.mult)\
                        .then_inc(s["xn2"], 1)
                dve.wait_ge(s["lg_ps"], i + 1)
                top2(step, i, 0, bank[2][0:TOK, 0:E])
                apart(dve)
                with dve.Fori(0, TOK // PAIR) as g:
                    dve.wait_ge(s["t1_ps"], i * NG + g * 2 + 2 + 1)
                    for b in range(2):
                        V.tensor_copy(t1[0:D2, 1].rearrange("p n k f -> p (n k f)")[:, b * 512:(b + 1) * 512],
                                      bank[2 + b][0:D2, :]).then_inc(s["t1b_in"], 1)
                    for half in range(2):
                        dve.wait_ge(s["h_ps"], i * NG + g * 2 + half + 1)
                        dve.wait_ge(s["h_in"], i * NG + g * 2 + 1)
                        V.scalar_tensor_tensor(hpre[:, half].rearrange("p (n f) -> p n f", f=F2),
                                               bank[4 + half][0:F1, :].rearrange("p (n f) -> p n f", f=F2),
                                               scale_u[:, 0:1], bias_u[:, :].unsqueeze(1).to_broadcast([F1, GRP, F2]),
                                               ALU.mult, ALU.add).then_inc(s["hpre_in"], 1)
                dve.wait_ge(s["lgd_ps"], i + 1)
                top2(step, i, 1, bank[6][0:TOK, 0:E])
                dve.wait_ge(s["drows_in"], i * 2 + 2)
                dve.wait_ge(s["xr_in"], i * 16 + 16)
                apart(dve)
                with dve.Fori(0, TOK // PAIR) as g:
                    for half in range(2):
                        dve.wait_ge(s["t2_ps"], i * NG + g * 2 + half + 1 + 1)
                        V.tensor_tensor(t2[0:F2, half].rearrange("p n k f -> p (n k) f"),
                                        bank[half][0:F2, :].rearrange("p (n f) -> p n f", f=D1),
                                        pb[:, bass.ds(g * PAIR + half * GRP, GRP), :].rearrange("p n k -> p (n k)")
                                        .unsqueeze(2).to_broadcast([F2, PAIR, D1]), ALU.mult).then_inc(s["t2_in"], 1)
                    for half in range(2):
                        dve.wait_ge(s["y2_ps"], i * NG + g * 2 + half + 1)
                        n0 = g * PAIR + half * GRP
                        yv = yo[:, half].rearrange("p (n j) -> p n j", j=D2)
                        V.scalar_tensor_tensor(yv, bank[2 + half][0:D1, 0:GRP * D2].rearrange("p (n j) -> p n j", j=D2),
                                               scale_d[:, 0:1], bias_d[:, :].unsqueeze(1).to_broadcast([D1, GRP, D2]),
                                               ALU.mult, ALU.add).then_inc(s["ys"], 1)
                        dve.wait_ge(s["ys"], i * NG + g * 2 + half + 1 + 1)
                        V.tensor_tensor(xr[0:D1, bass.ds(n0, GRP), :], xr[0:D1, bass.ds(n0, GRP), :], yv, ALU.add)\
                            .then_inc(s["out_sb"], 1)
                step.done()

        @block.tensor
        def _(pe):
            T = nc.tensor
            NG = TOK // GRP

            def mm(o, l, r, start=True, stop=True):
                return T.matmul(o, l, r, start=start, stop=stop)

            pe.wait_ge(s["weights"], 16 * 23 + 2)
            pe.wait_ge(s["selfs"], 14)
            general = General(pe, "pe")
            for free in ("t1_ps", "t2_ps",):
                pe.sem_inc(s[free], 1)
            with pe.Fori(0, NSEG) as i:
                def transposes(src, dst):
                    for c in range(TILES):
                        ins = T.transpose(dst[:, c * P:(c + 1) * P], src[:, c * P:(c + 1) * P], ident[:])
                    return ins

                def rows(layer):
                    ps = bank[6] if layer == 0 else bank[7]
                    apart(pe)
                    for k in range(2):
                        mm(ps[0:1, 128 + k * TOK:128 + (k + 1) * TOK], pr[:, 6 + k:7 + k], ident[0:TOK, 0:TOK])
                    for k in range(2):
                        ins = mm(ps[0:F1, 256 + k * TOK:256 + (k + 1) * TOK],
                                 pr[:, 4 + k:5 + k].to_broadcast([TOK, F1]), ident[0:TOK, 0:TOK])
                    ins.then_inc(s["row_ps"], 1)

                pe.wait_ge(s["xn1"], i * TILES + TILES)
                transposes(xn[:].rearrange("p c d -> p (c d)"), bank[0]).then_inc(s["xnT_ps"], 1)
                pe.wait_ge(s["xnT"], i + 1)
                mm(bank[1][0:LORA, :], w1[:], xnT[:]).then_inc(s["w1_ps"], 1)
                for c in range(TILES):
                    ins = mm(bank[2][:, c * HEADS:(c + 1) * HEADS], xnT[:, c * P:(c + 1) * P], win[:, C_DT:C_DT + HEADS])
                ins.then_inc(s["dt_ps"], 1)
                for a, col in enumerate((C_X, C_X + P, C_BC)):
                    mm(bank[3 + a][:], win[:, col:col + P], xnT[:]).then_inc(s["xbc_ps"], 1)
                for a in range(2):
                    mm(bank[6 + a][:], win[:, C_Z + a * P:C_Z + (a + 1) * P], xnT[:]).then_inc(s["z_ps"], 1)
                pe.wait_ge(s["lora"], i + 1)
                mm(bank[0][:], w2[:], lo[0:LORA, :]).then_inc(s["th_ps"], 1)
                pe.wait_ge(s["dt_tok"], i + 1)
                transposes(dtx[:].rearrange("p a k -> p (a k)"), bank[1]).then_inc(s["dtr_ps"], 1)
                for q in range(2):
                    pe.wait_ge(s["xc"], i * 3 + q + 1)
                    transposes(cv[:, q], bank[3 + q]).then_inc(s["x_tr"], 1)
                pe.wait_ge(s["viol_in"], i + 1)
                mm(bank[2][:, 64:65], ones[:], viol[:, 1:2]).then_inc(s["ok_ps"], 1)
                pe.wait_ge(s["zsilu"], i * 2 + 2)
                for q in range(2):
                    pe.wait_ge(s["k2r"], i * 2 + q + 1)
                    transposes(k2[:, q], bank[5 + q]).then_inc(s["bt_ps"], 1)
                    pe.wait_ge(s["keys"], i * 128 + 128)
                    pe.wait_ge(s["q1"], i * 2 + q + 1)
                    for c in range(NC):
                        for h in range(2):
                            half = slice(h * CHUNK, (h + 1) * CHUNK)
                            cols = slice(c * CHUNK, (c + 1) * CHUNK)
                            if c == h == 0:
                                apart(pe)
                            ins = mm(bank[q][half, cols], k1[half, q, cols], c1[half, q, cols])
                    ins.then_inc(s["g_ps"], 1)
                for q in range(2):
                    pe.wait_ge(s["btc"], i * 8 + 4 * q + 4)
                    pe.wait_ge(s["xds"], i * 8 + 4 * q + 4)
                    for c in range(NC):
                        for h in range(2):
                            half = slice(h * CHUNK, (h + 1) * CHUNK)
                            if c == h == 0:
                                apart(pe)
                            ins = mm([bank[7], bank[2]][q][half, c * HD:(c + 1) * HD], bt[half, q, c], xd[half, q, c])
                    ins.then_inc(s["u_ps"], 1)
                general.read_flag(i)
                with general.taken():
                    n = general.before()
                    for q in range(2):
                        with pe.Fori(0, HD) as p:
                            at_p = n * (2 * HD) + q * HD + p
                            pe.wait_ge(s["gen_sel"], at_p * 2 + 2)
                            mm(bank[5][:], sel[:, 0], cv[:, q]).then_inc(s["gen_x_ps"], 1)
                            pe.wait_ge(s["gen_prod"], at_p + 1)
                            mm(bank[6][:], sel[:, 1], gen_p).then_inc(s["gen_y_ps"], 1)
                    general.count()
                for q in range(2):
                    pe.wait_ge(s["gsm"], i * 2 + q + 1)
                    pe.wait_ge(s["q2"], i * 2 + q + 1)
                    pe.wait_ge(s["states"], i * 2 + q + 1)
                    for c in range(NC):
                        for h in range(2):
                            half = slice(h * CHUNK, (h + 1) * CHUNK)
                            cols = slice(c * CHUNK, (c + 1) * CHUNK)
                            if c == h == 0:
                                apart(pe)
                            mm(bank[3 + q][half, cols], xd[half, q, c], gs[half, q, c], True, False)
                            ins = mm(bank[3 + q][half, cols], ss[half, q, c], c2[half, q, cols], False, True)
                    ins.then_inc(s["y_ps"], 1)
                pe.wait_ge(s["gsq"], i * 2 + 2)
                for c in range(TILES):
                    rows_ = slice(c * P, (c + 1) * P)
                    for q in range(2):
                        mm(bank[6][:, c:c + 1], gq[:, q, rows_], ones[:, 0:1], q == 0, q == 1)
                for c in range(TILES):
                    rows_ = slice(c * P, (c + 1) * P)
                    for q in range(2):
                        ins = mm(bank[5][:, c * DM:(c + 1) * DM], gg[:, q, rows_], wout[:, q], q == 0, q == 1)
                ins.then_inc(s["o_ps"], 1)
                pe.wait_ge(s["xn2"], i * TILES + TILES)
                transposes(xn[:].rearrange("p c d -> p (c d)"), bank[7]).then_inc(s["x2T_ps"], 1)
                pe.wait_ge(s["x2T"], i + 1)
                xt = xnT[:].rearrange("p (n r) -> p r n", r=RPT)
                for r in range(RPT):
                    ins = mm(bank[2][0:TOK, 0:E], xt[:, r], wup[:, r], r == 0, r == RPT - 1)
                ins.then_inc(s["lg_ps"], 1)
                pe.wait_ge(s["probs"], i * 2 + 1)
                rows(0)
                pe.wait_ge(s["rows_in"], i * 2 + 2)
                apart(pe)
                with pe.Fori(0, TOK // PAIR) as g:
                    where = []
                    for half in range(2):
                        _, v = nc.values_load_multi_w_load_instructions(
                            offs[0:1, 0].rearrange("p n k -> p (n k)")[:, bass.ds(g * (2 * PAIR) + half * PAIR, PAIR)],
                            engines=[pe.engine], min_val=0, max_val=(E - 1) * F1,
                            skip_runtime_bounds_check_because="max_index of 64 logits gives 0 to 63")
                        where.append(v)
                    for half in range(2):
                        pe.wait_ge(s["xp_in"], i * NG + g * 2 + half + 1)
                        pe.wait_ge(s["t1a_in" if half == 0 else "t1b_in"], i * NG + g * 2 + 1)
                        for n in range(GRP):
                            for k in range(2):
                                col = (2 * n + k) * F1
                                b = bank[2 * half + col // 512]
                                ins = mm(b[0:D2, col % 512:col % 512 + F1], xp[:, half, n, k],
                                         au[:, :, :].rearrange("p e f -> p (e f)")[:, bass.ds(where[half][2 * n + k], F1)])
                        ins.then_inc(s["t1_ps"], 1)
                    for half in range(2):
                        pe.wait_ge(s["t1a_in" if half == 0 else "t1b_in"], i * NG + g * 2 + 3)
                        pe.wait_ge(s["hpre_in"], i * NG + g * 2 + 1)
                        for n in range(GRP):
                            for k in range(2):
                                ins = mm(bank[4 + half][0:F1, n * F2:(n + 1) * F2], t1[:, half, n, k],
                                         bu[:, :, :].rearrange("p e f -> p (e f)")[:, bass.ds(where[half][2 * n + k], F2)],
                                         k == 0, k == 1)
                        ins.then_inc(s["h_ps"], 1)
                pe.wait_ge(s["h_in"], i * NG + NG + 1)
                for f in range(F2):
                    ins = mm(bank[6][0:TOK, 0:E], hh[:, :, f], wdn[:, f], f == 0, f == F2 - 1)
                ins.then_inc(s["lgd_ps"], 1)
                pe.wait_ge(s["probs"], i * 2 + 2)
                rows(1)
                pe.wait_ge(s["drows_in"], i * 2 + 2)
                apart(pe)
                with pe.Fori(0, TOK // PAIR) as g:
                    where = []
                    for half in range(2):
                        _, v = nc.values_load_multi_w_load_instructions(
                            offs[0:1, 1].rearrange("p n k -> p (n k)")[:, bass.ds(g * (2 * PAIR) + half * PAIR, PAIR)],
                            engines=[pe.engine], min_val=0, max_val=(E - 1) * D1,
                            skip_runtime_bounds_check_because="max_index of 64 logits gives 0 to 63")
                        where.append(v)
                    for half in range(2):
                        pe.wait_ge(s["hs_in"], i * NG + g * 2 + half + 1)
                        pe.wait_ge(s["t2_in"], i * NG + g * 2 + 1)
                        for n in range(GRP):
                            for k in range(2):
                                ins = mm(bank[half][0:F2, (2 * n + k) * D1:(2 * n + k + 1) * D1], hs[:, half, n],
                                         ad[:, :, :].rearrange("p e f -> p (e f)")[:, bass.ds(where[half][2 * n + k], D1)])
                        ins.then_inc(s["t2_ps"], 1)
                    for half in range(2):
                        pe.wait_ge(s["t2_in"], i * NG + g * 2 + half + 1 + 1)
                        pe.wait_ge(s["ys"], i * NG + g * 2 + 1)
                        for n in range(GRP):
                            for k in range(2):
                                ins = mm(bank[2 + half][0:D1, n * D2:(n + 1) * D2], t2[:, half, n, k],
                                         bd[:, :, :].rearrange("p e f -> p (e f)")[:, bass.ds(where[half][2 * n + k], D2)],
                                         k == 0, k == 1)
                        ins.then_inc(s["y2_ps"], 1)


DVE_STEPS = 130


_ORDER = ["L0_attn_x", "w_in", "conv_w", "conv_b", "dt_bias", "lam_base", "th_base", "th_w1", "th_w2", "eta", "d_skip",
          "norm_w", "w_out", "w_up", "a_up", "b_up", "scale_up", "bias_up", "w_down", "a_down", "b_down",
          "scale_down", "bias_down", "seg_flags"]


def laid_out(i):
    g = {k: np.asarray(v) for k, v in i.items()}
    xf = g["L0_attn_x"].reshape(BATCH * LENGTH, DM)
    wi = g["L0_attn_in_proj_w"]
    bc = np.concatenate([np.arange(0, 2 * NK, 2), np.arange(1, 2 * NK, 2)])
    bc = np.concatenate([bc, 2 * NK + bc])
    rows = np.concatenate([np.arange(2 * DI), 2 * DI + bc, np.arange(2 * DI + 4 * NK, NW)])
    chans = np.concatenate([np.arange(DI), DI + bc])
    def col(a, n=P):
        return np.repeat(a.reshape(1, -1), n, 0)
    first = np.ones(NSEG, np.float32)
    first[::LENGTH // SEG] = 0.0
    return {
        "L0_attn_x": np.concatenate([xf, xf[:SEG]], 0),
        "w_in": wi[rows].T,
        "conv_w": g["L0_attn_conv_w"][chans].reshape(3, P, TAPS).transpose(1, 0, 2),
        "conv_b": g["L0_attn_conv_b"][chans].reshape(3, P).T,
        "dt_bias": col(g["L0_attn_dt_bias"]),
        "lam_base": g["L0_attn_lambda_base"].reshape(P, 1),
        "th_base": g["L0_attn_theta_base"].reshape(P, 1),
        "th_w1": g["L0_attn_theta_w1"],
        "th_w2": g["L0_attn_theta_w2"],
        "eta": g["L0_attn_viscosity_eta"].reshape(P, 1),
        "d_skip": np.repeat(g["L0_attn_D"], HD).reshape(2, P).T,
        "norm_w": g["L0_attn_norm_w"].reshape(2, P).T,
        "w_out": g["L0_attn_out_proj_w"].T.reshape(2, P, DM).transpose(1, 0, 2),
        "w_up": g["L0_ffn_W_up"].T.reshape(RPT, P, E).transpose(1, 0, 2),
        "a_up": g["L0_ffn_A_up"].transpose(2, 0, 1),
        "b_up": g["L0_ffn_B_up"].transpose(2, 0, 1),
        "scale_up": col(g["L0_ffn_scale_up"], F1),
        "bias_up": g["L0_ffn_bias_up"].reshape(F1, F2),
        "w_down": g["L0_ffn_W_down"].reshape(E, F1, F2).transpose(1, 2, 0),
        "a_down": g["L0_ffn_A_down"].transpose(2, 0, 1),
        "b_down": g["L0_ffn_B_down"].transpose(2, 0, 1),
        "scale_down": col(g["L0_ffn_scale_down"], D1),
        "bias_down": g["L0_ffn_bias_down"].reshape(D1, D2),
        "seg_flags": col(first),
    }


def kernel(**inputs):
    import concourse.bacc as _bacc
    from concourse.bass_utils import run_bass_kernel_spmd as _run

    nc = _bacc.Bacc("TRN2", target_bir_lowering=False, num_devices=1)
    arrays, args = {}, []
    laid = laid_out(inputs)
    for name in _ORDER:
        a = np.ascontiguousarray(laid[name])
        arrays[f"in_{name}"] = a
        args.append(nc.dram_tensor(f"in_{name}", a.shape, mybir.dt.from_np(a.dtype), kind="ExternalInput").ap())
    args.append(nc.dram_tensor("out_0", (BATCH * LENGTH, DM), FP32, kind="ExternalOutput").ap())
    for name in ("x1_scratch", "x2_scratch"):
        args.append(nc.dram_tensor(name, (BATCH * LENGTH, DM), FP32, kind="Internal").ap())
    block_kernel(nc, *args)
    r = _run(nc, [arrays], core_ids=[0])
    return r.results[0]["out_0"].reshape(BATCH, LENGTH, DM)
```

```python
import math
from contextlib import ExitStack

import numpy as np

import concourse.bass as bass
from concourse import mybir

FP32 = mybir.dt.float32
I32 = mybir.dt.int32
U32 = mybir.dt.uint32
ALU = mybir.AluOpType
ACT = mybir.ActivationFunctionType
AX = mybir.AxisListType

P = 128
BATCH, LENGTH, DM = 4, 1024, 128
DI = 256
HEADS, HD = 4, 64
NK = 32
LORA = 48
TAPS = 4
CHUNK = 64
SEG = 512
NSEG = BATCH * LENGTH // SEG
TILES = SEG // P
NC = SEG // CHUNK
MID = CHUNK // 2 - 1
LIMIT = 30.0
EPS = 1e-5
TWO_PI_HI = 6.28125
TWO_PI_LO = 2 * math.pi - 6.28125
ROUND = 12582912.0
PI_SAFE = 3.1415925

E = 64
D1 = D2 = 32
F1 = F2 = 64
TOK = SEG * DM // (D1 * D2)
RPT = D1 * D2 // DM
GRP = 8
UNIT = GRP // 2
NG = TOK // GRP
NU = TOK // UNIT

NW = 2 * DI + 2 * 2 * NK + HEADS
C_Z, C_X, C_BC, C_DT = 0, DI, 2 * DI, 2 * DI + 4 * NK


def block_kernel(nc, x, w_in, conv_w, conv_b, dt_bias, lam_base, th_base, th_w1, th_w2, eta, d_skip,
                 norm_w, w_out, w_up, a_up, b_up, scale_up, bias_up, w_down, a_down, b_down,
                 scale_down, bias_down, seg_flags, out, x1_scratch, x2_scratch):
    ctx = ExitStack()
    with ctx:
        def sb(name, shape, dt=FP32):
            return ctx.enter_context(nc.sbuf_tensor(name, shape, dt))

        def sem(name):
            return ctx.enter_context(nc.semaphore(name))

        ident = sb("ident", [P, P])
        ones = sb("ones", [P, P])
        causal = sb("causal", [P, CHUNK])
        keep = sb("keep", [P, SEG])
        im_sign = sb("im_sign", [P, 1])
        neg_sign = sb("neg_sign", [P, 1])
        re_row = sb("re_row", [P, 1])
        im_row = sb("im_row", [P, 1])
        minus_half = sb("minus_half", [P, TILES])
        half_pi = sb("half_pi", [P, 1])
        pick = sb("pick", [P, 2 * P])
        win = sb("win", [P, NW])
        w1 = sb("w1", [P, LORA])
        w2 = sb("w2", [LORA, P])
        wout = sb("wout", [P, 2, DM])
        wup = sb("wup", [P, RPT, E])
        cw = sb("cw", [P, 3, TAPS])
        cb = sb("cb", [P, 3])
        dtb = sb("dtb", [P, HEADS])
        lamb = sb("lamb", [P, 1])
        thb = sb("thb", [P, 1])
        etas = sb("etas", [P, 1])
        dsk = sb("dsk", [P, 2])
        nw = sb("nw", [P, 2])
        flags = sb("flags", [P, NSEG])
        tab = sb("tab", [P, E, F1])
        wdn = sb("wdn", [P, F2 // 2, E])
        bias_u = sb("bias_u", [F1, F2])
        bias_d = sb("bias_d", [D1, D2])
        scale_u = sb("scale_u", [F1, 1])
        scale_d = sb("scale_d", [D1, 1])

        xin = sb("xin", [P, TILES, DM])
        x1 = sb("x1", [P, TILES, DM])
        xn = sb("xn", [P, TILES, DM])
        xnT = sb("xnT", [P, SEG])
        xpre = sb("xpre", [P, 3, TAPS - 1 + SEG])
        cv = sb("cv", [P, 3, SEG])
        zs = sb("zs", [P, 2, SEG])
        tmp = sb("tmp", [P, SEG])
        tmp_p = sb("tmp_p", [P, SEG])
        dtx = sb("dtx", [P, TILES * HEADS, NK])
        stats = sb("stats", [P, TILES, 6])
        mv = sb("mv", [P, TILES, 2])
        rstd = sb("rstd", [P, TILES])
        dts = sb("dts", [P, 8, TILES * HEADS])
        phi = sb("phi", [P, NC + 1])
        ksm = sb("ksm", [P, 2, NC])
        fsm = sb("fsm", [P, 3, NC])
        mref = sb("mref", [P, 2, NC])
        bend = sb("bend", [P, NC])
        causal_ok = sb("causal_ok", [P, CHUNK])
        state = sb("state", [P, 2, HD])
        fdec = sb("fdec", [P, 2, 2, NC])
        viol = sb("viol", [P, 2])
        okf = sb("okf", [P, 2])
        oki = sb("oki", [1, 1], I32)
        lg = sb("lg", [TOK, E])
        top = sb("top", [TOK, 8])
        topi = sb("topi", [TOK, 8], U32)
        pr = sb("pr", [TOK, 8])
        offs = sb("offs", [1, 2, TOK, 2], I32)
        pb = sb("pb", [P, 2, TOK, 2])
        sel = sb("sel", [P, 2, P])

        xir = sb("xir", [2 * D1, TOK, D2])
        xp = sb("xp", [P, 2, GRP, 2, D2])
        t1 = sb("t1", [P, 2, UNIT, 2, F1])
        hpre = sb("hpre", [F1, 2, GRP, F2])
        hh = sb("hh", [P, TOK, F2 // 2])
        hs = sb("hs", [P, 2, GRP, 2, F2])
        t2 = sb("t2", [P, 2, GRP, 2, D1])

        arena = sb("arena", [P, 33 * SEG + 12 * NC + SEG])
        at = [0]

        def carve(words):
            at[0] += words
            return arena[:, at[0] - words:at[0]]

        BLK = 3 * NC + 2 * SEG
        st = carve(4 * BLK).rearrange("p (a n) -> p a n", a=2)
        cbr = carve(4 * SEG).rearrange("p (a n) -> p a n", a=4)
        k2 = carve(2 * SEG).rearrange("p (a n) -> p a n", a=2)
        c1 = carve(2 * SEG).rearrange("p (a n) -> p a n", a=2)
        c2 = carve(2 * SEG).rearrange("p (a n) -> p a n", a=2)
        cbq = carve(2 * SEG).rearrange("p (a n) -> p a n", a=2)
        late = at[0]
        lo = carve(SEG)
        th = carve(SEG)
        nl = carve(SEG)
        om = carve(SEG)
        rr = carve(SEG)
        ang = carve(SEG)
        dd = carve(SEG)
        dm = carve(SEG)
        ep = carve(SEG)
        em = carve(SEG)
        sn = carve(SEG)
        cs = carve(SEG)
        kk = carve(SEG)
        at[0] = late
        xd = carve(2 * SEG).rearrange("p (a c n) -> p a c n", a=2, n=HD)
        bt = carve(2 * SEG).rearrange("p (a c n) -> p a c n", a=2, n=2 * NK)
        gs = carve(2 * SEG).rearrange("p (a c n) -> p a c n", a=2, n=CHUNK)
        vv = carve(2 * SEG).rearrange("p (a c n) -> p a c n", a=2, n=HD)
        ss = carve(2 * SEG).rearrange("p (a c n) -> p a c n", a=2, n=HD)
        gg = carve(2 * SEG).rearrange("p (a n) -> p a n", a=2)
        gq = carve(2 * SEG).rearrange("p (a n) -> p a n", a=2)
        at[0] = late + 4 * SEG
        gen_st = carve(4 * SEG).rearrange("p (a n) -> p a n", a=4)
        gen_w = carve(SEG)
        gen_p = carve(SEG)
        at[0] = late + 12 * SEG
        gen_y = carve(2 * SEG).rearrange("p (a n) -> p a n", a=2)
        ec = sb("ec", [P, 2 * (BLK + SEG)])
        gen_src = sb("gen_src", [P, 2, SEG])

        bank = [ctx.enter_context(nc.psum_tensor(f"bank{n}", [P, 512], FP32)) for n in range(8)]

        names = ("weights zeros consts selfs x_in var1 rstd1 xn1 xnT_ps xnT w1_ps dt_ps xbc_ps z_ps tails lora th_ps "
                 "softneg softexp soft1p softln dt_tok dtr_ps xpre_in conv xc zsilu x_tr rep_bc dtheta thsq "
                 "viol_in ok_ps okd angle sincos expd ecs stacked cbq q1 q2 k2r bt_ps g_ps btc xds u_ps gsm "
                 "states y_ps gated gsq o_ps rmsin rms x1r var2 rstd2 xn2 x2T_ps x2T lg_ps diff pexp probs "
                 "row_ps rows_in scr xi_in xr_in xp_in xrb t1_ps t1_in h_ps hpre_in h_in lgd_ps drow_ps dpexp ddiff dprobs drows_in hs_in t2_ps "
                 "t2_in y2_ps out_sb stored dv fv pl plc sum2 flag gen_src_in gen_dma gen_sel gen_x_ps gen_prod gen_y_ps gen_done gen_steps gen_loop gen_add passed").split()
        s = {n: sem("s_" + n) for n in names}
        block = ctx.enter_context(nc.Block())

        class Steps:

            def __init__(self, eng, sem_, i, per):
                self.eng, self.sem, self.i, self.per, self.n = eng, sem_, i, per, 0

            def __call__(self, ins):
                ins.then_inc(self.sem, 1)
                self.n += 1
                self.eng.wait_ge(self.sem, self.i * self.per + self.n)

            def done(self):
                assert self.n == self.per, (self.n, self.per)

        def apart(eng):
            eng.sem_inc(s["passed"], 1)

        class General:

            def __init__(self, eng, name):
                self.eng = eng
                self.runs = eng.alloc_register(f"{name}_general_runs")
                self.flag = eng.alloc_register(f"{name}_factored")
                eng.reg_mov(self.runs, 0)

            def read_flag(self, i):
                self.eng.wait_ge(s["flag"], i + 1)
                apart(self.eng)
                self.eng.reg_load(self.flag, oki[0:1, 0:1])

            def taken(self):
                return self.eng.If_eq(self.flag, 0)

            def before(self):
                return self.eng.snap(self.runs, min_val=0, max_val=NSEG)

            def count(self):
                self.eng.reg_add(self.runs, self.runs, 1)

        PAIRS = ((0, 0), (0, 1), (1, 0), (1, 1))

        def passes(eng, one_pass):
            one_pass(0, True, False)
            with eng.Fori(1, NSEG) as i:
                one_pass(i, True, True)
            one_pass(NSEG, False, True)

        @block.sync
        def _(sp):
            for dst, src in ((win, w_in), (w1, th_w1), (w2, th_w2), (wup, w_up), (cw, conv_w), (cb, conv_b),
                             (dtb, dt_bias), (lamb, lam_base), (thb, th_base), (etas, eta), (dsk, d_skip),
                             (nw, norm_w), (wout, w_out), (flags, seg_flags), (bias_u, bias_up),
                             (bias_d, bias_down), (scale_u, scale_up), (scale_d, scale_down)):
                sp.dma_start(dst[:], src).then_inc(s["weights"], 16)
            sp.dma_start(xin[:], x[0:SEG, :].rearrange("(c p) d -> p c d", p=P)).then_inc(s["x_in"], 16)
            sp.dma_start(tab[0:D1], a_up).then_inc(s["weights"], 16)
            sp.dma_start(tab[D1:2 * D1], b_up).then_inc(s["weights"], 16)
            sp.dma_start(tab[F1:2 * F1, :, 0:D1], a_down).then_inc(s["weights"], 16)
            sp.dma_start(tab[F1:2 * F1, :, D1:2 * D1], b_down).then_inc(s["weights"], 16)
            sp.dma_start(wdn[0:F1], w_down[:, 0:F2 // 2]).then_inc(s["weights"], 16)
            sp.dma_start(wdn[F1:2 * F1], w_down[:, F2 // 2:]).then_inc(s["weights"], 16)
            general = General(sp, "sp")

            def ssm(i):
                sp.wait_ge(s["xc"], i * 3 + 3)
                for h in range(2):
                    for a, (first, second) in enumerate(((0, 0), (NK, NK), (2 * NK, 3 * NK), (3 * NK, 2 * NK))):
                        for r, src in ((0, first), (NK, second)):
                            to = h * 2 * NK + r
                            sp.dma_start(cbr[to:to + NK, a, :], cv[src:src + NK, 2, :]).then_inc(s["rep_bc"], 16)
                sp.wait_ge(s["ecs"], i + 1)
                sp.wait_ge(s["sum2"], i + 1)
                for q, h in PAIRS:
                    src, to = (2 * q + h) * NK, h * 2 * NK
                    sp.dma_start(st[to:to + NK, q], ec[src:src + NK, 0:2 * BLK]).then_inc(s["stacked"], 16)
                    sp.dma_start(st[to + NK:to + 2 * NK, q].rearrange("p (b n) -> p b n", b=2),
                                 ec[src:src + NK, :].rearrange("p (b n) -> p b n", b=2)[:, :, 0:BLK])\
                        .then_inc(s["stacked"], 16)
                general.read_flag(i)
                with general.taken():
                    n = general.before()
                    sp.wait_ge(s["gen_src_in"], n + 1)
                    for q in range(2):
                        if q == 1:
                            sp.wait_ge(s["gen_done"], n * 2 + 1)
                        for h in range(2):
                            for r in range(2):
                                src, to = (2 * q + h) * NK, h * 2 * NK + r * NK
                                for a, array in enumerate((gen_src[:, 0], cs, sn, gen_src[:, 1])):
                                    sp.dma_start(gen_st[to:to + NK, a], array[src:src + NK, :])\
                                        .then_inc(s["gen_dma"], 16)
                    general.count()
                here = i * SEG
                sp.wait_ge(s["x1r"], i * TILES + TILES)
                sp.dma_start(x1_scratch[bass.ds(here, SEG), :].rearrange("(c p) d -> p c d", p=P), x1[:])\
                    .then_inc(s["scr"], 16)
                sp.dma_start(xin[:], x[bass.ds(here + SEG, SEG), :].rearrange("(c p) d -> p c d", p=P))\
                    .then_inc(s["x_in"], 16)
                sp.wait_ge(s["xn2"], i * TILES + TILES)
                sp.dma_start(x2_scratch[bass.ds(here, SEG), :].rearrange("(c p) d -> p c d", p=P), xn[:])\
                    .then_inc(s["scr"], 16)

            def result(j):
                sp.wait_ge(s["out_sb"], j * NG + NG)
                sp.dma_start(out[bass.ds(j * SEG, SEG), :].rearrange("(n r) (q j) -> (r q) n j", r=RPT, j=D2),
                             xir[0:D1]).then_inc(s["stored"], 16)
                sp.wait_ge(s["stored"], j * 16 + 16)

            def tokens(i):
                here = i * SEG
                sp.wait_ge(s["scr"], i * 32 + 32)
                sp.dma_start(xir[D1:2 * D1], x2_scratch[bass.ds(here, SEG), :]
                             .rearrange("(n r) (q j) -> (r q) n j", r=RPT, j=D2)).then_inc(s["xi_in"], 16)
                sp.dma_start(xir[0:D1], x1_scratch[bass.ds(here, SEG), :]
                             .rearrange("(n r) (q j) -> (r q) n j", r=RPT, j=D2)).then_inc(s["xr_in"], 16)

            def one_pass(i, ssm_part, ffn_part):
                if ssm_part:
                    ssm(i)
                if ffn_part:
                    result(i - 1)
                if ssm_part:
                    tokens(i)

            passes(sp, one_pass)
            sp.wait_ge(s["stored"], 16 * NSEG)
            sp.wait_ge(s["x_in"], 16 * (NSEG + 1))
            sp.wait_ge(s["scr"], 32 * NSEG)

        @block.gpsimd
        def _(pool):
            for whole in (arena, ec, xp, t1, hs, t2):
                nc.gpsimd.memset(whole[:], 0.0).then_inc(s["consts"], 1)
            nc.gpsimd.memset(ones[:], 1.0).then_inc(s["consts"], 1)
            nc.gpsimd.memset(ident[:], 0.0).then_inc(s["consts"], 1)
            nc.gpsimd.memset(pick[:], 0.0).then_inc(s["consts"], 1)
            nc.gpsimd.memset(causal[:], 1.0).then_inc(s["consts"], 1)
            nc.gpsimd.memset(keep[:], 1.0).then_inc(s["consts"], 1)
            nc.gpsimd.memset(im_sign[:], 1.0).then_inc(s["consts"], 1)
            nc.gpsimd.memset(neg_sign[:], -1.0).then_inc(s["consts"], 1)
            nc.gpsimd.memset(re_row[:], 1.0).then_inc(s["consts"], 1)
            nc.gpsimd.memset(im_row[:], 0.0).then_inc(s["consts"], 1)
            nc.gpsimd.memset(minus_half[:], -0.5).then_inc(s["consts"], 1)
            nc.gpsimd.memset(half_pi[:], math.pi / 2).then_inc(s["consts"], 1)
            nc.gpsimd.memset(xpre[:], 0.0).then_inc(s["consts"], 1)
            nc.gpsimd.memset(phi[:], 0.0).then_inc(s["consts"], 1)
            nc.gpsimd.memset(state[:], 0.0).then_inc(s["consts"], 1)
            pool.wait_ge(s["consts"], 20)

            def shaped(ins):
                made[0] += 1
                ins.then_inc(s["selfs"], 1)
                pool.wait_ge(s["selfs"], made[0])

            made = [0]
            shaped(nc.gpsimd.affine_select(out=ident[:], in_=ident[:], compare_op=ALU.not_equal, fill=1.0, base=0,
                                           pattern=[[-1, P]], channel_multiplier=1))
            for h in range(2):
                half = slice(h * CHUNK, h * CHUNK + CHUNK)
                shaped(nc.gpsimd.affine_select(out=causal[half], in_=causal[half], compare_op=ALU.is_ge, fill=0.0,
                                               base=0, pattern=[[1, CHUNK]], channel_multiplier=-1))
                for column, value in ((im_sign, -1.0), (neg_sign, 1.0), (re_row, 0.0), (im_row, 1.0)):
                    shaped(nc.gpsimd.memset(column[h * CHUNK + NK:h * CHUNK + 2 * NK], value))
                shaped(nc.gpsimd.memset(pick[half, CHUNK + h * CHUNK:CHUNK + h * CHUNK + 1], 1.0))
            shaped(nc.gpsimd.memset(keep[:].rearrange("p (c n) -> p c n", n=CHUNK)[:, :, 0:1], 0.0))

            G = nc.gpsimd

            def alone(ins, sem_, value):
                ins.then_inc(sem_, 1)
                pool.wait_ge(sem_, value)

            def turned_queries(i):
                step = Steps(pool, s["plc"], i, 6)
                pool.wait_ge(s["rep_bc"], i * 256 + 256)
                apart(pool)
                step(G.tensor_scalar(tmp_p[:], cbr[:, 3], neg_sign[:, 0:1], None, ALU.mult))
                step(G.tensor_tensor(cbq[:, 0], cbr[:, 2], cbr[:, 0], ALU.mult))
                step(G.tensor_tensor(cbq[:, 1], tmp_p[:], cbr[:, 0], ALU.mult))
                step(G.tensor_tensor(tmp_p[:], tmp_p[:], cbr[:, 1], ALU.mult))
                step(G.tensor_tensor(cbq[:, 0], cbq[:, 0], tmp_p[:], ALU.add))
                step(G.tensor_tensor(tmp_p[:], cbr[:, 2], cbr[:, 1], ALU.mult))
                alone(G.tensor_tensor(cbq[:, 1], cbq[:, 1], tmp_p[:], ALU.subtract), s["cbq"], i + 1)
                step.done()

            def second_cos(i):
                pool.wait_ge(s["sincos"], i * 2 + 2)
                pool.wait_ge(s["expd"], i * 4 + 2)
                apart(pool)
                alone(G.tensor_tensor(ec[:, BLK + 2 * SEG:BLK + 3 * SEG], em, cs, ALU.mult), s["sum2"], i + 1)

            def norms(i):
                step = Steps(pool, s["pl"], i, 1)
                pool.wait_ge(s["rmsin"], i + 1)
                alone(G.tensor_tensor(rstd[:], mv[:, :, 0], minus_half[:], ALU.pow), s["rms"], i + 1)
                pool.wait_ge(s["var2"], i + 1)
                apart(pool)
                step(G.tensor_copy(rstd[:], mv[:, :, 1]))
                alone(G.tensor_tensor(rstd[:], rstd[:], minus_half[:], ALU.pow), s["rstd2"], i + 1)
                step.done()

            def weighted(j, groups):
                for g in groups:
                    if g == 0:
                        pool.wait_ge(s["xi_in"], j * 16 + 16)
                        pool.wait_ge(s["rows_in"], j * 2 + 2)
                        apart(pool)
                    if g >= 2:
                        pool.wait_ge(s["t1_ps"], j * NU + 2 * (g - 1))
                    n = slice(g * GRP, (g + 1) * GRP)
                    alone(G.tensor_tensor(xp[0:D1, g % 2], xir[D1:2 * D1, n].unsqueeze(2).to_broadcast([D1, GRP, 2, D2]),
                                          pb[D1:2 * D1, 0, n].unsqueeze(3).to_broadcast([D1, GRP, 2, D2]), ALU.mult),
                          s["xp_in"], j * NG + g + 1)

            def weighted_hidden(j, groups):
                for g in groups:
                    if g == 0:
                        pool.wait_ge(s["drows_in"], j * 2 + 2)
                        apart(pool)
                    if g >= 2:
                        pool.wait_ge(s["t2_ps"], j * NG + g - 1)
                    n = slice(g * GRP, (g + 1) * GRP)
                    for half in range(2):
                        f = slice(half * (F2 // 2), (half + 1) * (F2 // 2))
                        rows = slice(half * F1, (half + 1) * F1)
                        alone(G.tensor_tensor(hs[F1:2 * F1, g % 2, :, :, f],
                                              hh[rows, n].unsqueeze(2).to_broadcast([F1, GRP, 2, F2 // 2]),
                                              pb[rows, 1, n].unsqueeze(3).to_broadcast([F1, GRP, 2, F2 // 2]),
                                              ALU.mult), s["hs_in"], j * 2 * NG + 2 * g + half + 1)

            def residual(j):
                pool.wait_ge(s["xr_in"], j * 16 + 16)
                apart(pool)
                alone(G.tensor_tensor(xir[0:D1], xir[0:D1], bias_d[:, :].unsqueeze(1).to_broadcast([D1, TOK, D2]),
                                      ALU.add), s["xrb"], j + 1)

            def one_pass(i, ssm_part, ffn_part):
                if ssm_part:
                    pool.wait_ge(s["var1"], i + 1)
                    alone(G.tensor_tensor(rstd[:], mv[:, :, 1], minus_half[:], ALU.pow), s["rstd1"], i + 1)
                if ffn_part:
                    weighted(i - 1, range(0, 5))
                if ssm_part:
                    pool.wait_ge(s["dtheta"], i + 1)
                    alone(G.tensor_tensor(rr[:, :], th[:, :], th[:, :], ALU.mult), s["thsq"], i + 1)
                if ffn_part:
                    weighted(i - 1, range(5, NG))
                if ssm_part:
                    turned_queries(i)
                    second_cos(i)
                if ffn_part:
                    residual(i - 1)
                    weighted_hidden(i - 1, range(NG))
                if ssm_part:
                    norms(i)

            passes(pool, one_pass)

        @block.scalar
        def _(act):
            act.wait_ge(s["consts"], 20)
            act.wait_ge(s["selfs"], 14)
            A = nc.scalar

            def projections(i):
                act.wait_ge(s["xnT_ps"], i + 1)
                A.activation(xnT[:], bank[0][:], ACT.Copy).then_inc(s["xnT"], 1)
                act.wait_ge(s["w1_ps"], i + 1)
                A.activation(lo[0:LORA, :], bank[1][0:LORA, :], ACT.Tanh).then_inc(s["lora"], 1)
                act.wait_ge(s["tails"], i + 1)
                for a, b in enumerate((3, 0, 1)):
                    act.wait_ge(s["xbc_ps"], i * 3 + a + 1)
                    A.activation(xpre[:, a, TAPS - 1:], bank[b][:], ACT.Copy).then_inc(s["xpre_in"], 1)
                for a, b in enumerate((3, 0)):
                    act.wait_ge(s["z_ps"], i * 2 + a + 1)
                    A.activation(zs[:, a, :], bank[b][:], ACT.Silu).then_inc(s["zsilu"], 1)

            def softplus(i):
                act.wait_ge(s["softneg"], i + 1)
                A.activation(dts[:, 2, :], dts[:, 1, :], ACT.Exp).then_inc(s["softexp"], 1)
                act.wait_ge(s["soft1p"], i + 1)
                A.activation(dts[:, 4, :], dts[:, 3, :], ACT.Ln).then_inc(s["softln"], 1)

            def conv_silu(i, a):
                act.wait_ge(s["conv"], i * 3 + a + 1)
                A.activation(cv[:, a, :], cv[:, a, :], ACT.Silu).then_inc(s["xc"], 1)

            def turns(i):
                act.wait_ge(s["angle"], i * 2 + 2)
                A.activation(sn[:, :], ang[:, :], ACT.Sin).then_inc(s["sincos"], 1)
                A.activation(cs[:, :], kk[:, :], ACT.Sin, bias=half_pi[:, 0:1]).then_inc(s["sincos"], 1)
                act.wait_ge(s["okd"], i + 1)
                A.activation(ep[:, :], dd[:, :], ACT.Exp).then_inc(s["expd"], 1)
                A.activation(em[:, :], dm[:, :], ACT.Exp).then_inc(s["expd"], 1)
                A.activation(ec[:, 0:3 * NC], fsm[:, :, :].rearrange("p a c -> p (a c)"), ACT.Exp)\
                    .then_inc(s["expd"], 1)
                A.activation(gen_src[:, 0, :], nl[:, :], ACT.Exp).then_inc(s["expd"], 1)

            def end_keys(i):
                for q in range(2):
                    act.wait_ge(s["bt_ps"], i * 2 + q + 1)
                    for par in range(2):
                        for h in range(2):
                            A.activation(
                                bt[h * CHUNK:(h + 1) * CHUNK, q].rearrange("p (c two) n -> p c two n", two=2)[:, :, par, :],
                                bank[1 + q][par * CHUNK:(par + 1) * CHUNK, :]
                                .rearrange("p (c h n) -> p c h n", c=TILES, h=2)[:, :, h, :],
                                ACT.Copy).then_inc(s["btc"], 1)

            def squares(i):
                for q in range(2):
                    act.wait_ge(s["gated"], i * 2 + q + 1)
                    A.activation(gq[:, q, :], gg[:, q, :], ACT.Square).then_inc(s["gsq"], 1)

            def second_norm(i):
                act.wait_ge(s["x2T_ps"], i + 1)
                A.activation(xnT[:], bank[3][:], ACT.Copy).then_inc(s["x2T"], 1)

            def up_probs(i):
                act.wait_ge(s["diff"], i + 1)
                A.activation(pr[:, 1:2], pr[:, 0:1], ACT.Exp).then_inc(s["pexp"], 1)

            def up(j, units):
                for u in units:
                    act.wait_ge(s["t1_ps"], j * NU + u + 1)
                    if u >= 2:
                        act.wait_ge(s["h_ps"], j * NU + u - 1)
                    A.activation(t1[D1:2 * D1, u % 2].rearrange("p n k f -> p (n k f)"), bank[4 + u % 2][0:D2, :],
                                 ACT.Copy).then_inc(s["t1_in"], 1)

            def gelu(j, groups):
                for g in groups:
                    act.wait_ge(s["hpre_in"], j * NG + g + 1)
                    for half in range(2):
                        f = slice(half * (F2 // 2), (half + 1) * (F2 // 2))
                        A.activation(hh[half * F1:(half + 1) * F1, g * GRP:(g + 1) * GRP], hpre[:, g % 2, :, f],
                                     ACT.Gelu).then_inc(s["h_in"], 1)

            def down_probs(j):
                act.wait_ge(s["ddiff"], j + 1)
                A.activation(pr[:, 1:2], pr[:, 0:1], ACT.Exp).then_inc(s["dpexp"], 1)

            def down(j, groups):
                for g in groups:
                    act.wait_ge(s["t2_ps"], j * NG + g + 1)
                    if g >= 2:
                        act.wait_ge(s["y2_ps"], j * NG + g - 1)
                    A.activation(t2[F1:2 * F1, g % 2].rearrange("p n k f -> p (n k f)"), bank[4 + g % 2][0:F2, :],
                                 ACT.Copy).then_inc(s["t2_in"], 1)

            def one_pass(i, ssm_part, ffn_part):
                j = i - 1
                if ssm_part:
                    projections(i)
                if ffn_part:
                    up(j, (0, 1))
                if ssm_part:
                    softplus(i)
                if ffn_part:
                    up(j, (2, 3))
                if ssm_part:
                    conv_silu(i, 0)
                if ffn_part:
                    up(j, (4, 5))
                if ssm_part:
                    conv_silu(i, 1)
                if ffn_part:
                    up(j, (6, 7))
                if ssm_part:
                    conv_silu(i, 2)
                if ffn_part:
                    gelu(j, (0, 1))
                    up(j, (8, 9))
                    gelu(j, (2,))
                    up(j, (10, 11))
                if ssm_part:
                    turns(i)
                if ffn_part:
                    gelu(j, (3, 4))
                    up(j, (12, 13))
                    gelu(j, (5,))
                    up(j, (14, 15))
                    gelu(j, (6, 7))
                    down_probs(j)
                    down(j, (0, 1))
                if ssm_part:
                    end_keys(i)
                if ffn_part:
                    down(j, (2, 3, 4))
                if ssm_part:
                    squares(i)
                if ffn_part:
                    down(j, (5, 6))
                if ssm_part:
                    second_norm(i)
                if ffn_part:
                    down(j, (7,))
                if ssm_part:
                    up_probs(i)

            passes(act, one_pass)

        @block.vector
        def _(dve):
            dve.wait_ge(s["weights"], 16 * 24)
            dve.wait_ge(s["consts"], 20)
            dve.wait_ge(s["selfs"], 14)
            V = nc.vector
            for q in range(2):
                V.tensor_scalar(wout[:, q], wout[:, q], nw[:, q:q + 1], None, ALU.mult).then_inc(s["weights"], 1)

            def top2(step, i, layer, logits, ps):
                diff, pexp, probs, row_ps, rows_in = (s[n] for n in (
                    ("diff", "pexp", "probs", "row_ps", "rows_in"),
                    ("ddiff", "dpexp", "dprobs", "drow_ps", "drows_in"))[layer])
                step(V.tensor_copy(lg[:], logits))
                apart(dve)
                step(V.max(top[:], lg[:]))
                apart(dve)
                step(V.max_index(topi[:], top[:], lg[:]))
                step(V.tensor_scalar(pr[:, 6:8], topi[:, 0:2], float(F1), None, ALU.mult))
                V.tensor_tensor(pr[:, 0:1], top[:, 1:2], top[:, 0:1], ALU.subtract).then_inc(diff, 1)
                dve.wait_ge(pexp, i + 1)
                step(V.tensor_scalar(pr[:, 2:3], pr[:, 1:2], 1.0, None, ALU.add))
                step(V.reciprocal(pr[:, 4:5], pr[:, 2:3]))
                V.tensor_tensor(pr[:, 5:6], pr[:, 4:5], pr[:, 1:2], ALU.mult).then_inc(probs, 1)
                dve.wait_ge(row_ps, i + 1)
                V.tensor_copy(offs[:, layer].rearrange("p n k -> p k n"),
                              ps[0:1, 128:128 + 2 * TOK].rearrange("p (k n) -> p k n", k=2)).then_inc(rows_in, 1)
                V.tensor_copy(pb[:, layer].rearrange("p n k -> p k n"),
                              ps[:, 256:256 + 2 * TOK].rearrange("p (k n) -> p k n", k=2)).then_inc(rows_in, 1)

            def reduce_angle(step, ang_, k_):
                step(V.tensor_scalar(k_, ang_, 1 / (2 * math.pi), ROUND, ALU.mult, ALU.add))
                step(V.tensor_scalar(k_, k_, ROUND, None, ALU.subtract))
                step(V.scalar_tensor_tensor(ang_, k_, -TWO_PI_HI, ang_, ALU.mult, ALU.add))
                step(V.scalar_tensor_tensor(ang_, k_, -TWO_PI_LO, ang_, ALU.mult, ALU.add))

            def layernorm_stats(step, src, name, i):
                for c in range(TILES):
                    ins = V.bn_stats(stats[:, c], src[:, c])
                    if c < TILES - 1:
                        ins.then_inc(s["dv"], 1)
                        step.n += 1
                    else:
                        step(ins)
                for c in range(TILES):
                    apart(dve)
                    step(V.bn_aggr(mv[:, c], stats[:, c]))
                V.tensor_scalar(mv[:, :, 1], mv[:, :, 1], EPS, None, ALU.add).then_inc(s[name], 1)

            general = General(dve, "dve")

            def first_norm(step, i, first):
                dve.wait_ge(s["x_in"], i * 16 + 16)
                V.tensor_scalar(xpre[:, :, 0:TAPS - 1], xpre[:, :, SEG:], flags[:, bass.ds(i, 1)], None, ALU.mult)\
                    .then_inc(s["tails"], 1)
                layernorm_stats(step, xin, "var1", i)
                dve.wait_ge(s["rstd1"], i + 1)
                if not first:
                    dve.wait_ge(s["scr"], i * 32)
                for c in range(TILES):
                    V.tensor_scalar(xn[:, c], xin[:, c], mv[:, c, 0:1], rstd[:, c:c + 1], ALU.subtract, ALU.mult)\
                        .then_inc(s["xn1"], 1)

            def softplus(step, i):
                dve.wait_ge(s["dt_ps"], i + 1)
                step(V.tensor_tensor(dts[:, 0].rearrange("p (c h) -> p c h", h=HEADS),
                                     bank[2][:, 0:TILES * HEADS].rearrange("p (c h) -> p c h", h=HEADS),
                                     dtb[:, :].unsqueeze(1).to_broadcast([P, TILES, HEADS]), ALU.add))
                V.scalar_tensor_tensor(dts[:, 1], dts[:, 0], -1.0, dts[:, 0], ALU.mult, ALU.min).then_inc(s["softneg"], 1)
                dve.wait_ge(s["softexp"], i + 1)
                V.tensor_scalar(dts[:, 3], dts[:, 2], 1.0, None, ALU.add).then_inc(s["soft1p"], 1)
                dve.wait_ge(s["soft1p"], i + 1)
                step(V.tensor_scalar(dts[:, 5], dts[:, 3], -1.0, None, ALU.add))
                step(V.tensor_scalar(dts[:, 6], dts[:, 5], 1e-30, None, ALU.max))
                step(V.reciprocal(dts[:, 6], dts[:, 6]))
                step(V.tensor_tensor(dts[:, 6], dts[:, 6], dts[:, 2], ALU.mult))
                step(V.tensor_scalar(dts[:, 5], dts[:, 5], 0.0, None, ALU.is_equal))
                step(V.tensor_tensor(dts[:, 5], dts[:, 5], dts[:, 2], ALU.mult))
                dve.wait_ge(s["softln"], i + 1)
                step(V.tensor_tensor(dts[:, 6], dts[:, 6], dts[:, 4], ALU.mult))
                step(V.tensor_tensor(dts[:, 6], dts[:, 6], dts[:, 5], ALU.add))
                step(V.tensor_scalar(dts[:, 0], dts[:, 0], 0.0, None, ALU.max))
                V.tensor_tensor(dtx[:], dts[:, 6].unsqueeze(2).to_broadcast([P, TILES * HEADS, NK]),
                                dts[:, 0].unsqueeze(2).to_broadcast([P, TILES * HEADS, NK]), ALU.add)\
                    .then_inc(s["dt_tok"], 1)

            def conv(step, i, a):
                dve.wait_ge(s["xpre_in"], i * 3 + a + 1)
                step(V.tensor_scalar(cv[:, a], xpre[:, a, 0:SEG], cw[:, a, 0:1], cb[:, a:a + 1], ALU.mult, ALU.add))
                for k in range(1, TAPS):
                    ins = V.scalar_tensor_tensor(cv[:, a], xpre[:, a, k:k + SEG], cw[:, a, k:k + 1], cv[:, a],
                                                 ALU.mult, ALU.add)
                    if k < TAPS - 1:
                        step(ins)
                    else:
                        ins.then_inc(s["conv"], 1)

            def decays(step, i):
                dve.wait_ge(s["th_ps"], i + 1)
                step(V.tensor_scalar(th[:, :], bank[1][:], thb[:, 0:1], math.pi / 2, ALU.add, ALU.min))
                V.tensor_scalar(th[:, :], th[:, :], -math.pi / 2, None, ALU.max).then_inc(s["dtheta"], 1)
                dve.wait_ge(s["dtheta"], i + 1)
                dve.wait_ge(s["dtr_ps"], i + 1)
                step(V.tensor_copy(gen_src[:, 1, :], bank[2][:]))
                step(V.tensor_tensor(om[:, :], th[:, :], gen_src[:, 1, :], ALU.mult))
                step(V.tensor_tensor_scan(ang[:, :], keep[:], om[:, :], 0.0, ALU.mult, ALU.add))
                dve.wait_ge(s["thsq"], i + 1)
                step(V.tensor_scalar(rr[:, :], rr[:, :], etas[:, 0:1], lamb[:, 0:1], ALU.mult, ALU.add))
                step(V.scalar_tensor_tensor(nl[:, :], rr[:, :], -1.0, gen_src[:, 1, :], ALU.mult, ALU.mult))
                step(V.tensor_tensor_scan(rr[:, :], keep[:], nl[:, :], 0.0, ALU.mult, ALU.add))
                rc = rr[:, :].rearrange("p (c n) -> p c n", n=CHUNK)
                step(V.tensor_tensor(dd[:, :].rearrange("p (c n) -> p c n", n=CHUNK), rc,
                                     rc[:, :, MID:MID + 1].to_broadcast([P, NC, CHUNK]), ALU.subtract))
                step(V.tensor_reduce(viol[:, 0:1], dd[:, :], AX.X, ALU.max, apply_absolute_value=True))
                V.tensor_scalar(viol[:, 1:2], viol[:, 0:1], LIMIT, None, ALU.is_le).then_inc(s["viol_in"], 1)

            def phases(step, i):
                step(V.tensor_scalar(phi[:, 0:1], phi[:, NC:NC + 1], flags[:, bass.ds(i, 1)], None, ALU.mult))
                angc = ang[:, :].rearrange("p (c n) -> p c n", n=CHUNK)
                step(V.tensor_copy(ksm[:, 0], angc[:, :, CHUNK - 1]))
                reduce_angle(step, ksm[:, 0], ksm[:, 1])
                step(V.tensor_tensor_scan(phi[:, 1:], ones[:, 0:NC], ksm[:, 0], phi[:, 0:1], ALU.mult, ALU.add))
                step(V.tensor_tensor(angc, angc, phi[:, 0:NC].unsqueeze(2).to_broadcast([P, NC, CHUNK]), ALU.add))
                reduce_angle(step, ang[:, :], kk[:, :])
                V.tensor_scalar(ang[:, :], ang[:, :], PI_SAFE, -PI_SAFE, ALU.min, ALU.max).then_inc(s["angle"], 1)
                dve.wait_ge(s["angle"], i * 2 + 1)
                V.scalar_tensor_tensor(kk[:, :], ang[:, :], -1.0, ang[:, :], ALU.mult, ALU.min).then_inc(s["angle"], 1)

            def exponents(step, i):
                rc = rr[:, :].rearrange("p (c n) -> p c n", n=CHUNK)
                dve.wait_ge(s["ok_ps"], i + 1)
                step(V.tensor_scalar(okf[:, 0:1], bank[1][:, 64:65], P - 0.5, None, ALU.is_gt))
                step(V.tensor_scalar(okf[:, 1:2], okf[:, 0:1], -1.0, 1.0, ALU.mult, ALU.add))
                V.tensor_copy(oki[:], okf[0:1, 0:1]).then_inc(s["flag"], 1)
                step(V.tensor_scalar(causal_ok[:], causal[:], okf[:, 0:1], None, ALU.mult))
                step(V.tensor_scalar(mref[:, 0], rc[:, :, MID], okf[:, 0:1], None, ALU.mult))
                step(V.scalar_tensor_tensor(mref[:, 1], rc[:, :, CHUNK - 1], okf[:, 1:2], mref[:, 0],
                                            ALU.mult, ALU.add))
                step(V.tensor_copy(fsm[:, 0], mref[:, 0]))
                step(V.tensor_tensor(fsm[:, 1], rc[:, :, CHUNK - 1], mref[:, 1], ALU.subtract))
                step(V.tensor_tensor(fsm[:, 2], mref[:, 1], mref[:, 0], ALU.subtract))
                step(V.tensor_tensor(dd[:, :].rearrange("p (c n) -> p c n", n=CHUNK), rc,
                                     mref[:, 0].unsqueeze(2).to_broadcast([P, NC, CHUNK]), ALU.subtract))
                V.tensor_tensor(dm[:, :].rearrange("p (c n) -> p c n", n=CHUNK),
                                mref[:, 1].unsqueeze(2).to_broadcast([P, NC, CHUNK]), rc, ALU.subtract)\
                    .then_inc(s["okd"], 1)

            def turned(step, i):
                dve.wait_ge(s["sincos"], i * 2 + 2)
                dve.wait_ge(s["expd"], i * 4 + 4)
                for at_, e_, t_ in ((3 * NC, ep, cs), (3 * NC + SEG, ep, sn), (BLK, em, cs), (BLK + SEG, em, sn)):
                    ins = V.tensor_tensor(ec[:, at_:at_ + SEG], e_, t_, ALU.mult)
                    if at_ < BLK + SEG:
                        step(ins)
                    else:
                        ins.then_inc(s["ecs"], 1)

            def scaled_x(i):
                for q in range(2):
                    dve.wait_ge(s["x_tr"], i * 2 + q + 1)
                    for par in range(2):
                        rows = slice(par * CHUNK, (par + 1) * CHUNK)
                        for h in range(2):
                            V.tensor_tensor(
                                xd[h * CHUNK:(h + 1) * CHUNK, q].rearrange("p (c two) n -> p c two n", two=2)[:, :, par, :],
                                bank[(3, 0)[q]][rows, :].rearrange("p (c h n) -> p c h n", c=TILES, h=2)[:, :, h, :],
                                dtx[rows].rearrange("p (c h) k -> p c h k", h=HEADS)[:, :, 2 * q + h, 0:1]
                                .to_broadcast([CHUNK, TILES, HD]),
                                ALU.mult).then_inc(s["xds"], 1)

            def general_path(step, i):
                general.read_flag(i)
                with general.taken():
                    n = general.before()
                    once = Steps(dve, s["gen_steps"], n, 15)
                    once(V.tensor_tensor(gen_src[:, 0], gen_src[:, 0], keep[:], ALU.mult))
                    V.tensor_copy(gen_src[:, 1], gen_src[:, 1]).then_inc(s["gen_src_in"], 1)
                    for q in range(2):
                        decay, cosine, sine, keys = (gen_st[:, a] for a in range(4))
                        dve.wait_ge(s["gen_dma"], n * 512 + q * 256 + 256)
                        once(V.tensor_scalar(gen_w, cosine, re_row[:, 0:1], None, ALU.mult))
                        once(V.scalar_tensor_tensor(gen_w, sine, im_row[:, 0:1], gen_w, ALU.mult, ALU.add))
                        once(V.tensor_tensor(keys, keys, gen_w, ALU.mult))
                        once(V.tensor_tensor(tmp[:], cbq[:, 0], cosine, ALU.mult))
                        once(V.tensor_tensor(gen_w, cbq[:, 1], sine, ALU.mult))
                        once(V.tensor_tensor(tmp[:], tmp[:], gen_w, ALU.add))
                        once(V.memset(gen_y[:, q], 0.0))
                        apart(dve)
                        with dve.Fori(0, HD) as p:
                            at_p = n * (2 * HD) + q * HD + p
                            loop = Steps(dve, s["gen_loop"], at_p, 3)
                            V.tensor_copy(sel[:, 0].rearrange("p (h k) -> p h k", h=2),
                                          ident[:].rearrange("p (h w) -> p h w", h=2)[:, :, bass.ds(p, 1)]
                                          .to_broadcast([P, 2, 2 * NK])).then_inc(s["gen_sel"], 1)
                            V.tensor_copy(sel[:, 1], pick[:, bass.ds(p * -1 + HD, P)]).then_inc(s["gen_sel"], 1)
                            dve.wait_ge(s["gen_x_ps"], at_p + 1)
                            loop(V.tensor_tensor(gen_p, bank[1][:], keys, ALU.mult))
                            loop(V.tensor_tensor_scan(gen_w, decay, gen_p, 0.0, ALU.mult, ALU.add))
                            V.tensor_tensor(gen_p, gen_w, tmp[:], ALU.mult).then_inc(s["gen_prod"], 1)
                            dve.wait_ge(s["gen_y_ps"], at_p + 1)
                            loop(V.tensor_tensor(gen_y[:, q], gen_y[:, q], bank[2][:], ALU.add))
                            apart(dve)
                        V.tensor_copy(okf[:, 0:1], okf[:, 0:1]).then_inc(s["gen_done"], 1)
                        dve.wait_ge(s["gen_done"], n * 2 + q + 1)
                        apart(dve)
                    once.done()

            def queries_keys(step, i):
                b_re = cbr[:, 0].rearrange("p (c n) -> p c n", n=CHUNK)[:, :, CHUNK - 1]
                b_im = cbr[:, 1].rearrange("p (c n) -> p c n", n=CHUNK)[:, :, CHUNK - 1]
                step(V.tensor_scalar(bend[:], b_re, im_sign[:, 0:1], None, ALU.mult))

                def chunked(a):
                    return a.rearrange("p (c n) -> p c n", n=CHUNK)

                for q in range(2):
                    cosp, sinp = (st[:, q, 3 * NC + n * SEG:3 * NC + (n + 1) * SEG] for n in range(2))
                    keys_, others = (st[:, q, BLK + n * SEG:BLK + (n + 1) * SEG] for n in range(2))
                    step(V.tensor_tensor(chunked(k2[:, q]), chunked(keys_),
                                         bend[:].unsqueeze(2).to_broadcast([P, NC, CHUNK]), ALU.mult))
                    step(V.tensor_tensor(chunked(tmp[:]), chunked(others),
                                         b_im.unsqueeze(2).to_broadcast([P, NC, CHUNK]), ALU.mult))
                    V.tensor_tensor(k2[:, q], k2[:, q], tmp[:], ALU.add).then_inc(s["k2r"], 1)
                    dve.wait_ge(s["k2r"], i * 2 + q + 1)
                    step(V.tensor_tensor(c1[:, q], cbq[:, 0], cosp, ALU.mult))
                    step(V.tensor_tensor(tmp[:], cbq[:, 1], sinp, ALU.mult))
                    V.tensor_tensor(c1[:, q], c1[:, q], tmp[:], ALU.add).then_inc(s["q1"], 1)
                    dve.wait_ge(s["q1"], i * 2 + q + 1)
                    step(V.scalar_tensor_tensor(c2[:, q], cbr[:, 2], im_sign[:, 0:1], cosp, ALU.mult, ALU.mult))
                    step(V.tensor_tensor(tmp[:], cbr[:, 3], sinp, ALU.mult))
                    V.tensor_tensor(c2[:, q], c2[:, q], tmp[:], ALU.subtract).then_inc(s["q2"], 1)
                    if q == 0:
                        dve.wait_ge(s["q2"], i * 2 + 1)
                for q in range(2):
                    step(V.tensor_scalar(state[:, q], state[:, q], flags[:, bass.ds(i, 1)], None, ALU.mult))

            def chunks(step, i):
                for q in range(2):
                    dve.wait_ge(s["g_ps"], i * 2 + q + 1)
                    V.tensor_tensor(gs[:, q], bank[(3, 0)[q]][:].rearrange("p (c n) -> p c n", n=CHUNK),
                                    causal_ok[:, :].unsqueeze(1).to_broadcast([P, NC, CHUNK]), ALU.mult)\
                        .then_inc(s["gsm"], 1)
                for q in range(2):
                    emid, gend, rho = (st[:, q, n * NC:(n + 1) * NC] for n in range(3))
                    step(V.tensor_tensor(fdec[:, q, 0, 0:NC - 1], gend[:, 0:NC - 1], emid[:, 1:NC], ALU.mult))
                    step(V.tensor_tensor(fdec[:, q, 1, 0:NC - 1], fdec[:, q, 0, 0:NC - 1], rho[:, 1:NC], ALU.mult))
                    step(V.tensor_scalar(ss[:, q, 0], state[:, q], emid[:, 0:1], None, ALU.mult))
                dve.wait_ge(s["u_ps"], i * 2 + 2)
                uq = [bank[1], bank[2]]
                for c in range(NC):
                    for q in range(2):
                        u = uq[q][:, c * HD:(c + 1) * HD]
                        if c == 0:
                            rho0 = st[:, q, 2 * NC:2 * NC + 1]
                            ins = V.scalar_tensor_tensor(vv[:, q, 0], ss[:, q, 0], rho0, u, ALU.mult, ALU.add)
                        else:
                            ins = V.scalar_tensor_tensor(vv[:, q, c], vv[:, q, c - 1], fdec[:, q, 1, c - 1:c], u,
                                                         ALU.mult, ALU.add)
                        step(ins)
                for q in range(2):
                    V.tensor_tensor(ss[:, q, 1:NC], vv[:, q, 0:NC - 1],
                                    fdec[:, q, 0, 0:NC - 1].unsqueeze(2).to_broadcast([P, NC - 1, HD]), ALU.mult)\
                        .then_inc(s["states"], 1)
                    step(V.tensor_scalar(state[:, q], vv[:, q, NC - 1], st[:, q, 2 * NC - 1:2 * NC],
                                         None, ALU.mult))

            def gated(step, i):
                dve.wait_ge(s["zsilu"], i * 2 + 2)
                for q in range(2):
                    dve.wait_ge(s["y_ps"], i * 2 + q + 1)
                    apart(dve)
                    with general.taken():
                        n = general.before()
                        V.tensor_tensor(bank[(3, 0)[q]][:], bank[(3, 0)[q]][:], gen_y[:, q], ALU.add)\
                            .then_inc(s["gen_add"], 1)
                        dve.wait_ge(s["gen_add"], n * 2 + q + 1)
                        apart(dve)
                        if q == 1:
                            general.count()
                    step(V.scalar_tensor_tensor(tmp[:], cv[:, q], dsk[:, q:q + 1], bank[(3, 0)[q]][:], ALU.mult, ALU.add))
                    V.tensor_tensor(gg[:, q], tmp[:], zs[:, q], ALU.mult).then_inc(s["gated"], 1)
                    if q == 0:
                        dve.wait_ge(s["gated"], i * 2 + 1)

            def residual(i):
                dve.wait_ge(s["o_ps"], i + 1)
                V.tensor_scalar(mv[:, :, 0], bank[1][:, 0:TILES], 1.0 / DI, EPS, ALU.mult, ALU.add)\
                    .then_inc(s["rmsin"], 1)
                dve.wait_ge(s["rms"], i + 1)
                for c in range(TILES):
                    V.scalar_tensor_tensor(x1[:, c], bank[2][:, c * DM:(c + 1) * DM], rstd[:, c:c + 1], xin[:, c],
                                           ALU.mult, ALU.add).then_inc(s["x1r"], 1)

            def second_norm(step, i):
                dve.wait_ge(s["x1r"], i * TILES + TILES)
                layernorm_stats(step, x1, "var2", i)
                dve.wait_ge(s["rstd2"], i + 1)
                for c in range(TILES):
                    V.tensor_scalar(xn[:, c], x1[:, c], mv[:, c, 0:1], rstd[:, c:c + 1], ALU.subtract, ALU.mult)\
                        .then_inc(s["xn2"], 1)

            def hidden(j, g):
                dve.wait_ge(s["h_ps"], j * NU + 2 * g + 2)
                if g >= 2:
                    dve.wait_ge(s["h_in"], j * 2 * NG + 2 * (g - 1))
                V.scalar_tensor_tensor(hpre[:, g % 2],
                                       bank[6 + g % 2][0:F1, :].rearrange("p (n f) -> p n f", f=F2),
                                       scale_u[:, 0:1], bias_u[:, :].unsqueeze(1).to_broadcast([F1, GRP, F2]),
                                       ALU.mult, ALU.add).then_inc(s["hpre_in"], 1)

            def down_router(j):
                step = Steps(dve, s["fv"], j, 6)
                dve.wait_ge(s["lgd_ps"], j + 1)
                top2(step, j, 1, bank[6][0:TOK, 0:E], bank[7])
                step.done()

            def results(j, groups):
                for g in groups:
                    if g == 0:
                        dve.wait_ge(s["xrb"], j + 1)
                        apart(dve)
                    dve.wait_ge(s["y2_ps"], j * NG + g + 1)
                    xr = xir[0:D1, g * GRP:(g + 1) * GRP]
                    V.scalar_tensor_tensor(xr, bank[6 + g % 2][0:D1, 0:GRP * D2].rearrange("p (n j) -> p n j", j=D2),
                                           scale_d[:, 0:1], xr, ALU.mult, ALU.add).then_inc(s["out_sb"], 1)

            def one_pass(i, ssm_part, ffn_part):
                j = i - 1
                step = Steps(dve, s["dv"], i, DVE_STEPS)
                if ssm_part:
                    first_norm(step, i, not ffn_part)
                    softplus(step, i)
                    conv(step, i, 0)
                if ffn_part:
                    hidden(j, 0)
                if ssm_part:
                    conv(step, i, 1)
                if ffn_part:
                    hidden(j, 1)
                if ssm_part:
                    conv(step, i, 2)
                    decays(step, i)
                if ffn_part:
                    hidden(j, 2)
                if ssm_part:
                    phases(step, i)
                if ffn_part:
                    hidden(j, 3)
                if ssm_part:
                    exponents(step, i)
                if ffn_part:
                    hidden(j, 4)
                if ssm_part:
                    turned(step, i)
                if ffn_part:
                    hidden(j, 5)
                if ssm_part:
                    scaled_x(i)
                if ffn_part:
                    hidden(j, 6)
                    hidden(j, 7)
                    down_router(j)
                if ssm_part:
                    dve.wait_ge(s["rep_bc"], i * 256 + 256)
                    dve.wait_ge(s["cbq"], i + 1)
                    apart(dve)
                    dve.wait_ge(s["stacked"], i * 128 + 128)
                    apart(dve)
                    general_path(step, i)
                    queries_keys(step, i)
                if ffn_part:
                    results(j, (0,))
                if ssm_part:
                    chunks(step, i)
                if ffn_part:
                    results(j, (1, 2))
                if ssm_part:
                    gated(step, i)
                if ffn_part:
                    results(j, (3, 4))
                if ssm_part:
                    residual(i)
                    second_norm(step, i)
                if ffn_part:
                    results(j, (5, 6, 7))
                if ssm_part:
                    dve.wait_ge(s["lg_ps"], i + 1)
                    top2(step, i, 0, bank[0][0:TOK, 0:E], bank[1])
                    step.done()

            passes(dve, one_pass)

        @block.tensor
        def _(pe):
            T = nc.tensor
            NG = TOK // GRP

            def mm(o, l, r, start=True, stop=True):
                return T.matmul(o, l, r, start=start, stop=stop)

            pe.wait_ge(s["weights"], 16 * 24 + 2)
            pe.wait_ge(s["selfs"], 14)
            general = General(pe, "pe")
            where = [[pe.alloc_register(f"table_{set_}_{n}") for n in range(2 * GRP)] for set_ in range(2)]
            table = tab[:].rearrange("p e f -> p (e f)")
            table_b = tab[:, :, :].rearrange("p e f -> p (e f)")[:, D1:]

            def find(layer, g):
                at_ = g * 2 * GRP
                pe.reg_load(where[g % 2], offs[:, layer].rearrange("p n k -> p (n k)")[:, at_:at_ + 2 * GRP])

            def offset(n, k):
                return pe.snap(where[(n // GRP) % 2][2 * (n % GRP) + k], min_val=0, max_val=(E - 1) * F1)

            def transposes(src, dst):
                for c in range(TILES):
                    ins = T.transpose(dst[:, c * P:(c + 1) * P], src[:, c * P:(c + 1) * P], ident[:])
                return ins

            def rows(ps):
                apart(pe)
                for k in range(2):
                    mm(ps[0:1, 128 + k * TOK:128 + (k + 1) * TOK], pr[:, 6 + k:7 + k], ident[0:TOK, 0:TOK])
                for k in range(2):
                    ins = mm(ps[:, 256 + k * TOK:256 + (k + 1) * TOK],
                             pr[:, 4 + k:5 + k].to_broadcast([TOK, P]), ident[0:TOK, 0:TOK])
                return ins

            def projections(i):
                pe.wait_ge(s["xn1"], i * TILES + TILES)
                transposes(xn[:].rearrange("p c d -> p (c d)"), bank[0]).then_inc(s["xnT_ps"], 1)
                pe.wait_ge(s["xnT"], i + 1)
                mm(bank[1][0:LORA, :], w1[:], xnT[:]).then_inc(s["w1_ps"], 1)
                for c in range(TILES):
                    ins = mm(bank[2][:, c * HEADS:(c + 1) * HEADS], xnT[:, c * P:(c + 1) * P], win[:, C_DT:C_DT + HEADS])
                ins.then_inc(s["dt_ps"], 1)
                mm(bank[3][:], win[:, C_X:C_X + P], xnT[:]).then_inc(s["xbc_ps"], 1)
                mm(bank[0][:], win[:, C_X + P:C_X + 2 * P], xnT[:]).then_inc(s["xbc_ps"], 1)
                pe.wait_ge(s["lora"], i + 1)
                mm(bank[1][:], win[:, C_BC:C_BC + P], xnT[:]).then_inc(s["xbc_ps"], 1)
                for a, b in enumerate((3, 0)):
                    pe.wait_ge(s["xpre_in"], i * 3 + a + 1)
                    mm(bank[b][:], win[:, C_Z + a * P:C_Z + (a + 1) * P], xnT[:]).then_inc(s["z_ps"], 1)

            def theta(i):
                pe.wait_ge(s["xpre_in"], i * 3 + 3)
                mm(bank[1][:], w2[:], lo[0:LORA, :]).then_inc(s["th_ps"], 1)

            def dt_rows(i):
                pe.wait_ge(s["dt_tok"], i + 1)
                transposes(dtx[:].rearrange("p a k -> p (a k)"), bank[2]).then_inc(s["dtr_ps"], 1)

            def x_turned(i):
                for q in range(2):
                    pe.wait_ge(s["zsilu"], i * 2 + q + 1)
                    pe.wait_ge(s["xc"], i * 3 + q + 1)
                    transposes(cv[:, q], bank[(3, 0)[q]]).then_inc(s["x_tr"], 1)

            def all_within(i):
                pe.wait_ge(s["viol_in"], i + 1)
                mm(bank[1][:, 64:65], ones[:], viol[:, 1:2]).then_inc(s["ok_ps"], 1)

            def general_path(i):
                general.read_flag(i)
                with general.taken():
                    n = general.before()
                    for q in range(2):
                        with pe.Fori(0, HD) as p:
                            at_p = n * (2 * HD) + q * HD + p
                            pe.wait_ge(s["gen_sel"], at_p * 2 + 2)
                            mm(bank[1][:], sel[:, 0], cv[:, q]).then_inc(s["gen_x_ps"], 1)
                            pe.wait_ge(s["gen_prod"], at_p + 1)
                            mm(bank[2][:], sel[:, 1], gen_p).then_inc(s["gen_y_ps"], 1)
                    general.count()

            def scores(i):
                for q in range(2):
                    pe.wait_ge(s["k2r"], i * 2 + q + 1)
                    transposes(k2[:, q], bank[1 + q]).then_inc(s["bt_ps"], 1)
                    pe.wait_ge(s["stacked"], i * 128 + 128)
                    pe.wait_ge(s["q1"], i * 2 + q + 1)
                    apart(pe)
                    pe.wait_ge(s["xds"], i * 8 + 4 * q + 4)
                    apart(pe)
                    for c in range(NC):
                        for h in range(2):
                            half = slice(h * CHUNK, (h + 1) * CHUNK)
                            cols = slice(c * CHUNK, (c + 1) * CHUNK)
                            ins = mm(bank[(3, 0)[q]][half, cols],
                                     st[half, q, BLK + c * CHUNK:BLK + (c + 1) * CHUNK], c1[half, q, cols])
                    ins.then_inc(s["g_ps"], 1)

            def updates(i):
                for q in range(2):
                    pe.wait_ge(s["btc"], i * 8 + 4 * q + 4)
                    apart(pe)
                    for c in range(NC):
                        for h in range(2):
                            half = slice(h * CHUNK, (h + 1) * CHUNK)
                            ins = mm(bank[1 + q][half, c * HD:(c + 1) * HD], bt[half, q, c], xd[half, q, c])
                    ins.then_inc(s["u_ps"], 1)

            def outputs(i):
                for q in range(2):
                    pe.wait_ge(s["gsm"], i * 2 + q + 1)
                    pe.wait_ge(s["q2"], i * 2 + q + 1)
                    pe.wait_ge(s["states"], i * 2 + q + 1)
                    apart(pe)
                    for c in range(NC):
                        for h in range(2):
                            half = slice(h * CHUNK, (h + 1) * CHUNK)
                            cols = slice(c * CHUNK, (c + 1) * CHUNK)
                            b = bank[(3, 0)[q]]
                            mm(b[half, cols], xd[half, q, c], gs[half, q, c], True, False)
                            ins = mm(b[half, cols], ss[half, q, c], c2[half, q, cols], False, True)
                    ins.then_inc(s["y_ps"], 1)

            def projected(i):
                pe.wait_ge(s["gsq"], i * 2 + 2)
                for c in range(TILES):
                    rows_ = slice(c * P, (c + 1) * P)
                    for q in range(2):
                        mm(bank[1][:, c:c + 1], gq[:, q, rows_], ones[:, 0:1], q == 0, q == 1)
                for c in range(TILES):
                    rows_ = slice(c * P, (c + 1) * P)
                    for q in range(2):
                        ins = mm(bank[2][:, c * DM:(c + 1) * DM], gg[:, q, rows_], wout[:, q], q == 0, q == 1)
                ins.then_inc(s["o_ps"], 1)

            def second_norm(i):
                pe.wait_ge(s["xn2"], i * TILES + TILES)
                transposes(xn[:].rearrange("p c d -> p (c d)"), bank[3]).then_inc(s["x2T_ps"], 1)

            def up_router(i):
                pe.wait_ge(s["x2T"], i + 1)
                xt = xnT[:].rearrange("p (n r) -> p r n", r=RPT)
                for r in range(RPT):
                    ins = mm(bank[0][0:TOK, 0:E], xt[:, r], wup[:, r], r == 0, r == RPT - 1)
                ins.then_inc(s["lg_ps"], 1)
                pe.wait_ge(s["probs"], i + 1)
                rows(bank[1]).then_inc(s["row_ps"], 1)

            def up_second(j, u):
                g = u // 2
                pe.wait_ge(s["t1_in"], j * NU + u + 1)
                if u % 2 == 0 and g >= 2:
                    pe.wait_ge(s["hpre_in"], j * NG + g - 1)
                for n in range(UNIT):
                    col = ((u % 2) * UNIT + n) * F2
                    for k in range(2):
                        ins = mm(bank[6 + g % 2][0:F1, col:col + F2], t1[:, u % 2, n, k],
                                 table[:, bass.ds(offset(u * UNIT + n, k), F2)], k == 0, k == 1)
                ins.then_inc(s["h_ps"], 1)

            def up(j, units):
                for u in units:
                    if u == 0:
                        pe.wait_ge(s["rows_in"], j * 2 + 2)
                        apart(pe)
                    if u % 2 == 0:
                        find(0, u // 2)
                    pe.wait_ge(s["xp_in"], j * NG + u // 2 + 1)
                    if u >= 2:
                        pe.wait_ge(s["t1_in"], j * NU + u - 1)
                    apart(pe)
                    for n in range(UNIT):
                        for k in range(2):
                            col = (2 * n + k) * F1
                            ins = mm(bank[4 + u % 2][0:D2, col:col + F1], xp[:, (u // 2) % 2, (u % 2) * UNIT + n, k],
                                     table[:, bass.ds(offset(u * UNIT + n, k), F1)])
                    ins.then_inc(s["t1_ps"], 1)
                    if u >= 1:
                        up_second(j, u - 1)
                    if u == NU - 1:
                        up_second(j, u)

            def down_router(j):
                pe.wait_ge(s["h_in"], j * 2 * NG + 2 * NG)
                for f in range(F2 // 2):
                    ins = mm(bank[6][0:TOK, 0:E], hh[:, :, f], wdn[:, f], f == 0, f == F2 // 2 - 1)
                ins.then_inc(s["lgd_ps"], 1)
                pe.wait_ge(s["dprobs"], j + 1)
                rows(bank[7]).then_inc(s["drow_ps"], 1)

            def down_second(j, g):
                pe.wait_ge(s["t2_in"], j * NG + g + 1)
                if g >= 2:
                    pe.wait_ge(s["out_sb"], j * NG + g - 1)
                for n in range(GRP):
                    for k in range(2):
                        ins = mm(bank[6 + g % 2][0:D1, n * D2:(n + 1) * D2], t2[:, g % 2, n, k],
                                 table_b[:, bass.ds(offset(g * GRP + n, k), D2)], k == 0, k == 1)
                ins.then_inc(s["y2_ps"], 1)

            def down(j, groups):
                for g in groups:
                    if g == 0:
                        pe.wait_ge(s["drows_in"], j * 2 + 2)
                        apart(pe)
                    find(1, g)
                    pe.wait_ge(s["hs_in"], j * 2 * NG + 2 * g + 2)
                    if g >= 2:
                        pe.wait_ge(s["t2_in"], j * NG + g - 1)
                    apart(pe)
                    for n in range(GRP):
                        for k in range(2):
                            col = (2 * n + k) * D1
                            ins = mm(bank[4 + g % 2][0:F2, col:col + D1], hs[:, g % 2, n, k],
                                     table[:, bass.ds(offset(g * GRP + n, k), D1)])
                    ins.then_inc(s["t2_ps"], 1)
                    if g >= 1:
                        down_second(j, g - 1)
                    if g == NG - 1:
                        down_second(j, g)

            def one_pass(i, ssm_part, ffn_part):
                j = i - 1
                if ssm_part:
                    projections(i)
                if ffn_part:
                    up(j, (0, 1))
                if ssm_part:
                    theta(i)
                if ffn_part:
                    up(j, (2, 3))
                if ssm_part:
                    dt_rows(i)
                if ffn_part:
                    up(j, (4, 5, 6, 7))
                if ssm_part:
                    x_turned(i)
                if ffn_part:
                    up(j, (8, 9))
                if ssm_part:
                    all_within(i)
                if ffn_part:
                    up(j, range(10, NU))
                    down_router(j)
                if ssm_part:
                    general_path(i)
                if ffn_part:
                    down(j, (0, 1))
                if ssm_part:
                    scores(i)
                if ffn_part:
                    down(j, (2, 3))
                if ssm_part:
                    updates(i)
                if ffn_part:
                    down(j, (4,))
                if ssm_part:
                    outputs(i)
                if ffn_part:
                    down(j, (5,))
                if ssm_part:
                    projected(i)
                if ffn_part:
                    down(j, (6,))
                if ssm_part:
                    second_norm(i)
                if ffn_part:
                    down(j, (7,))
                if ssm_part:
                    up_router(i)

            passes(pe, one_pass)


DVE_STEPS = 115


_ORDER = ["L0_attn_x", "w_in", "conv_w", "conv_b", "dt_bias", "lam_base", "th_base", "th_w1", "th_w2", "eta", "d_skip",
          "norm_w", "w_out", "w_up", "a_up", "b_up", "scale_up", "bias_up", "w_down", "a_down", "b_down",
          "scale_down", "bias_down", "seg_flags"]


def laid_out(i):
    g = {k: np.asarray(v) for k, v in i.items()}
    xf = g["L0_attn_x"].reshape(BATCH * LENGTH, DM)
    wi = g["L0_attn_in_proj_w"]
    bc = np.concatenate([np.arange(0, 2 * NK, 2), np.arange(1, 2 * NK, 2)])
    bc = np.concatenate([bc, 2 * NK + bc])
    rows = np.concatenate([np.arange(2 * DI), 2 * DI + bc, np.arange(2 * DI + 4 * NK, NW)])
    chans = np.concatenate([np.arange(DI), DI + bc])
    def col(a, n=P):
        return np.repeat(a.reshape(1, -1), n, 0)
    first = np.ones(NSEG, np.float32)
    first[::LENGTH // SEG] = 0.0
    return {
        "L0_attn_x": np.concatenate([xf, xf[:SEG]], 0),
        "w_in": wi[rows].T,
        "conv_w": g["L0_attn_conv_w"][chans].reshape(3, P, TAPS).transpose(1, 0, 2),
        "conv_b": g["L0_attn_conv_b"][chans].reshape(3, P).T,
        "dt_bias": col(g["L0_attn_dt_bias"]),
        "lam_base": g["L0_attn_lambda_base"].reshape(P, 1),
        "th_base": g["L0_attn_theta_base"].reshape(P, 1),
        "th_w1": g["L0_attn_theta_w1"],
        "th_w2": g["L0_attn_theta_w2"],
        "eta": g["L0_attn_viscosity_eta"].reshape(P, 1),
        "d_skip": np.repeat(g["L0_attn_D"], HD).reshape(2, P).T,
        "norm_w": g["L0_attn_norm_w"].reshape(2, P).T,
        "w_out": g["L0_attn_out_proj_w"].T.reshape(2, P, DM).transpose(1, 0, 2),
        "w_up": g["L0_ffn_W_up"].T.reshape(RPT, P, E).transpose(1, 0, 2),
        "a_up": g["L0_ffn_A_up"].transpose(2, 0, 1),
        "b_up": g["L0_ffn_B_up"].transpose(2, 0, 1),
        "scale_up": col(g["L0_ffn_scale_up"], F1),
        "bias_up": g["L0_ffn_bias_up"].reshape(F1, F2),
        "w_down": g["L0_ffn_W_down"].reshape(E, F1, F2).transpose(1, 2, 0),
        "a_down": g["L0_ffn_A_down"].transpose(2, 0, 1),
        "b_down": g["L0_ffn_B_down"].transpose(2, 0, 1),
        "scale_down": col(g["L0_ffn_scale_down"], D1),
        "bias_down": g["L0_ffn_bias_down"].reshape(D1, D2),
        "seg_flags": col(first),
    }


def kernel(**inputs):
    import concourse.bacc as _bacc
    from concourse.bass_utils import run_bass_kernel_spmd as _run

    nc = _bacc.Bacc("TRN2", target_bir_lowering=False, num_devices=1)
    arrays, args = {}, []
    laid = laid_out(inputs)
    for name in _ORDER:
        a = np.ascontiguousarray(laid[name])
        arrays[f"in_{name}"] = a
        args.append(nc.dram_tensor(f"in_{name}", a.shape, mybir.dt.from_np(a.dtype), kind="ExternalInput").ap())
    args.append(nc.dram_tensor("out_0", (BATCH * LENGTH, DM), FP32, kind="ExternalOutput").ap())
    for name in ("x1_scratch", "x2_scratch"):
        args.append(nc.dram_tensor(name, (BATCH * LENGTH, DM), FP32, kind="Internal").ap())
    block_kernel(nc, *args)
    r = _run(nc, [arrays], core_ids=[0])
    return r.results[0]["out_0"].reshape(BATCH, LENGTH, DM)
```

```python
import math
from contextlib import ExitStack

import numpy as np

import concourse.bass as bass
from concourse import mybir

FP32 = mybir.dt.float32
I32 = mybir.dt.int32
U32 = mybir.dt.uint32
ALU = mybir.AluOpType
ACT = mybir.ActivationFunctionType
AX = mybir.AxisListType

P = 128
BATCH, LENGTH, DM = 4, 1024, 128
DI = 256
HEADS, HD = 4, 64
NK = 32
LORA = 48
TAPS = 4
CHUNK = 64
SEG = 512
NSEG = BATCH * LENGTH // SEG
TILES = SEG // P
NC = SEG // CHUNK
MID = CHUNK // 2 - 1
LIMIT = 30.0
EPS = 1e-5
TWO_PI_HI = 6.28125
TWO_PI_LO = 2 * math.pi - 6.28125
ROUND = 12582912.0
PI_SAFE = 3.1415925

E = 64
D1 = D2 = 32
F1 = F2 = 64
TOK = SEG * DM // (D1 * D2)
RPT = D1 * D2 // DM
GRP = 8
UNIT = GRP // 2
NG = TOK // GRP
NU = TOK // UNIT

NW = 2 * DI + 2 * 2 * NK + HEADS
C_Z, C_X, C_BC, C_DT = 0, DI, 2 * DI, 2 * DI + 4 * NK

EARLY_WIDTHS = (NW, LORA, 3 * TAPS, 3, HEADS, 1, 1, 1, 2, 2, NSEG, 1, 1)
EARLY_PARTS = tuple((sum(EARLY_WIDTHS[:n]), w) for n, w in enumerate(EARLY_WIDTHS))
EARLY = sum(EARLY_WIDTHS)


def block_kernel(nc, x, first_weights, th_w2, w_out, w_up, a_up, b_up, bias_up, w_down, a_down, b_down,
                 bias_down, out, x1_scratch, x2_scratch):
    ctx = ExitStack()
    with ctx:
        def sb(name, shape, dt=FP32):
            return ctx.enter_context(nc.sbuf_tensor(name, shape, dt))

        def sem(name):
            return ctx.enter_context(nc.semaphore(name))

        ident = sb("ident", [P, P])
        ones = sb("ones", [P, P])
        causal = sb("causal", [P, P])
        keep = sb("keep", [P, SEG])
        im_sign = sb("im_sign", [P, 1])
        neg_sign = sb("neg_sign", [P, 1])
        re_row = sb("re_row", [P, 1])
        im_row = sb("im_row", [P, 1])
        minus_half = sb("minus_half", [P, TILES])
        half_pi = sb("half_pi", [P, 1])
        pick = sb("pick", [P, 2 * P])
        early = sb("early", [P, EARLY])
        (win, w1, cw, cb, dtb, lamb, thb, etas, dsk, nw, flags, scale_u, scale_d) = (
            early[:, at_:at_ + width] for at_, width in EARLY_PARTS)
        cw = cw.rearrange("p (a k) -> p a k", k=TAPS)
        w2 = sb("w2", [LORA, P])
        wout = sb("wout", [P, 2, DM])
        wup = sb("wup", [P, RPT, E])
        tab = sb("tab", [P, E, F1])
        wdn = sb("wdn", [P, F2 // 2, E])
        bias_u = sb("bias_u", [F1, F2])
        bias_d = sb("bias_d", [D1, D2])

        xin = sb("xin", [P, TILES, DM])
        x1 = sb("x1", [P, TILES, DM])
        xn = sb("xn", [P, TILES, DM])
        xnT = sb("xnT", [P, SEG])
        xpre = sb("xpre", [P, 3, TAPS - 1 + SEG])
        cv = sb("cv", [P, 3, SEG])
        zs = sb("zs", [P, 2, SEG])
        tmp = sb("tmp", [P, SEG])
        tmp_p = sb("tmp_p", [P, SEG])
        dtx = sb("dtx", [P, TILES * HEADS, NK])
        stats = sb("stats", [P, TILES, 6])
        mv = sb("mv", [P, TILES, 2])
        rstd = sb("rstd", [P, TILES])
        dts = sb("dts", [P, 8, TILES * HEADS])
        phi = sb("phi", [P, NC + 1])
        ksm = sb("ksm", [P, 2, NC])
        fsm = sb("fsm", [P, 3, NC])
        mref = sb("mref", [P, 2, NC])
        bend = sb("bend", [P, NC])
        causal_ok = sb("causal_ok", [P, P])
        state = sb("state", [P, 2, HD])
        fdec = sb("fdec", [P, 2, 2, NC])
        viol = sb("viol", [P, 2])
        okf = sb("okf", [P, 2])
        oki = sb("oki", [1, 1], I32)
        lg = sb("lg", [TOK, E])
        top = sb("top", [TOK, 8])
        topi = sb("topi", [TOK, 8], U32)
        pr = sb("pr", [TOK, 8])
        offs = sb("offs", [1, 2, TOK, 2], I32)
        pb = sb("pb", [P, 2, TOK, 2])
        sel = sb("sel", [P, 2, P])

        xir = sb("xir", [2 * D1, TOK, D2])
        xp = sb("xp", [P, 2, GRP, 2, D2])
        t1 = sb("t1", [P, 2, UNIT, 2, F1])
        hpre = sb("hpre", [F1, 4, GRP, F2])
        hh = sb("hh", [P, TOK, F2 // 2])
        hs = sb("hs", [P, 2, GRP, 2, F2])
        t2 = sb("t2", [P, 2, GRP, 2, D1])

        arena = sb("arena", [P, 34 * SEG + 12 * NC])
        at = [0]

        def carve(words):
            at[0] += words
            return arena[:, at[0] - words:at[0]]

        BLK = 3 * NC + 2 * SEG
        st = carve(4 * BLK).rearrange("p (a n) -> p a n", a=2)
        cbr = carve(4 * SEG).rearrange("p (a n) -> p a n", a=4)
        k2 = carve(2 * SEG).rearrange("p (a n) -> p a n", a=2)
        c1 = carve(2 * SEG).rearrange("p (a n) -> p a n", a=2)
        c2 = carve(2 * SEG).rearrange("p (a n) -> p a n", a=2)
        cbq = carve(2 * SEG).rearrange("p (a n) -> p a n", a=2)
        late = at[0]
        lo = carve(SEG)
        th = carve(SEG)
        nl = carve(SEG)
        om = carve(SEG)
        rr = carve(SEG)
        ang = carve(SEG)
        dd = carve(SEG)
        dm = carve(SEG)
        ep = carve(SEG)
        em = carve(SEG)
        sn = carve(SEG)
        cs = carve(SEG)
        kk = carve(SEG)
        at[0] = late
        xd = carve(2 * SEG).rearrange("p (a c n) -> p a c n", a=2, c=TILES)
        bt = carve(2 * SEG).rearrange("p (a c n) -> p a c n", a=2, c=TILES)
        gs = carve(4 * SEG).rearrange("p (a h c n) -> p a h c n", a=2, h=2, n=P)
        vv = carve(2 * SEG).rearrange("p (a c n) -> p a c n", a=2, n=HD)
        gg = carve(2 * SEG).rearrange("p (a n) -> p a n", a=2)
        gq = carve(2 * SEG).rearrange("p (a n) -> p a n", a=2)
        at[0] = late + 4 * SEG
        gen_st = carve(4 * SEG).rearrange("p (a n) -> p a n", a=4)
        gen_w = carve(SEG)
        gen_p = carve(SEG)
        at[0] = late + 12 * SEG
        gen_y = carve(2 * SEG).rearrange("p (a n) -> p a n", a=2)
        ss = sb("ss", [P, 2, NC, 2 * HD])
        ec = sb("ec", [P, 2 * (BLK + SEG)])
        gen_src = sb("gen_src", [P, 2, SEG])

        bank = [ctx.enter_context(nc.psum_tensor(f"bank{n}", [P, 512], FP32)) for n in range(8)]

        names = ("early weights tables scaled zeros consts selfs x_in var1 rstd1 xn1 xnT_ps xnT "
                 "w1_ps dt_ps xbc_ps z_ps tails lora th_ps softneg softexp soft1p softln dt_tok "
                 "dtr_ps xpre_in conv xc zsilu x_tr rep_bc dtheta thsq viol_in ok_ps okd angle "
                 "sincos expd ecs stacked cbq q1 q2 k2r bt_ps g_ps btc xds u_ps gsm states y_ps "
                 "gated gsq o_ps rmsin rms x1r var2 rstd2 xn2 x2T_ps x2T lg_ps diff pexp probs "
                 "row_ps rows_in scr xi_in xr_in xp_in xrb t1_ps t1_in h_ps hpre_in h_in lgd_ps "
                 "drow_ps dpexp ddiff dprobs drows_in hs_in t2_ps t2_in y2_ps out_sb stored dv fv "
                 "plc plk dt_in cos_again flag gen_src_in gen_dma gen_sel gen_x_ps gen_prod gen_y_ps "
                 "gen_done gen_steps gen_loop gen_add passed").split()
        s = {n: sem("s_" + n) for n in names}
        block = ctx.enter_context(nc.Block())

        class Steps:

            def __init__(self, eng, sem_, i, per):
                self.eng, self.sem, self.i, self.per, self.n = eng, sem_, i, per, 0

            def __call__(self, ins):
                ins.then_inc(self.sem, 1)
                self.n += 1
                self.eng.wait_ge(self.sem, self.i * self.per + self.n)

            def done(self):
                assert self.n == self.per, (self.n, self.per)

        def apart(eng):
            eng.sem_inc(s["passed"], 1)

        class General:

            def __init__(self, eng, name):
                self.eng = eng
                self.runs = eng.alloc_register(f"{name}_general_runs")
                self.flag = eng.alloc_register(f"{name}_factored")
                eng.reg_mov(self.runs, 0)

            def read_flag(self, i):
                self.eng.wait_ge(s["flag"], i + 1)
                apart(self.eng)
                self.eng.reg_load(self.flag, oki[0:1, 0:1])

            def taken(self):
                return self.eng.If_eq(self.flag, 0)

            def before(self):
                return self.eng.snap(self.runs, min_val=0, max_val=NSEG)

            def count(self):
                self.eng.reg_add(self.runs, self.runs, 1)

        ORDER = (2, 0, 1)
        PAIRS = ((0, 0), (0, 1), (1, 0), (1, 1))

        def update(q, c):
            at_ = (q * TILES + c // 2) * HD
            return bank[(3, 0)[c % 2]][:, at_:at_ + HD]

        def passes(eng, one_pass):
            one_pass(0, True, False)
            with eng.Fori(1, NSEG) as i:
                one_pass(i, True, True)
            one_pass(NSEG, False, True)

        @block.sync
        def _(sp):
            sp.dma_start(xin[:], x[0:SEG, :].rearrange("(c p) d -> p c d", p=P)).then_inc(s["x_in"], 16)
            sp.dma_start(early[:], first_weights).then_inc(s["early"], 16)
            for dst, src in ((w2, th_w2), (wout, w_out), (wup, w_up), (bias_u, bias_up), (bias_d, bias_down)):
                sp.dma_start(dst[:], src).then_inc(s["weights"], 16)
            sp.dma_start(tab[0:D1], a_up).then_inc(s["tables"], 16)
            sp.dma_start(tab[D1:2 * D1], b_up).then_inc(s["tables"], 16)
            sp.dma_start(tab[F1:2 * F1, :, 0:D1], a_down).then_inc(s["tables"], 16)
            sp.dma_start(tab[F1:2 * F1, :, D1:2 * D1], b_down).then_inc(s["tables"], 16)
            sp.dma_start(wdn[0:F1], w_down[:, 0:F2 // 2]).then_inc(s["tables"], 16)
            sp.dma_start(wdn[F1:2 * F1], w_down[:, F2 // 2:]).then_inc(s["tables"], 16)
            general = General(sp, "sp")

            def ssm(i):
                sp.wait_ge(s["xc"], i * 3 + 1)
                for h in range(2):
                    for a, (first, second) in enumerate(((0, 0), (NK, NK), (2 * NK, 3 * NK), (3 * NK, 2 * NK))):
                        for r, src in ((0, first), (NK, second)):
                            to = h * 2 * NK + r
                            sp.dma_start(cbr[to:to + NK, a, :], cv[src:src + NK, 2, :]).then_inc(s["rep_bc"], 16)
                sp.wait_ge(s["ecs"], i + 1)
                sp.wait_ge(s["cos_again"], i + 1)
                for q, h in PAIRS:
                    src, to = (2 * q + h) * NK, h * 2 * NK
                    sp.dma_start(st[to:to + NK, q], ec[src:src + NK, 0:2 * BLK]).then_inc(s["stacked"], 16)
                    sp.dma_start(st[to + NK:to + 2 * NK, q].rearrange("p (b n) -> p b n", b=2),
                                 ec[src:src + NK, :].rearrange("p (b n) -> p b n", b=2)[:, :, 0:BLK])\
                        .then_inc(s["stacked"], 16)
                general.read_flag(i)
                with general.taken():
                    n = general.before()
                    sp.wait_ge(s["gen_src_in"], n + 1)
                    for q in range(2):
                        if q == 1:
                            sp.wait_ge(s["gen_done"], n * 2 + 1)
                        for h in range(2):
                            for r in range(2):
                                src, to = (2 * q + h) * NK, h * 2 * NK + r * NK
                                for a, array in enumerate((gen_src[:, 0], cs, sn, gen_src[:, 1])):
                                    sp.dma_start(gen_st[to:to + NK, a], array[src:src + NK, :])\
                                        .then_inc(s["gen_dma"], 16)
                    general.count()
                here = i * SEG
                sp.wait_ge(s["x1r"], i * TILES + TILES)
                sp.dma_start(x1_scratch[bass.ds(here, SEG), :].rearrange("(c p) d -> p c d", p=P), x1[:])\
                    .then_inc(s["scr"], 16)
                sp.dma_start(xin[:], x[bass.ds(here + SEG, SEG), :].rearrange("(c p) d -> p c d", p=P))\
                    .then_inc(s["x_in"], 16)
                sp.wait_ge(s["xn2"], i * TILES + TILES)
                sp.dma_start(x2_scratch[bass.ds(here, SEG), :].rearrange("(c p) d -> p c d", p=P), xn[:])\
                    .then_inc(s["scr"], 16)

            def result(j):
                sp.wait_ge(s["out_sb"], j * NG + NG)
                sp.dma_start(out[bass.ds(j * SEG, SEG), :].rearrange("(n r) (q j) -> (r q) n j", r=RPT, j=D2),
                             xir[0:D1]).then_inc(s["stored"], 16)
                sp.wait_ge(s["stored"], j * 16 + 16)

            def tokens(i, first):
                sp.wait_ge(s["scr"], i * 32 + 32)
                if not first:
                    apart(sp)
                    sp.wait_ge(s["xp_in"], i * NG)
                    apart(sp)
                sp.dma_start(xir[D1:2 * D1], x2_scratch[bass.ds(i * SEG, SEG), :]
                             .rearrange("(n r) (q j) -> (r q) n j", r=RPT, j=D2)).then_inc(s["xi_in"], 16)

            def residual(i):
                sp.dma_start(xir[0:D1], x1_scratch[bass.ds(i * SEG, SEG), :]
                             .rearrange("(n r) (q j) -> (r q) n j", r=RPT, j=D2)).then_inc(s["xr_in"], 16)

            def one_pass(i, ssm_part, ffn_part):
                if ssm_part:
                    ssm(i)
                    tokens(i, not ffn_part)
                if ffn_part:
                    result(i - 1)
                if ssm_part:
                    residual(i)

            passes(sp, one_pass)
            sp.wait_ge(s["stored"], 16 * NSEG)
            sp.wait_ge(s["x_in"], 16 * (NSEG + 1))
            sp.wait_ge(s["scr"], 32 * NSEG)

        @block.gpsimd
        def _(pool):
            nc.gpsimd.memset(ident[:], 0.0).then_inc(s["consts"], 1)
            nc.gpsimd.memset(causal[:], 0.0).then_inc(s["consts"], 1)
            nc.gpsimd.memset(ones[:], 1.0).then_inc(s["consts"], 1)
            nc.gpsimd.memset(pick[:], 0.0).then_inc(s["consts"], 1)
            nc.gpsimd.memset(keep[:], 1.0).then_inc(s["consts"], 1)
            nc.gpsimd.memset(im_sign[:], 1.0).then_inc(s["consts"], 1)
            nc.gpsimd.memset(neg_sign[:], -1.0).then_inc(s["consts"], 1)
            nc.gpsimd.memset(re_row[:], 1.0).then_inc(s["consts"], 1)
            nc.gpsimd.memset(im_row[:], 0.0).then_inc(s["consts"], 1)
            nc.gpsimd.memset(minus_half[:], -0.5).then_inc(s["consts"], 1)
            nc.gpsimd.memset(half_pi[:], math.pi / 2).then_inc(s["consts"], 1)
            pool.wait_ge(s["consts"], 11)

            def shaped(ins):
                made[0] += 1
                ins.then_inc(s["selfs"], 1)
                pool.wait_ge(s["selfs"], made[0])

            made = [0]
            shaped(nc.gpsimd.affine_select(out=ident[:], in_=ident[:], compare_op=ALU.not_equal, fill=1.0, base=0,
                                           pattern=[[-1, P]], channel_multiplier=1))
            for h in range(2):
                half = slice(h * CHUNK, h * CHUNK + CHUNK)
                shaped(nc.gpsimd.memset(causal[half, half], 1.0))
                shaped(nc.gpsimd.affine_select(out=causal[half, half], in_=causal[half, half], compare_op=ALU.is_ge,
                                               fill=0.0, base=0, pattern=[[1, CHUNK]], channel_multiplier=-1))
                for column, value in ((im_sign, -1.0), (neg_sign, 1.0), (re_row, 0.0), (im_row, 1.0)):
                    shaped(nc.gpsimd.memset(column[h * CHUNK + NK:h * CHUNK + 2 * NK], value))
                shaped(nc.gpsimd.memset(pick[half, CHUNK + h * CHUNK:CHUNK + h * CHUNK + 1], 1.0))
            shaped(nc.gpsimd.memset(keep[:].rearrange("p (c n) -> p c n", n=CHUNK)[:, :, 0:1], 0.0))

            G = nc.gpsimd

            def alone(ins, sem_, value):
                ins.then_inc(sem_, 1)
                pool.wait_ge(sem_, value)

            def turned_queries(i):
                step = Steps(pool, s["plc"], i, 6)
                pool.wait_ge(s["rep_bc"], i * 256 + 256)
                apart(pool)
                step(G.tensor_tensor(tmp_p[:], cbr[:, 3], neg_sign[:, 0:1].to_broadcast([P, SEG]), ALU.mult))
                step(G.tensor_tensor(cbq[:, 0], cbr[:, 2], cbr[:, 0], ALU.mult))
                step(G.tensor_tensor(cbq[:, 1], tmp_p[:], cbr[:, 0], ALU.mult))
                step(G.tensor_tensor(tmp_p[:], tmp_p[:], cbr[:, 1], ALU.mult))
                step(G.tensor_tensor(cbq[:, 0], cbq[:, 0], tmp_p[:], ALU.add))
                step(G.tensor_tensor(tmp_p[:], cbr[:, 2], cbr[:, 1], ALU.mult))
                alone(G.tensor_tensor(cbq[:, 1], cbq[:, 1], tmp_p[:], ALU.subtract), s["cbq"], i + 1)
                step.done()

            def second_cos(i):
                pool.wait_ge(s["sincos"], i * 2 + 2)
                pool.wait_ge(s["expd"], i * 4 + 2)
                apart(pool)
                alone(G.tensor_tensor(ec[:, BLK + 2 * SEG:BLK + 3 * SEG], em, cs, ALU.mult), s["cos_again"], i + 1)

            def first_deviation(i):
                pool.wait_ge(s["var1"], i + 1)
                alone(G.tensor_tensor(rstd[:], mv[:, :, 1], minus_half[:], ALU.pow), s["rstd1"], i + 1)

            def theta_squared(i):
                pool.wait_ge(s["dtheta"], i + 1)
                alone(G.tensor_tensor(rr[:, :], th[:, :], th[:, :], ALU.mult), s["thsq"], i + 1)

            def root_mean_square(i):
                pool.wait_ge(s["rmsin"], i + 1)
                alone(G.tensor_tensor(rstd[:], mv[:, :, 0], minus_half[:], ALU.pow), s["rms"], i + 1)

            def second_deviation(i):
                pool.wait_ge(s["var2"], i + 1)
                alone(G.tensor_tensor(rstd[:], mv[:, :, 1], minus_half[:], ALU.pow), s["rstd2"], i + 1)

            def weighted(j, groups):
                for g in groups:
                    if g == 0:
                        pool.wait_ge(s["xi_in"], j * 16 + 16)
                        pool.wait_ge(s["rows_in"], j * 2 + 2)
                        apart(pool)
                    if g >= 2:
                        pool.wait_ge(s["t1_ps"], j * NU + 2 * (g - 1))
                    n = slice(g * GRP, (g + 1) * GRP)
                    alone(G.tensor_tensor(xp[0:D1, g % 2], xir[D1:2 * D1, n].unsqueeze(2).to_broadcast([D1, GRP, 2, D2]),
                                          pb[D1:2 * D1, 0, n].unsqueeze(3).to_broadcast([D1, GRP, 2, D2]), ALU.mult),
                          s["xp_in"], j * NG + g + 1)

            def weighted_hidden(j, groups):
                for g in groups:
                    if g == 0:
                        pool.wait_ge(s["drows_in"], j * 2 + 2)
                        apart(pool)
                    if g >= 2:
                        pool.wait_ge(s["t2_ps"], j * NG + g - 1)
                    n = slice(g * GRP, (g + 1) * GRP)
                    for half in range(2):
                        f = slice(half * (F2 // 2), (half + 1) * (F2 // 2))
                        rows = slice(half * F1, (half + 1) * F1)
                        alone(G.tensor_tensor(hs[F1:2 * F1, g % 2, :, :, f],
                                              hh[rows, n].unsqueeze(2).to_broadcast([F1, GRP, 2, F2 // 2]),
                                              pb[rows, 1, n].unsqueeze(3).to_broadcast([F1, GRP, 2, F2 // 2]),
                                              ALU.mult), s["hs_in"], j * 2 * NG + 2 * g + half + 1)

            def chunked(a):
                return a.rearrange("p (c n) -> p c n", n=CHUNK)

            def end_keys(i, q):
                step = Steps(pool, s["plk"], i * 2 + q, 3)
                pool.wait_ge(s["stacked"], i * 128 + 128)
                apart(pool)
                b_end = (chunked(cbr[:, a])[:, :, CHUNK - 1] for a in range(2))
                b_re, b_im = b_end
                keys_, others = (st[:, q, BLK + n * SEG:BLK + (n + 1) * SEG] for n in range(2))
                step(G.tensor_scalar(bend[:], b_re, im_sign[:, 0:1], None, ALU.mult))
                step(G.tensor_tensor(chunked(k2[:, q]), chunked(keys_),
                                     bend[:].unsqueeze(2).to_broadcast([P, NC, CHUNK]), ALU.mult))
                step(G.tensor_tensor(chunked(tmp_p[:]), chunked(others),
                                     b_im.unsqueeze(2).to_broadcast([P, NC, CHUNK]), ALU.mult))
                alone(G.tensor_tensor(k2[:, q], k2[:, q], tmp_p[:], ALU.add), s["k2r"], i * 2 + q + 1)
                step.done()

            def residual(j):
                pool.wait_ge(s["weights"], 16 * 5)
                pool.wait_ge(s["xr_in"], j * 16 + 16)
                apart(pool)
                alone(G.tensor_tensor(xir[0:D1], xir[0:D1], bias_d[:, :].unsqueeze(1).to_broadcast([D1, TOK, D2]),
                                      ALU.add), s["xrb"], j + 1)

            def one_pass(i, ssm_part, ffn_part):
                j = i - 1
                if ffn_part:
                    weighted(j, (0, 1))
                if ssm_part:
                    first_deviation(i)
                if ffn_part:
                    weighted(j, (2, 3))
                    residual(j)
                if ssm_part:
                    theta_squared(i)
                if ffn_part:
                    weighted(j, (4, 5, 6))
                if ssm_part:
                    turned_queries(i)
                    second_cos(i)
                if ffn_part:
                    weighted(j, (7,))
                if ssm_part:
                    end_keys(i, 0)
                    end_keys(i, 1)
                if ffn_part:
                    weighted_hidden(j, (0, 1, 2, 3, 4, 5, 6, 7))
                if ssm_part:
                    root_mean_square(i)
                    second_deviation(i)

            passes(pool, one_pass)

        @block.scalar
        def _(act):
            act.wait_ge(s["consts"], 11)
            act.wait_ge(s["selfs"], 16)
            A = nc.scalar

            def turned_rows(i):
                act.wait_ge(s["xnT_ps"], i + 1)
                A.activation(xnT[:], bank[0][:], ACT.Copy).then_inc(s["xnT"], 1)

            def lora(i):
                act.wait_ge(s["w1_ps"], i + 1)
                A.activation(lo[0:LORA, :], bank[1][0:LORA, :], ACT.Tanh).then_inc(s["lora"], 1)

            def before_conv(i, a):
                act.wait_ge(s["tails"], i + 1)
                act.wait_ge(s["xbc_ps"], i * 3 + a + 1)
                A.activation(xpre[:, ORDER[a], TAPS - 1:], bank[(3, 0, 1)[a]][:], ACT.Copy).then_inc(s["xpre_in"], 1)

            def gate(i, a):
                act.wait_ge(s["z_ps"], i * 2 + a + 1)
                A.activation(zs[:, a, :], bank[(3, 0)[a]][:], ACT.Silu).then_inc(s["zsilu"], 1)

            def soft_exp(i):
                act.wait_ge(s["softneg"], i + 1)
                A.activation(dts[:, 2, :], dts[:, 1, :], ACT.Exp).then_inc(s["softexp"], 1)

            def soft_ln(i):
                act.wait_ge(s["soft1p"], i + 1)
                A.activation(dts[:, 4, :], dts[:, 3, :], ACT.Ln).then_inc(s["softln"], 1)

            def conv_silu(i, a):
                act.wait_ge(s["conv"], i * 3 + a + 1)
                A.activation(cv[:, ORDER[a], :], cv[:, ORDER[a], :], ACT.Silu).then_inc(s["xc"], 1)

            def step_sizes(i):
                act.wait_ge(s["dtr_ps"], i + 1)
                A.activation(gen_src[:, 1, :], bank[2][:], ACT.Copy).then_inc(s["dt_in"], 1)

            def sines(i):
                act.wait_ge(s["angle"], i * 2 + 2)
                A.activation(sn[:, :], ang[:, :], ACT.Sin).then_inc(s["sincos"], 1)
                A.activation(cs[:, :], kk[:, :], ACT.Sin, bias=half_pi[:, 0:1]).then_inc(s["sincos"], 1)

            def exponentials(i):
                act.wait_ge(s["okd"], i + 1)
                A.activation(ep[:, :], dd[:, :], ACT.Exp).then_inc(s["expd"], 1)
                A.activation(em[:, :], dm[:, :], ACT.Exp).then_inc(s["expd"], 1)
                A.activation(ec[:, 0:3 * NC], fsm[:, :, :].rearrange("p a c -> p (a c)"), ACT.Exp)\
                    .then_inc(s["expd"], 1)
                A.activation(gen_src[:, 0, :], nl[:, :], ACT.Exp).then_inc(s["expd"], 1)

            def end_keys(i, q):
                act.wait_ge(s["bt_ps"], i * 2 + q + 1)
                A.activation(bt[:, q].rearrange("p c n -> p (c n)"), bank[1 + q][:], ACT.Copy).then_inc(s["btc"], 1)

            def squares(i, q):
                act.wait_ge(s["gated"], i * 2 + q + 1)
                A.activation(gq[:, q, :], gg[:, q, :], ACT.Square).then_inc(s["gsq"], 1)

            def second_norm(i):
                act.wait_ge(s["x2T_ps"], i + 1)
                A.activation(xnT[:], bank[2][:], ACT.Copy).then_inc(s["x2T"], 1)

            def up_probs(i):
                act.wait_ge(s["diff"], i + 1)
                A.activation(pr[:, 1:2], pr[:, 0:1], ACT.Exp).then_inc(s["pexp"], 1)

            def up(j, units):
                for u in units:
                    act.wait_ge(s["t1_ps"], j * NU + u + 1)
                    if u >= 2:
                        act.wait_ge(s["h_ps"], j * NU + u - 1)
                    A.activation(t1[D1:2 * D1, u % 2].rearrange("p n k f -> p (n k f)"), bank[4 + u % 2][0:D2, :],
                                 ACT.Copy).then_inc(s["t1_in"], 1)

            def gelu(j, groups):
                for g in groups:
                    act.wait_ge(s["hpre_in"], j * NG + g + 1)
                    for half in range(2):
                        f = slice(half * (F2 // 2), (half + 1) * (F2 // 2))
                        A.activation(hh[half * F1:(half + 1) * F1, g * GRP:(g + 1) * GRP], hpre[:, g % 4, :, f],
                                     ACT.Gelu).then_inc(s["h_in"], 1)

            def down_probs(j):
                act.wait_ge(s["ddiff"], j + 1)
                A.activation(pr[:, 1:2], pr[:, 0:1], ACT.Exp).then_inc(s["dpexp"], 1)

            def down(j, groups):
                for g in groups:
                    act.wait_ge(s["t2_ps"], j * NG + g + 1)
                    if g >= 2:
                        act.wait_ge(s["y2_ps"], j * NG + g - 1)
                    A.activation(t2[F1:2 * F1, g % 2].rearrange("p n k f -> p (n k f)"), bank[4 + g % 2][0:F2, :],
                                 ACT.Copy).then_inc(s["t2_in"], 1)

            def one_pass(i, ssm_part, ffn_part):
                j = i - 1
                if ffn_part:
                    up(j, (0, 1))
                if ssm_part:
                    turned_rows(i)
                    lora(i)
                    before_conv(i, 0)
                    before_conv(i, 1)
                    before_conv(i, 2)
                    soft_exp(i)
                    soft_ln(i)
                    gate(i, 0)
                    gate(i, 1)
                if ffn_part:
                    up(j, (2,))
                if ssm_part:
                    conv_silu(i, 0)
                if ffn_part:
                    up(j, (3,))
                if ssm_part:
                    conv_silu(i, 1)
                if ffn_part:
                    gelu(j, (0,))
                if ssm_part:
                    step_sizes(i)
                if ffn_part:
                    up(j, (4,))
                    gelu(j, (1,))
                    up(j, (5,))
                if ssm_part:
                    conv_silu(i, 2)
                if ffn_part:
                    up(j, (6, 7, 8, 9, 10))
                if ssm_part:
                    sines(i)
                if ffn_part:
                    up(j, (11,))
                    gelu(j, (2,))
                if ssm_part:
                    exponentials(i)
                if ffn_part:
                    up(j, (12, 13, 14))
                    gelu(j, (3,))
                    up(j, (15,))
                    gelu(j, (4, 5, 6, 7))
                    down_probs(j)
                    down(j, (0, 1))
                if ssm_part:
                    end_keys(i, 0)
                    end_keys(i, 1)
                if ffn_part:
                    down(j, (2, 3, 4, 5))
                if ssm_part:
                    squares(i, 0)
                    squares(i, 1)
                if ffn_part:
                    down(j, (6, 7))
                if ssm_part:
                    second_norm(i)
                    up_probs(i)

            passes(act, one_pass)

        @block.vector
        def _(dve):
            V = nc.vector
            for whole in (xpre, phi, state):
                V.memset(whole[:], 0.0).then_inc(s["zeros"], 1)
            dve.wait_ge(s["zeros"], 3)
            dve.wait_ge(s["early"], 16)
            dve.wait_ge(s["consts"], 11)
            dve.wait_ge(s["selfs"], 16)

            def top2(step, i, layer, logits, ps):
                diff, pexp, probs, row_ps, rows_in = (s[n] for n in (
                    ("diff", "pexp", "probs", "row_ps", "rows_in"),
                    ("ddiff", "dpexp", "dprobs", "drow_ps", "drows_in"))[layer])
                step(V.tensor_copy(lg[:], logits))
                apart(dve)
                step(V.max(top[:], lg[:]))
                apart(dve)
                step(V.max_index(topi[:], top[:], lg[:]))
                step(V.tensor_scalar(pr[:, 6:8], topi[:, 0:2], float(F1), None, ALU.mult))
                V.tensor_tensor(pr[:, 0:1], top[:, 1:2], top[:, 0:1], ALU.subtract).then_inc(diff, 1)
                dve.wait_ge(pexp, i + 1)
                step(V.tensor_scalar(pr[:, 2:3], pr[:, 1:2], 1.0, None, ALU.add))
                step(V.reciprocal(pr[:, 4:5], pr[:, 2:3]))
                V.tensor_tensor(pr[:, 5:6], pr[:, 4:5], pr[:, 1:2], ALU.mult).then_inc(probs, 1)
                dve.wait_ge(row_ps, i + 1)
                V.tensor_copy(offs[:, layer].rearrange("p n k -> p k n"),
                              ps[0:1, 128:128 + 2 * TOK].rearrange("p (k n) -> p k n", k=2)).then_inc(rows_in, 1)
                V.tensor_copy(pb[:, layer].rearrange("p n k -> p k n"),
                              ps[:, 256:256 + 2 * TOK].rearrange("p (k n) -> p k n", k=2)).then_inc(rows_in, 1)

            def reduce_angle(step, ang_, k_):
                step(V.tensor_scalar(k_, ang_, 1 / (2 * math.pi), ROUND, ALU.mult, ALU.add))
                step(V.tensor_scalar(k_, k_, ROUND, None, ALU.subtract))
                step(V.scalar_tensor_tensor(ang_, k_, -TWO_PI_HI, ang_, ALU.mult, ALU.add))
                step(V.scalar_tensor_tensor(ang_, k_, -TWO_PI_LO, ang_, ALU.mult, ALU.add))

            def layernorm_stats(step, src, name, i):
                for c in range(TILES):
                    ins = V.bn_stats(stats[:, c], src[:, c])
                    if c < TILES - 1:
                        ins.then_inc(s["dv"], 1)
                        step.n += 1
                    else:
                        step(ins)
                apart(dve)
                for c in range(TILES):
                    ins = V.bn_aggr(mv[:, c], stats[:, c])
                    if c < TILES - 1:
                        ins.then_inc(s["dv"], 1)
                        step.n += 1
                    else:
                        step(ins)
                V.tensor_scalar(mv[:, :, 1], mv[:, :, 1], EPS, None, ALU.add).then_inc(s[name], 1)

            general = General(dve, "dve")

            def first_norm(step, i, first):
                dve.wait_ge(s["x_in"], i * 16 + 16)
                V.tensor_scalar(xpre[:, :, 0:TAPS - 1], xpre[:, :, SEG:], flags[:, bass.ds(i, 1)], None, ALU.mult)\
                    .then_inc(s["tails"], 1)
                layernorm_stats(step, xin, "var1", i)
                dve.wait_ge(s["rstd1"], i + 1)
                if not first:
                    dve.wait_ge(s["scr"], i * 32)
                for c in range(TILES):
                    V.tensor_scalar(xn[:, c], xin[:, c], mv[:, c, 0:1], rstd[:, c:c + 1], ALU.subtract, ALU.mult)\
                        .then_inc(s["xn1"], 1)
                if first:
                    for whole in (ss, xp, t1, hs, t2):
                        V.memset(whole[:], 0.0).then_inc(s["zeros"], 1)
                    V.memset(ec[:, BLK + 3 * SEG:], 0.0).then_inc(s["zeros"], 1)
                    dve.wait_ge(s["zeros"], 9)
                    dve.wait_ge(s["weights"], 16 * 5)
                    for q in range(2):
                        V.tensor_scalar(wout[:, q], wout[:, q], nw[:, q:q + 1], None, ALU.mult).then_inc(s["scaled"], 1)

            def softplus(step, i):
                dve.wait_ge(s["dt_ps"], i + 1)
                step(V.tensor_tensor(dts[:, 0].rearrange("p (c h) -> p c h", h=HEADS),
                                     bank[2][:, 0:TILES * HEADS].rearrange("p (c h) -> p c h", h=HEADS),
                                     dtb[:, :].unsqueeze(1).to_broadcast([P, TILES, HEADS]), ALU.add))
                V.scalar_tensor_tensor(dts[:, 1], dts[:, 0], -1.0, dts[:, 0], ALU.mult, ALU.min).then_inc(s["softneg"], 1)

            def softplus_log(step, i):
                dve.wait_ge(s["softexp"], i + 1)
                V.tensor_scalar(dts[:, 3], dts[:, 2], 1.0, None, ALU.add).then_inc(s["soft1p"], 1)
                dve.wait_ge(s["soft1p"], i + 1)
                step(V.tensor_scalar(dts[:, 5], dts[:, 3], -1.0, None, ALU.add))
                step(V.tensor_scalar(dts[:, 6], dts[:, 5], 1e-30, None, ALU.max))
                step(V.reciprocal(dts[:, 6], dts[:, 6]))
                step(V.tensor_tensor(dts[:, 6], dts[:, 6], dts[:, 2], ALU.mult))
                step(V.tensor_scalar(dts[:, 5], dts[:, 5], 0.0, None, ALU.is_equal))
                step(V.tensor_tensor(dts[:, 5], dts[:, 5], dts[:, 2], ALU.mult))

            def softplus_end(step, i):
                dve.wait_ge(s["softln"], i + 1)
                step(V.tensor_tensor(dts[:, 6], dts[:, 6], dts[:, 4], ALU.mult))
                step(V.tensor_tensor(dts[:, 6], dts[:, 6], dts[:, 5], ALU.add))
                step(V.tensor_scalar(dts[:, 0], dts[:, 0], 0.0, None, ALU.max))
                V.tensor_tensor(dtx[:], dts[:, 6].unsqueeze(2).to_broadcast([P, TILES * HEADS, NK]),
                                dts[:, 0].unsqueeze(2).to_broadcast([P, TILES * HEADS, NK]), ALU.add)\
                    .then_inc(s["dt_tok"], 1)

            def conv(step, i, a):
                dve.wait_ge(s["xpre_in"], i * 3 + a + 1)
                step(V.tensor_scalar(cv[:, ORDER[a]], xpre[:, ORDER[a], 0:SEG], cw[:, ORDER[a], 0:1], cb[:, ORDER[a]:ORDER[a] + 1], ALU.mult, ALU.add))
                for k in range(1, TAPS):
                    ins = V.scalar_tensor_tensor(cv[:, ORDER[a]], xpre[:, ORDER[a], k:k + SEG], cw[:, ORDER[a], k:k + 1], cv[:, ORDER[a]],
                                                 ALU.mult, ALU.add)
                    if k < TAPS - 1:
                        step(ins)
                    else:
                        ins.then_inc(s["conv"], 1)

            def decays(step, i):
                dve.wait_ge(s["th_ps"], i + 1)
                step(V.tensor_scalar(th[:, :], bank[1][:], thb[:, 0:1], math.pi / 2, ALU.add, ALU.min))
                V.tensor_scalar(th[:, :], th[:, :], -math.pi / 2, None, ALU.max).then_inc(s["dtheta"], 1)
                dve.wait_ge(s["dtheta"], i + 1)
                dve.wait_ge(s["dt_in"], i + 1)
                step(V.tensor_tensor(om[:, :], th[:, :], gen_src[:, 1, :], ALU.mult))
                step(V.tensor_tensor_scan(ang[:, :], keep[:], om[:, :], 0.0, ALU.mult, ALU.add))
                dve.wait_ge(s["thsq"], i + 1)
                step(V.tensor_scalar(rr[:, :], rr[:, :], etas[:, 0:1], lamb[:, 0:1], ALU.mult, ALU.add))
                step(V.scalar_tensor_tensor(nl[:, :], rr[:, :], -1.0, gen_src[:, 1, :], ALU.mult, ALU.mult))
                step(V.tensor_tensor_scan(rr[:, :], keep[:], nl[:, :], 0.0, ALU.mult, ALU.add))
                rc = rr[:, :].rearrange("p (c n) -> p c n", n=CHUNK)
                step(V.tensor_tensor(dd[:, :].rearrange("p (c n) -> p c n", n=CHUNK), rc,
                                     rc[:, :, MID:MID + 1].to_broadcast([P, NC, CHUNK]), ALU.subtract))
                step(V.tensor_reduce(viol[:, 0:1], dd[:, :], AX.X, ALU.max, apply_absolute_value=True))
                V.tensor_scalar(viol[:, 1:2], viol[:, 0:1], LIMIT, None, ALU.is_le).then_inc(s["viol_in"], 1)

            def phases(step, i):
                step(V.tensor_scalar(phi[:, 0:1], phi[:, NC:NC + 1], flags[:, bass.ds(i, 1)], None, ALU.mult))
                angc = ang[:, :].rearrange("p (c n) -> p c n", n=CHUNK)
                step(V.tensor_copy(ksm[:, 0], angc[:, :, CHUNK - 1]))
                reduce_angle(step, ksm[:, 0], ksm[:, 1])
                step(V.tensor_tensor_scan(phi[:, 1:], ones[:, 0:NC], ksm[:, 0], phi[:, 0:1], ALU.mult, ALU.add))
                step(V.tensor_tensor(angc, angc, phi[:, 0:NC].unsqueeze(2).to_broadcast([P, NC, CHUNK]), ALU.add))
                reduce_angle(step, ang[:, :], kk[:, :])
                V.tensor_scalar(ang[:, :], ang[:, :], PI_SAFE, -PI_SAFE, ALU.min, ALU.max).then_inc(s["angle"], 1)
                dve.wait_ge(s["angle"], i * 2 + 1)
                V.scalar_tensor_tensor(kk[:, :], ang[:, :], -1.0, ang[:, :], ALU.mult, ALU.min).then_inc(s["angle"], 1)

            def exponents(step, i):
                rc = rr[:, :].rearrange("p (c n) -> p c n", n=CHUNK)
                dve.wait_ge(s["ok_ps"], i + 1)
                step(V.tensor_scalar(okf[:, 0:1], bank[1][:, 64:65], P - 0.5, None, ALU.is_gt))
                step(V.tensor_scalar(okf[:, 1:2], okf[:, 0:1], -1.0, 1.0, ALU.mult, ALU.add))
                V.tensor_copy(oki[:], okf[0:1, 0:1]).then_inc(s["flag"], 1)
                step(V.tensor_scalar(causal_ok[:], causal[:], okf[:, 0:1], None, ALU.mult))
                step(V.tensor_scalar(mref[:, 0], rc[:, :, MID], okf[:, 0:1], None, ALU.mult))
                step(V.scalar_tensor_tensor(mref[:, 1], rc[:, :, CHUNK - 1], okf[:, 1:2], mref[:, 0],
                                            ALU.mult, ALU.add))
                step(V.tensor_copy(fsm[:, 0], mref[:, 0]))
                step(V.tensor_tensor(fsm[:, 1], rc[:, :, CHUNK - 1], mref[:, 1], ALU.subtract))
                step(V.tensor_tensor(fsm[:, 2], mref[:, 1], mref[:, 0], ALU.subtract))
                step(V.tensor_tensor(dd[:, :].rearrange("p (c n) -> p c n", n=CHUNK), rc,
                                     mref[:, 0].unsqueeze(2).to_broadcast([P, NC, CHUNK]), ALU.subtract))
                V.tensor_tensor(dm[:, :].rearrange("p (c n) -> p c n", n=CHUNK),
                                mref[:, 1].unsqueeze(2).to_broadcast([P, NC, CHUNK]), rc, ALU.subtract)\
                    .then_inc(s["okd"], 1)

            def turned(step, i):
                dve.wait_ge(s["sincos"], i * 2 + 2)
                dve.wait_ge(s["expd"], i * 4 + 4)
                for at_, e_, t_ in ((3 * NC, ep, cs), (3 * NC + SEG, ep, sn), (BLK, em, cs), (BLK + SEG, em, sn)):
                    ins = V.tensor_tensor(ec[:, at_:at_ + SEG], e_, t_, ALU.mult)
                    if at_ < BLK + SEG:
                        step(ins)
                    else:
                        ins.then_inc(s["ecs"], 1)

            def scaled_x(i, q):
                dve.wait_ge(s["x_tr"], i * 2 + q + 1)
                V.tensor_tensor(xd[:, q].rearrange("p c (h n) -> p c h n", h=2),
                                bank[(3, 0)[q]][:].rearrange("p (c h n) -> p c h n", c=TILES, h=2),
                                dtx[:].rearrange("p (c h) k -> p c h k", h=HEADS)[:, :, 2 * q:2 * q + 2, 0:1]
                                .to_broadcast([P, TILES, 2, HD]), ALU.mult).then_inc(s["xds"], 1)

            def general_path(step, i):
                general.read_flag(i)
                with general.taken():
                    n = general.before()
                    once = Steps(dve, s["gen_steps"], n, 15)
                    once(V.tensor_tensor(gen_src[:, 0], gen_src[:, 0], keep[:], ALU.mult))
                    V.tensor_copy(gen_src[:, 1], gen_src[:, 1]).then_inc(s["gen_src_in"], 1)
                    for q in range(2):
                        decay, cosine, sine, keys = (gen_st[:, a] for a in range(4))
                        dve.wait_ge(s["gen_dma"], n * 512 + q * 256 + 256)
                        once(V.tensor_scalar(gen_w, cosine, re_row[:, 0:1], None, ALU.mult))
                        once(V.scalar_tensor_tensor(gen_w, sine, im_row[:, 0:1], gen_w, ALU.mult, ALU.add))
                        once(V.tensor_tensor(keys, keys, gen_w, ALU.mult))
                        once(V.tensor_tensor(tmp[:], cbq[:, 0], cosine, ALU.mult))
                        once(V.tensor_tensor(gen_w, cbq[:, 1], sine, ALU.mult))
                        once(V.tensor_tensor(tmp[:], tmp[:], gen_w, ALU.add))
                        once(V.memset(gen_y[:, q], 0.0))
                        apart(dve)
                        with dve.Fori(0, HD) as p:
                            at_p = n * (2 * HD) + q * HD + p
                            loop = Steps(dve, s["gen_loop"], at_p, 3)
                            V.tensor_copy(sel[:, 0].rearrange("p (h k) -> p h k", h=2),
                                          ident[:].rearrange("p (h w) -> p h w", h=2)[:, :, bass.ds(p, 1)]
                                          .to_broadcast([P, 2, 2 * NK])).then_inc(s["gen_sel"], 1)
                            V.tensor_copy(sel[:, 1], pick[:, bass.ds(p * -1 + HD, P)]).then_inc(s["gen_sel"], 1)
                            dve.wait_ge(s["gen_x_ps"], at_p + 1)
                            loop(V.tensor_tensor(gen_p, bank[1][:], keys, ALU.mult))
                            loop(V.tensor_tensor_scan(gen_w, decay, gen_p, 0.0, ALU.mult, ALU.add))
                            V.tensor_tensor(gen_p, gen_w, tmp[:], ALU.mult).then_inc(s["gen_prod"], 1)
                            dve.wait_ge(s["gen_y_ps"], at_p + 1)
                            loop(V.tensor_tensor(gen_y[:, q], gen_y[:, q], bank[2][:], ALU.add))
                            apart(dve)
                        V.tensor_copy(okf[:, 0:1], okf[:, 0:1]).then_inc(s["gen_done"], 1)
                        dve.wait_ge(s["gen_done"], n * 2 + q + 1)
                        apart(dve)
                    once.done()

            def inherited(step, i):
                for q in range(2):
                    step(V.tensor_scalar(state[:, q], state[:, q], flags[:, bass.ds(i, 1)], None, ALU.mult))

            def score_queries(step, i, q):
                cosp, sinp = (st[:, q, 3 * NC + n * SEG:3 * NC + (n + 1) * SEG] for n in range(2))
                step(V.tensor_tensor(c1[:, q], cbq[:, 0], cosp, ALU.mult))
                step(V.tensor_tensor(tmp[:], cbq[:, 1], sinp, ALU.mult))
                V.tensor_tensor(c1[:, q], c1[:, q], tmp[:], ALU.add).then_inc(s["q1"], 1)
                dve.wait_ge(s["q1"], i * 2 + q + 1)

            def state_queries(step, i, q):
                cosp, sinp = (st[:, q, 3 * NC + n * SEG:3 * NC + (n + 1) * SEG] for n in range(2))
                step(V.scalar_tensor_tensor(c2[:, q], cbr[:, 2], im_sign[:, 0:1], cosp, ALU.mult, ALU.mult))
                step(V.tensor_tensor(tmp[:], cbr[:, 3], sinp, ALU.mult))
                V.tensor_tensor(c2[:, q], c2[:, q], tmp[:], ALU.subtract).then_inc(s["q2"], 1)
                dve.wait_ge(s["q2"], i * 2 + q + 1)

            def masked(i, q):
                for h in range(2):
                    dve.wait_ge(s["g_ps"], i * 4 + 2 * q + h + 1)
                    V.tensor_tensor(gs[:, q, h], bank[((3, 0), (1, 2))[q][h]][:].rearrange("p (c n) -> p c n", n=P),
                                    causal_ok[:, :].unsqueeze(1).to_broadcast([P, TILES, P]), ALU.mult)\
                        .then_inc(s["gsm"], 1)

            def decays_between(step, i):
                for q in range(2):
                    emid, gend, rho = (st[:, q, n * NC:(n + 1) * NC] for n in range(3))
                    step(V.tensor_tensor(fdec[:, q, 0, 0:NC - 1], gend[:, 0:NC - 1], emid[:, 1:NC], ALU.mult))
                    step(V.tensor_tensor(fdec[:, q, 1, 0:NC - 1], fdec[:, q, 0, 0:NC - 1], rho[:, 1:NC], ALU.mult))
                    for h in range(2):
                        half = slice(h * 2 * NK, (h + 1) * 2 * NK)
                        step(V.tensor_scalar(ss[half, q, 0, h * HD:(h + 1) * HD], state[half, q], emid[half, 0:1],
                                             None, ALU.mult))
                    step(V.tensor_scalar(fdec[:, q, 0, NC - 1:NC], emid[:, 0:1], rho[:, 0:1], None, ALU.mult))

            def recurrence(step, i):
                dve.wait_ge(s["u_ps"], i * 2 + 2)
                for c in range(NC):
                    for q in range(2):
                        u = update(q, c)
                        if c == 0:
                            ins = V.scalar_tensor_tensor(vv[:, q, 0], state[:, q], fdec[:, q, 0, NC - 1:NC], u,
                                                         ALU.mult, ALU.add)
                        else:
                            ins = V.scalar_tensor_tensor(vv[:, q, c], vv[:, q, c - 1], fdec[:, q, 1, c - 1:c], u,
                                                         ALU.mult, ALU.add)
                        step(ins)
                for q in range(2):
                    for h in range(2):
                        half = slice(h * 2 * NK, (h + 1) * 2 * NK)
                        V.tensor_tensor(ss[half, q, 1:NC, h * HD:(h + 1) * HD], vv[half, q, 0:NC - 1],
                                        fdec[half, q, 0, 0:NC - 1].unsqueeze(2).to_broadcast([2 * NK, NC - 1, HD]),
                                        ALU.mult).then_inc(s["states"], 1)
                    step(V.tensor_scalar(state[:, q], vv[:, q, NC - 1], st[:, q, 2 * NC - 1:2 * NC],
                                         None, ALU.mult))

            def gated(step, i, q):
                dve.wait_ge(s["zsilu"], i * 2 + 2)
                dve.wait_ge(s["y_ps"], i * 2 + q + 1)
                apart(dve)
                with general.taken():
                    n = general.before()
                    V.tensor_tensor(bank[1 + q][:], bank[1 + q][:], gen_y[:, q], ALU.add)\
                        .then_inc(s["gen_add"], 1)
                    dve.wait_ge(s["gen_add"], n * 2 + q + 1)
                    apart(dve)
                    if q == 1:
                        general.count()
                step(V.scalar_tensor_tensor(tmp[:], cv[:, q], dsk[:, q:q + 1], bank[1 + q][:], ALU.mult, ALU.add))
                V.tensor_tensor(gg[:, q], tmp[:], zs[:, q], ALU.mult).then_inc(s["gated"], 1)
                if q == 0:
                    dve.wait_ge(s["gated"], i * 2 + 1)

            def residual(i):
                dve.wait_ge(s["o_ps"], i + 1)
                V.tensor_scalar(mv[:, :, 0], bank[3][:, 0:TILES], 1.0 / DI, EPS, ALU.mult, ALU.add)\
                    .then_inc(s["rmsin"], 1)
                dve.wait_ge(s["rms"], i + 1)
                for c in range(TILES):
                    V.scalar_tensor_tensor(x1[:, c], bank[0][:, c * DM:(c + 1) * DM], rstd[:, c:c + 1], xin[:, c],
                                           ALU.mult, ALU.add).then_inc(s["x1r"], 1)

            def second_norm(step, i):
                dve.wait_ge(s["x1r"], i * TILES + TILES)
                layernorm_stats(step, x1, "var2", i)
                dve.wait_ge(s["rstd2"], i + 1)
                for c in range(TILES):
                    V.tensor_scalar(xn[:, c], x1[:, c], mv[:, c, 0:1], rstd[:, c:c + 1], ALU.subtract, ALU.mult)\
                        .then_inc(s["xn2"], 1)

            def stacked(i):
                dve.wait_ge(s["rep_bc"], i * 256 + 256)
                dve.wait_ge(s["cbq"], i + 1)
                apart(dve)
                dve.wait_ge(s["stacked"], i * 128 + 128)
                apart(dve)

            def up_router(step, i):
                dve.wait_ge(s["lg_ps"], i + 1)
                top2(step, i, 0, bank[3][0:TOK, 0:E], bank[1])
                step.done()

            def hidden(j, g):
                dve.wait_ge(s["h_ps"], j * NU + 2 * g + 2)
                if g >= 4:
                    dve.wait_ge(s["h_in"], j * 2 * NG + 2 * (g - 3))
                V.scalar_tensor_tensor(hpre[:, g % 4],
                                       bank[6 + g % 2][0:F1, :].rearrange("p (n f) -> p n f", f=F2),
                                       scale_u[0:F1, 0:1], bias_u[:, :].unsqueeze(1).to_broadcast([F1, GRP, F2]),
                                       ALU.mult, ALU.add).then_inc(s["hpre_in"], 1)

            def down_router(j):
                step = Steps(dve, s["fv"], j, 6)
                dve.wait_ge(s["lgd_ps"], j + 1)
                top2(step, j, 1, bank[6][0:TOK, 0:E], bank[7])
                step.done()

            def results(j, groups):
                for g in groups:
                    if g == 0:
                        dve.wait_ge(s["xrb"], j + 1)
                        apart(dve)
                    dve.wait_ge(s["y2_ps"], j * NG + g + 1)
                    xr = xir[0:D1, g * GRP:(g + 1) * GRP]
                    V.scalar_tensor_tensor(xr, bank[6 + g % 2][0:D1, 0:GRP * D2].rearrange("p (n j) -> p n j", j=D2),
                                           scale_d[0:D1, 0:1], xr, ALU.mult, ALU.add).then_inc(s["out_sb"], 1)

            def one_pass(i, ssm_part, ffn_part):
                j = i - 1
                step = Steps(dve, s["dv"], i, DVE_STEPS)
                if ssm_part:
                    first_norm(step, i, not ffn_part)
                    softplus(step, i)
                    conv(step, i, 0)
                    softplus_log(step, i)
                if ffn_part:
                    hidden(j, 0)
                if ssm_part:
                    conv(step, i, 1)
                    softplus_end(step, i)
                if ffn_part:
                    hidden(j, 1)
                if ssm_part:
                    conv(step, i, 2)
                    decays(step, i)
                if ffn_part:
                    hidden(j, 2)
                if ssm_part:
                    phases(step, i)
                if ffn_part:
                    hidden(j, 3)
                if ssm_part:
                    exponents(step, i)
                if ffn_part:
                    hidden(j, 4)
                if ssm_part:
                    turned(step, i)
                    scaled_x(i, 0)
                if ffn_part:
                    hidden(j, 5)
                if ssm_part:
                    scaled_x(i, 1)
                if ffn_part:
                    hidden(j, 6)
                    hidden(j, 7)
                    down_router(j)
                if ssm_part:
                    stacked(i)
                    general_path(step, i)
                    inherited(step, i)
                if ffn_part:
                    results(j, (0,))
                if ssm_part:
                    score_queries(step, i, 0)
                    score_queries(step, i, 1)
                    masked(i, 0)
                    state_queries(step, i, 0)
                    state_queries(step, i, 1)
                    masked(i, 1)
                    decays_between(step, i)
                if ffn_part:
                    results(j, (1, 2))
                if ssm_part:
                    recurrence(step, i)
                    gated(step, i, 0)
                if ffn_part:
                    results(j, (3, 4))
                if ssm_part:
                    gated(step, i, 1)
                if ffn_part:
                    results(j, (5,))
                if ssm_part:
                    residual(i)
                    second_norm(step, i)
                if ffn_part:
                    results(j, (6, 7))
                if ssm_part:
                    up_router(step, i)

            passes(dve, one_pass)

        @block.tensor
        def _(pe):
            T = nc.tensor
            NG = TOK // GRP

            def mm(o, l, r, start=True, stop=True):
                return T.matmul(o, l, r, start=start, stop=stop)

            pe.wait_ge(s["early"], 16)
            pe.wait_ge(s["selfs"], 16)
            general = General(pe, "pe")
            where = [[pe.alloc_register(f"table_{set_}_{n}") for n in range(2 * GRP)] for set_ in range(2)]
            table = tab[:].rearrange("p e f -> p (e f)")
            table_b = tab[:, :, :].rearrange("p e f -> p (e f)")[:, D1:]

            def find(layer, g):
                at_ = g * 2 * GRP
                pe.reg_load(where[g % 2], offs[:, layer].rearrange("p n k -> p (n k)")[:, at_:at_ + 2 * GRP])

            def offset(n, k):
                return pe.snap(where[(n // GRP) % 2][2 * (n % GRP) + k], min_val=0, max_val=(E - 1) * F1)

            def transposes(src, dst):
                for c in range(TILES):
                    ins = T.transpose(dst[:, c * P:(c + 1) * P], src[:, c * P:(c + 1) * P], ident[:])
                return ins

            def rows(ps):
                apart(pe)
                for k in range(2):
                    mm(ps[0:1, 128 + k * TOK:128 + (k + 1) * TOK], pr[:, 6 + k:7 + k], ident[0:TOK, 0:TOK])
                for k in range(2):
                    ins = mm(ps[:, 256 + k * TOK:256 + (k + 1) * TOK],
                             pr[:, 4 + k:5 + k].to_broadcast([TOK, P]), ident[0:TOK, 0:TOK])
                return ins

            def first_norm(i):
                pe.wait_ge(s["xn1"], i * TILES + TILES)
                transposes(xn[:].rearrange("p c d -> p (c d)"), bank[0]).then_inc(s["xnT_ps"], 1)

            def projections(i):
                pe.wait_ge(s["xnT"], i + 1)
                mm(bank[1][0:LORA, :], w1[:], xnT[:]).then_inc(s["w1_ps"], 1)
                for c in range(TILES):
                    ins = mm(bank[2][:, c * HEADS:(c + 1) * HEADS], xnT[:, c * P:(c + 1) * P], win[:, C_DT:C_DT + HEADS])
                ins.then_inc(s["dt_ps"], 1)
                mm(bank[3][:], win[:, C_BC:C_BC + P], xnT[:]).then_inc(s["xbc_ps"], 1)
                mm(bank[0][:], win[:, C_X:C_X + P], xnT[:]).then_inc(s["xbc_ps"], 1)

            def more_projections(i):
                pe.wait_ge(s["lora"], i + 1)
                mm(bank[1][:], win[:, C_X + P:C_X + 2 * P], xnT[:]).then_inc(s["xbc_ps"], 1)
                for a, b in enumerate((3, 0)):
                    pe.wait_ge(s["xpre_in"], i * 3 + a + 1)
                    mm(bank[b][:], win[:, C_Z + a * P:C_Z + (a + 1) * P], xnT[:]).then_inc(s["z_ps"], 1)

            def theta(i):
                pe.wait_ge(s["weights"], 16 * 5)
                pe.wait_ge(s["xpre_in"], i * 3 + 3)
                mm(bank[1][:], w2[:], lo[0:LORA, :]).then_inc(s["th_ps"], 1)

            def dt_rows(i):
                pe.wait_ge(s["dt_tok"], i + 1)
                transposes(dtx[:].rearrange("p a k -> p (a k)"), bank[2]).then_inc(s["dtr_ps"], 1)

            def x_turned(i, q):
                pe.wait_ge(s["zsilu"], i * 2 + q + 1)
                pe.wait_ge(s["xc"], i * 3 + q + 2)
                transposes(cv[:, q], bank[(3, 0)[q]]).then_inc(s["x_tr"], 1)

            def all_within(i):
                pe.wait_ge(s["viol_in"], i + 1)
                mm(bank[1][:, 64:65], ones[:], viol[:, 1:2]).then_inc(s["ok_ps"], 1)

            def general_path(i):
                pe.wait_ge(s["dt_in"], i + 1)
                general.read_flag(i)
                with general.taken():
                    n = general.before()
                    for q in range(2):
                        with pe.Fori(0, HD) as p:
                            at_p = n * (2 * HD) + q * HD + p
                            pe.wait_ge(s["gen_sel"], at_p * 2 + 2)
                            mm(bank[1][:], sel[:, 0], cv[:, q]).then_inc(s["gen_x_ps"], 1)
                            pe.wait_ge(s["gen_prod"], at_p + 1)
                            mm(bank[2][:], sel[:, 1], gen_p).then_inc(s["gen_y_ps"], 1)
                    pe.wait_ge(s["gen_done"], n * 2 + 2)
                    apart(pe)
                    general.count()

            def end_keys(i, q):
                pe.wait_ge(s["k2r"], i * 2 + q + 1)
                transposes(k2[:, q], bank[1 + q]).then_inc(s["bt_ps"], 1)

            def scores(i, q):
                pe.wait_ge(s["stacked"], i * 128 + 128)
                pe.wait_ge(s["q1"], i * 2 + q + 1)
                apart(pe)
                for h in range(2):
                    if q == 0:
                        pe.wait_ge(s["xds"], i * 2 + h + 1)
                    else:
                        pe.wait_ge(s["btc"], i * 2 + h + 1)
                    apart(pe)
                    half = slice(h * CHUNK, (h + 1) * CHUNK)
                    for c in range(TILES):
                        cols = slice(c * P, (c + 1) * P)
                        ins = mm(bank[((3, 0), (1, 2))[q][h]][:, cols],
                                 st[half, q, BLK + c * P:BLK + (c + 1) * P], c1[half, q, cols])
                    ins.then_inc(s["g_ps"], 1)

            def updates(i):
                for q in range(2):
                    pe.wait_ge(s["btc"], i * 2 + q + 1)
                    pe.wait_ge(s["gsm"], i * 4 + 2)
                    apart(pe)
                    for c in range(NC):
                        rows_ = slice((c % 2) * CHUNK, (c % 2 + 1) * CHUNK)
                        for h in range(2):
                            half = slice(h * CHUNK, (h + 1) * CHUNK)
                            ins = mm(update(q, c)[half], bt[rows_, q, c // 2, half],
                                     xd[rows_, q, c // 2, half])
                    ins.then_inc(s["u_ps"], 1)

            def outputs(i, q):
                pe.wait_ge(s["gsm"], i * 4 + 4)
                pe.wait_ge(s["q2"], i * 2 + q + 1)
                pe.wait_ge(s["states"], i * 4 + 2 * q + 2)
                apart(pe)
                for c in range(TILES):
                    for h in range(2):
                        half = slice(h * CHUNK, (h + 1) * CHUNK)
                        mm(bank[1 + q][half, c * P:(c + 1) * P], xd[:, q, c, half], gs[:, q, h, c], True, False)
                    for par in range(2):
                        cols = slice((2 * c + par) * CHUNK, (2 * c + par + 1) * CHUNK)
                        ins = mm(bank[1 + q][:, cols], ss[:, q, 2 * c + par], c2[:, q, cols], False, par == 1)
                ins.then_inc(s["y_ps"], 1)

            def projected(i):
                pe.wait_ge(s["scaled"], 2)
                pe.wait_ge(s["gated"], i * 2 + 2)
                for c in range(TILES):
                    rows_ = slice(c * P, (c + 1) * P)
                    for q in range(2):
                        mm(bank[0][:, c * DM:(c + 1) * DM], gg[:, q, rows_], wout[:, q], q == 0, q == 1)
                pe.wait_ge(s["gsq"], i * 2 + 2)
                for c in range(TILES):
                    rows_ = slice(c * P, (c + 1) * P)
                    for q in range(2):
                        ins = mm(bank[3][:, c:c + 1], gq[:, q, rows_], ones[:, 0:1], q == 0, q == 1)
                ins.then_inc(s["o_ps"], 1)

            def second_norm(i):
                pe.wait_ge(s["xn2"], i * TILES + TILES)
                transposes(xn[:].rearrange("p c d -> p (c d)"), bank[2]).then_inc(s["x2T_ps"], 1)

            def up_router(i):
                pe.wait_ge(s["x2T"], i + 1)
                xt = xnT[:].rearrange("p (n r) -> p r n", r=RPT)
                for r in range(RPT):
                    ins = mm(bank[3][0:TOK, 0:E], xt[:, r], wup[:, r], r == 0, r == RPT - 1)
                ins.then_inc(s["lg_ps"], 1)

            def up_rows(i):
                pe.wait_ge(s["probs"], i + 1)
                rows(bank[1]).then_inc(s["row_ps"], 1)

            def up_second(j, u):
                g = u // 2
                pe.wait_ge(s["t1_in"], j * NU + u + 1)
                if u % 2 == 0 and g >= 2:
                    pe.wait_ge(s["hpre_in"], j * NG + g - 1)
                for n in range(UNIT):
                    col = ((u % 2) * UNIT + n) * F2
                    for k in range(2):
                        ins = mm(bank[6 + g % 2][0:F1, col:col + F2], t1[:, u % 2, n, k],
                                 table[:, bass.ds(offset(u * UNIT + n, k), F2)], k == 0, k == 1)
                ins.then_inc(s["h_ps"], 1)

            def up(j, units):
                for u in units:
                    if u == 0:
                        pe.wait_ge(s["tables"], 16 * 6)
                        pe.wait_ge(s["rows_in"], j * 2 + 2)
                        apart(pe)
                    if u % 2 == 0:
                        find(0, u // 2)
                    pe.wait_ge(s["xp_in"], j * NG + u // 2 + 1)
                    if u >= 2:
                        pe.wait_ge(s["t1_in"], j * NU + u - 1)
                    apart(pe)
                    for n in range(UNIT):
                        for k in range(2):
                            col = (2 * n + k) * F1
                            ins = mm(bank[4 + u % 2][0:D2, col:col + F1], xp[:, (u // 2) % 2, (u % 2) * UNIT + n, k],
                                     table[:, bass.ds(offset(u * UNIT + n, k), F1)])
                    ins.then_inc(s["t1_ps"], 1)
                    if u >= 1:
                        up_second(j, u - 1)
                    if u == NU - 1:
                        up_second(j, u)

            def down_router(j):
                pe.wait_ge(s["h_in"], j * 2 * NG + 2 * NG)
                for f in range(F2 // 2):
                    ins = mm(bank[6][0:TOK, 0:E], hh[:, :, f], wdn[:, f], f == 0, f == F2 // 2 - 1)
                ins.then_inc(s["lgd_ps"], 1)

            def down_rows(j):
                pe.wait_ge(s["dprobs"], j + 1)
                rows(bank[7]).then_inc(s["drow_ps"], 1)

            def down_second(j, g):
                pe.wait_ge(s["t2_in"], j * NG + g + 1)
                if g >= 2:
                    pe.wait_ge(s["out_sb"], j * NG + g - 1)
                for n in range(GRP):
                    for k in range(2):
                        ins = mm(bank[6 + g % 2][0:D1, n * D2:(n + 1) * D2], t2[:, g % 2, n, k],
                                 table_b[:, bass.ds(offset(g * GRP + n, k), D2)], k == 0, k == 1)
                ins.then_inc(s["y2_ps"], 1)

            def down(j, groups):
                for g in groups:
                    if g == 0:
                        pe.wait_ge(s["drows_in"], j * 2 + 2)
                        apart(pe)
                    find(1, g)
                    pe.wait_ge(s["hs_in"], j * 2 * NG + 2 * g + 2)
                    if g >= 2:
                        pe.wait_ge(s["t2_in"], j * NG + g - 1)
                    apart(pe)
                    for n in range(GRP):
                        for k in range(2):
                            col = (2 * n + k) * D1
                            ins = mm(bank[4 + g % 2][0:F2, col:col + D1], hs[:, g % 2, n, k],
                                     table[:, bass.ds(offset(g * GRP + n, k), D1)])
                    ins.then_inc(s["t2_ps"], 1)
                    if g >= 1:
                        down_second(j, g - 1)
                    if g == NG - 1:
                        down_second(j, g)

            def one_pass(i, ssm_part, ffn_part):
                j = i - 1
                if ffn_part:
                    up(j, (0, 1))
                if ssm_part:
                    first_norm(i)
                    projections(i)
                    more_projections(i)
                if ffn_part:
                    up(j, (2,))
                if ssm_part:
                    theta(i)
                if ffn_part:
                    up(j, (3, 4))
                if ssm_part:
                    dt_rows(i)
                if ffn_part:
                    up(j, (5,))
                if ssm_part:
                    x_turned(i, 0)
                if ffn_part:
                    up(j, (6,))
                if ssm_part:
                    x_turned(i, 1)
                if ffn_part:
                    up(j, (7, 8, 9))
                if ssm_part:
                    all_within(i)
                if ffn_part:
                    up(j, (10, 11, 12, 13, 14, 15))
                    down_router(j)
                    down_rows(j)
                    down(j, (0,))
                if ssm_part:
                    general_path(i)
                if ffn_part:
                    down(j, (1,))
                if ssm_part:
                    end_keys(i, 0)
                    end_keys(i, 1)
                if ffn_part:
                    down(j, (2,))
                if ssm_part:
                    scores(i, 0)
                    scores(i, 1)
                if ffn_part:
                    down(j, (3,))
                if ssm_part:
                    updates(i)
                if ffn_part:
                    down(j, (4, 5))
                if ssm_part:
                    outputs(i, 0)
                    outputs(i, 1)
                if ffn_part:
                    down(j, (6,))
                if ssm_part:
                    projected(i)
                if ffn_part:
                    down(j, (7,))
                if ssm_part:
                    second_norm(i)
                    up_router(i)
                    up_rows(i)

            passes(pe, one_pass)


DVE_STEPS = 113


_ORDER = ["L0_attn_x", "first_weights", "th_w2", "w_out", "w_up", "a_up", "b_up", "bias_up", "w_down", "a_down",
          "b_down", "bias_down"]


def laid_out(i):
    g = {k: np.asarray(v) for k, v in i.items()}
    xf = g["L0_attn_x"].reshape(BATCH * LENGTH, DM)
    wi = g["L0_attn_in_proj_w"]
    bc = np.concatenate([np.arange(0, 2 * NK, 2), np.arange(1, 2 * NK, 2)])
    bc = np.concatenate([bc, 2 * NK + bc])
    rows = np.concatenate([np.arange(2 * DI), 2 * DI + bc, np.arange(2 * DI + 4 * NK, NW)])
    chans = np.concatenate([np.arange(DI), DI + bc])
    def col(a, n=P):
        return np.repeat(a.reshape(1, -1), n, 0)
    first = np.ones(NSEG, np.float32)
    first[::LENGTH // SEG] = 0.0
    return {
        "L0_attn_x": np.concatenate([xf, xf[:SEG]], 0),
        "first_weights": np.concatenate([
            wi[rows].T,
            g["L0_attn_theta_w1"],
            g["L0_attn_conv_w"][chans].reshape(3, P, TAPS).transpose(1, 0, 2).reshape(P, 3 * TAPS),
            g["L0_attn_conv_b"][chans].reshape(3, P).T,
            col(g["L0_attn_dt_bias"]),
            g["L0_attn_lambda_base"].reshape(P, 1),
            g["L0_attn_theta_base"].reshape(P, 1),
            g["L0_attn_viscosity_eta"].reshape(P, 1),
            np.repeat(g["L0_attn_D"], HD).reshape(2, P).T,
            g["L0_attn_norm_w"].reshape(2, P).T,
            col(first),
            col(g["L0_ffn_scale_up"]),
            col(g["L0_ffn_scale_down"])], 1),
        "th_w2": g["L0_attn_theta_w2"],
        "w_out": g["L0_attn_out_proj_w"].T.reshape(2, P, DM).transpose(1, 0, 2),
        "w_up": g["L0_ffn_W_up"].T.reshape(RPT, P, E).transpose(1, 0, 2),
        "a_up": g["L0_ffn_A_up"].transpose(2, 0, 1),
        "b_up": g["L0_ffn_B_up"].transpose(2, 0, 1),
        "bias_up": g["L0_ffn_bias_up"].reshape(F1, F2),
        "w_down": g["L0_ffn_W_down"].reshape(E, F1, F2).transpose(1, 2, 0),
        "a_down": g["L0_ffn_A_down"].transpose(2, 0, 1),
        "b_down": g["L0_ffn_B_down"].transpose(2, 0, 1),
        "bias_down": g["L0_ffn_bias_down"].reshape(D1, D2),
    }


def kernel(**inputs):
    import concourse.bacc as _bacc
    from concourse.bass_utils import run_bass_kernel_spmd as _run

    nc = _bacc.Bacc("TRN2", target_bir_lowering=False, num_devices=1)
    arrays, args = {}, []
    laid = laid_out(inputs)
    for name in _ORDER:
        a = np.ascontiguousarray(laid[name])
        arrays[f"in_{name}"] = a
        args.append(nc.dram_tensor(f"in_{name}", a.shape, mybir.dt.from_np(a.dtype), kind="ExternalInput").ap())
    args.append(nc.dram_tensor("out_0", (BATCH * LENGTH, DM), FP32, kind="ExternalOutput").ap())
    for name in ("x1_scratch", "x2_scratch"):
        args.append(nc.dram_tensor(name, (BATCH * LENGTH, DM), FP32, kind="Internal").ap())
    block_kernel(nc, *args)
    r = _run(nc, [arrays], core_ids=[0])
    return r.results[0]["out_0"].reshape(BATCH, LENGTH, DM)
```
